# Optimizing a Trainium2 kernel written in Bass

```python
import numpy as np
import jax
import jax.numpy as jnp

def _softmax(x, axis=-1):
    return jax.nn.softmax(x, axis=axis)

def _gelu(x):
    return jax.nn.gelu(x, approximate=True)

def _silu(x):
    return jax.nn.silu(x)

def _sigmoid(x):
    return jax.nn.sigmoid(x)

def _layernorm(x, axis=-1, eps=1e-05):
    m = jnp.mean(x, axis=axis, keepdims=True)
    v = jnp.var(x, axis=axis, keepdims=True)
    return (x - m) / jnp.sqrt(v + eps)

def _scatter_add(tgt, idx, src, axis=0):
    return tgt.at[idx].add(src)

def _segment_sum(src, seg, n):
    return jax.ops.segment_sum(src, seg, n)
kernel_name = 'mk_decoder_postln_d1_seqx_r4_0fdf3f'

def setup_inputs(seed: int=0):
    np.random.seed(seed)
    _w = jnp.asarray

    def _rec_inputs():
        import jax
        import jax.numpy as jnp
        _rk = jax.random.key(seed)
        x = -0.0002928 + 1 * jax.random.normal(jax.random.fold_in(_rk, 1), (8, 512, 256), jnp.float32)
        _lenS = 512 - jax.random.randint(jax.random.fold_in(_rk, 7), (8,), 0, max(1, 512 // 4) + 1, jnp.int32)
        _lenS2 = 1024 - jax.random.randint(jax.random.fold_in(_rk, 8), (8,), 0, max(1, 1024 // 4) + 1, jnp.int32)
        _ctx_512P = jax.random.normal(jax.random.fold_in(_rk, 11), (8, 16, 128), jnp.float32)
        _ctx_512c = jax.random.dirichlet(jax.random.fold_in(_rk, 511), 0.3 * jnp.ones((16,), jnp.float32), (8, 1024))
        _ctx_512t = jnp.einsum('bsk,bkd->bsd', _ctx_512c, _ctx_512P)
        _ctx_512t = _ctx_512t * jax.lax.rsqrt(jnp.mean(jnp.square(_ctx_512t)) + 1e-12) * 0.953939
        ctx_512 = 0.00222621 + 0.99962 * (_ctx_512t + 0.3 * jax.random.normal(jax.random.fold_in(_rk, 611), (8, 1024, 128), jnp.float32))
        return (x, ctx_512)
    x, ctx_512 = _rec_inputs()

    def _L0_attn_setup():
        import jax, jax.numpy as jnp
        import numpy as np
        import math
        B, N, DIM = (4, 1024, 256)
        HEADS, DHEAD, NRF = (16, 64, 64)
        STAB = 1e-06

        def _phi(t, RF):
            return jax.nn.relu(jnp.einsum('bhnd,hdr->bhnr', t, RF))
        key = jax.random.key(seed)
        k1, k2, k3, k4 = jax.random.split(key, 4)
        x = jax.random.normal(k1, (B, N, DIM), dtype=jnp.float32)
        W_qkv = jax.random.normal(k2, (DIM, 3 * HEADS * DHEAD), dtype=jnp.float32) * (1.0 / math.sqrt(DIM))
        RF = jax.random.normal(k3, (HEADS, DHEAD, NRF), dtype=jnp.float32) / math.sqrt(NRF)
        W_out = jax.random.normal(k4, (HEADS * DHEAD, DIM), dtype=jnp.float32) * (1.0 / math.sqrt(HEADS * DHEAD))
        b_out = jnp.zeros((DIM,), dtype=jnp.float32)
        return {'x': x, 'W_qkv': W_qkv, 'RF': RF, 'W_out': W_out, 'b_out': b_out}
    _L0_attn_all = _L0_attn_setup()
    _L0_attn_in = {k: v for k, v in _L0_attn_all.items() if k in ('W_qkv', 'RF', 'W_out', 'b_out')}
    del _L0_attn_all

    def _L0_xattn_setup():
        import jax, jax.numpy as jnp
        import numpy as np
        B, T, TC, C, CC, H = (2, 512, 128, 256, 128, 16)
        D = C // H

        def _heads(t):
            b, l, _ = t.shape
            return t.reshape(b, l, H, D).transpose(0, 2, 1, 3)
        key = jax.random.key(seed)
        ks = jax.random.split(key, 18)
        w = lambda k, i, o: jax.random.normal(k, (i, o), jnp.float32) / np.sqrt(i).astype(np.float32)
        return {'x': jax.random.normal(ks[0], (B, T, C), jnp.float32), 'cross_input': jax.random.normal(ks[1], (B, TC, CC), jnp.float32), 'Wk': w(ks[2], C, C), 'bk': jnp.zeros((C,), jnp.float32), 'Wq': w(ks[3], C, C), 'bq': jnp.zeros((C,), jnp.float32), 'Wv': w(ks[4], C, C), 'bv': jnp.zeros((C,), jnp.float32), 'Wck': w(ks[5], CC, C), 'bck': jnp.zeros((C,), jnp.float32), 'Wcq': w(ks[6], C, C), 'bcq': jnp.zeros((C,), jnp.float32), 'Wcv': w(ks[7], CC, C), 'bcv': jnp.zeros((C,), jnp.float32), 'Wp': w(ks[8], C, C), 'bp': jnp.zeros((C,), jnp.float32)}
    _L0_xattn_all = _L0_xattn_setup()
    _L0_xattn_in = {k: v for k, v in _L0_xattn_all.items() if k in ('Wk', 'bk', 'Wq', 'bq', 'Wv', 'bv', 'Wck', 'bck', 'Wcq', 'bcq', 'Wcv', 'bcv', 'Wp', 'bp')}
    del _L0_xattn_all

    def _L0_ffn_setup():
        import jax, jax.numpy as jnp
        import numpy as np
        B, S, D, H, E = (4, 512, 256, 1024, 8)
        key = jax.random.key(seed)
        ks = jax.random.split(key, 8)
        s_d = 1.0 / np.sqrt(D)
        s_h = 1.0 / np.sqrt(H)
        return {'x': jax.random.normal(ks[0], (B, S, D), dtype=jnp.float32), 'gate_w': jax.random.uniform(ks[1], (E, D), jnp.float32, -s_d, s_d), 'gate_b': jax.random.uniform(ks[2], (E,), jnp.float32, -s_d, s_d), 'w1': jax.random.uniform(ks[3], (E, H, D), jnp.float32, -s_d, s_d), 'b1': jax.random.uniform(ks[4], (E, H), jnp.float32, -s_d, s_d), 'w2': jax.random.uniform(ks[5], (E, D, H), jnp.float32, -s_h, s_h), 'b2': jax.random.uniform(ks[6], (E, D), jnp.float32, -s_h, s_h)}
    _L0_ffn_all = _L0_ffn_setup()
    _L0_ffn_in = {k: v for k, v in _L0_ffn_all.items() if k in ('gate_w', 'gate_b', 'w1', 'b1', 'w2', 'b2')}
    del _L0_ffn_all
    return {'x': x, 'ctx_512': ctx_512, 'L0_attn_W_qkv': _L0_attn_in['W_qkv'], 'L0_attn_RF': _L0_attn_in['RF'], 'L0_attn_W_out': _L0_attn_in['W_out'], 'L0_attn_b_out': _L0_attn_in['b_out'], 'L0_xattn_Wk': _L0_xattn_in['Wk'], 'L0_xattn_bk': _L0_xattn_in['bk'], 'L0_xattn_Wq': _L0_xattn_in['Wq'], 'L0_xattn_bq': _L0_xattn_in['bq'], 'L0_xattn_Wv': _L0_xattn_in['Wv'], 'L0_xattn_bv': _L0_xattn_in['bv'], 'L0_xattn_Wck': _L0_xattn_in['Wck'], 'L0_xattn_bck': _L0_xattn_in['bck'], 'L0_xattn_Wcq': _L0_xattn_in['Wcq'], 'L0_xattn_bcq': _L0_xattn_in['bcq'], 'L0_xattn_Wcv': _L0_xattn_in['Wcv'], 'L0_xattn_bcv': _L0_xattn_in['bcv'], 'L0_xattn_Wp': _L0_xattn_in['Wp'], 'L0_xattn_bp': _L0_xattn_in['bp'], 'L0_ffn_gate_w': _L0_ffn_in['gate_w'], 'L0_ffn_gate_b': _L0_ffn_in['gate_b'], 'L0_ffn_w1': _L0_ffn_in['w1'], 'L0_ffn_b1': _L0_ffn_in['b1'], 'L0_ffn_w2': _L0_ffn_in['w2'], 'L0_ffn_b2': _L0_ffn_in['b2']}

def reference(x, ctx_512, L0_attn_W_qkv, L0_attn_RF, L0_attn_W_out, L0_attn_b_out, L0_xattn_Wk, L0_xattn_bk, L0_xattn_Wq, L0_xattn_bq, L0_xattn_Wv, L0_xattn_bv, L0_xattn_Wck, L0_xattn_bck, L0_xattn_Wcq, L0_xattn_bcq, L0_xattn_Wcv, L0_xattn_bcv, L0_xattn_Wp, L0_xattn_bp, L0_ffn_gate_w, L0_ffn_gate_b, L0_ffn_w1, L0_ffn_b1, L0_ffn_w2, L0_ffn_b2):
    import jax
    import jax.numpy as jnp

    def _L0_attn_ref(x, W_qkv, RF, W_out, b_out):
        import jax, jax.numpy as jnp
        import numpy as np
        import math
        B, N, DIM = (4, 1024, 256)
        HEADS, DHEAD, NRF = (16, 64, 64)
        STAB = 1e-06

        def _phi(t, RF):
            return jax.nn.relu(jnp.einsum('bhnd,hdr->bhnr', t, RF))
        b, n, _ = x.shape
        qkv = x @ W_qkv
        q, k, v = jnp.split(qkv, 3, axis=-1)

        def to_heads(t):
            return t.reshape(b, n, HEADS, DHEAD).transpose(0, 2, 1, 3)
        q, k, v = (to_heads(q), to_heads(k), to_heads(v))
        phi_q = _phi(q, RF)
        phi_k = _phi(k, RF)
        kv = jnp.einsum('bhnr,bhnd->bhrd', phi_k, v)
        out = jnp.einsum('bhnr,bhrd->bhnd', phi_q, kv)
        k_sum = phi_k.sum(axis=2)
        normalizer = jnp.einsum('bhnr,bhr->bhn', phi_q, k_sum)[..., None] + STAB
        out = out / normalizer
        out = out.transpose(0, 2, 1, 3).reshape(b, n, HEADS * DHEAD)
        out = out @ W_out + b_out
        return out

    def _L0_xattn_ref(x, cross_input, Wk, bk, Wq, bq, Wv, bv, Wck, bck, Wcq, bcq, Wcv, bcv, Wp, bp):
        import jax, jax.numpy as jnp
        import numpy as np
        B, T, TC, C, CC, H = (2, 512, 128, 256, 128, 16)
        D = C // H

        def _heads(t):
            b, l, _ = t.shape
            return t.reshape(b, l, H, D).transpose(0, 2, 1, 3)
        scale = np.float32(1.0 / np.sqrt(D))
        q = _heads(x @ Wq + bq)
        k = _heads(x @ Wk + bk)
        v = _heads(x @ Wv + bv)
        att = jnp.einsum('bhqd,bhkd->bhqk', q, k) * scale
        causal = jnp.tril(jnp.ones((T, T), bool))
        att = jnp.where(causal[None, None], att, -jnp.inf)
        y = jnp.einsum('bhqk,bhkd->bhqd', jax.nn.softmax(att, axis=-1), v)
        qc = _heads(x @ Wcq + bcq)
        kc = _heads(cross_input @ Wck + bck)
        vc = _heads(cross_input @ Wcv + bcv)
        attc = jnp.einsum('bhqd,bhkd->bhqk', qc, kc) * scale
        y = y + jnp.einsum('bhqk,bhkd->bhqd', jax.nn.softmax(attc, axis=-1), vc)
        y = y.transpose(0, 2, 1, 3).reshape(x.shape[0], T, C)
        return y @ Wp + bp

    def _L0_ffn_ref(x, gate_w, gate_b, w1, b1, w2, b2):
        import jax, jax.numpy as jnp
        import numpy as np
        B, S, D, H, E = (4, 512, 256, 1024, 8)
        b, s, d = x.shape
        xf = x.reshape(-1, d)
        logits = xf @ gate_w.T + gate_b
        top1 = jnp.argmax(logits, axis=-1)
        out = jnp.zeros_like(xf)
        n_experts = w1.shape[0]
        for e in range(n_experts):
            h = jax.nn.relu(xf @ w1[e].T + b1[e])
            y = h @ w2[e].T + b2[e]
            out = out + jnp.where((top1 == e)[:, None], y, jnp.zeros((), y.dtype))
        return out.reshape(b, s, d)
    x = _layernorm(x + _L0_attn_ref(x, L0_attn_W_qkv, L0_attn_RF, L0_attn_W_out, L0_attn_b_out), axis=-1)
    x = _layernorm(x + _L0_xattn_ref(x, ctx_512, L0_xattn_Wk, L0_xattn_bk, L0_xattn_Wq, L0_xattn_bq, L0_xattn_Wv, L0_xattn_bv, L0_xattn_Wck, L0_xattn_bck, L0_xattn_Wcq, L0_xattn_bcq, L0_xattn_Wcv, L0_xattn_bcv, L0_xattn_Wp, L0_xattn_bp), axis=-1)
    x = _layernorm(x + _L0_ffn_ref(x, L0_ffn_gate_w, L0_ffn_gate_b, L0_ffn_w1, L0_ffn_b1, L0_ffn_w2, L0_ffn_b2), axis=-1)
    return x

_drawn_inputs = setup_inputs


def setup_inputs(seed=0):
    import zlib

    import numpy as np

    out = dict(_drawn_inputs(seed))
    spreads = {'L0_attn_b_out': (0.0, 0.1),
     'L0_xattn_bk': (0.0, 0.8),
     'L0_xattn_bq': (0.0, 0.1),
     'L0_xattn_bv': (0.0, 0.1),
     'L0_xattn_bck': (0.0, 0.8),
     'L0_xattn_bcq': (0.0, 0.1),
     'L0_xattn_bcv': (0.0, 0.1),
     'L0_xattn_bp': (0.0, 0.1)}
    factors = {'L0_ffn_b1': 4.01, 'L0_ffn_b2': 3.163}
    for name, (base, spread) in spreads.items():
        noise = np.random.default_rng([zlib.crc32(name.encode()), seed]).standard_normal(out[name].shape)
        drawn = base * np.exp(spread * noise) if base else spread * noise
        out[name] = jnp.asarray(drawn.astype(out[name].dtype))
    for name, factor in factors.items():
        out[name] = (out[name] * factor).astype(out[name].dtype)
    return out
```

```python
import numpy as np
import concourse.bass as bass
from concourse import mybir
from contextlib import ExitStack

F32 = mybir.dt.float32
F32R = mybir.dt.float32r
BF16 = mybir.dt.bfloat16
I32 = mybir.dt.int32
U32 = mybir.dt.uint32
ALU = mybir.AluOpType
ACT = mybir.ActivationFunctionType
AX = mybir.AxisListType

P = 128
B, T, C = 8, 512, 256
NT = T // P
KC = C // P
LH, LD = 16, 64
LR = LH * LD
NPAIR = LH // 2
XH, XD = 16, 16
TC_, CC = 1024, 128
NTC = TC_ // P
E, HID = 8, 1024
NHC = HID // P
LN_EPS = 1e-5
STAB = 1e-6
SCALE = float(1.0 / np.sqrt(XD))
NEG = -1e30
KROW = 4 * XD
MROW = KROW
VW = XD + 1

JOBS = [("kf0", "D"), ("qf0", "A"), ("kf1", "D"), ("qf1", "A"), ("kf2", "D"), ("qf2", "A"), ("kf3", "D"),
        ("qf3", "A"), ("g0", "A"), ("g1", "D"), ("ksum", "D"), ("kv", "A"), ("norm", "D"), ("m0", "A"),
        ("m1", "A"), ("rT", "A"), ("bc0", "D"), ("bc1", "D"), ("bc2", "D"), ("bc3", "D"), ("attn", "D"),
        ("vc0", "D"), ("vc1", "D"), ("kc0", "B"), ("kc1", "B"),
        ("x1T", "A"), ("k", "B"), ("q", "B"), ("qc", "B"), ("v", "D"),
        ("yT", "A"), ("proj", "D"), ("x2T", "A"), ("gate", "D")]
NJ = len(JOBS)
JN = {name: n for n, (name, _) in enumerate(JOBS)}
ACT_AT = {name: sum(w in "AB" for _, w in JOBS[:n + 1]) for n, (name, w) in enumerate(JOBS)}
DVE_AT = {name: sum(w in "DB" for _, w in JOBS[:n + 1]) for n, (name, w) in enumerate(JOBS)}
N_ACT, N_DVE = ACT_AT["gate"], DVE_AT["gate"]
STAGED = ["kc0", "kc1", "k", "q", "qc"]
STORES = {"kc0": 1, "kc1": 1, "k": 2, "q": 2, "qc": 2}

NSB = 3 + 2 * NT
SELF_MAX = [[(3, 0)], [(2, 0), (0, 384)], [(1, 0)]]
NE_ = 2 + NTC // 2
SELF_EXP = [[(0, 0), (1, 512), (3, 896)], [(2, 0)]]
S_PLAN = [3, 2, 2, 2, 2, 0]
HS = 4
HG = 4


def heads_order():
    order = [("bank", 0, n) for n in range(NSB)] + [("maxima", 0, 0)]
    for h in range(XH):
        s = 0
        for n in range(NE_):
            order.append(("scores", h, n))
            if h + 1 < XH:
                for _ in range(S_PLAN[n]):
                    order.append(("bank", h + 1, s))
                    s += 1
            if n == 0 and h and h % HG == 0:
                order.append(("keep", h // HG - 1, 0))
            if n == 2 and h and h % HG == 0:
                order += [("turn", h // HG - 1, 0), ("turn", h // HG - 1, 1)]
            if 1 <= n < NE_ - 1:
                order.append(("weigh", h, n - 1))
        if h + 1 < XH:
            order.append(("maxima", h + 1, 0))
        order += [("weigh", h, NE_ - 2), ("weigh", h, NE_ - 1)]
    return order + [("keep", XH // HG - 1, 0), ("turn", XH // HG - 1, 0), ("turn", XH // HG - 1, 1)]


ORDER = heads_order()
RING = [e for e in ORDER if e[0] in ("bank", "maxima", "turn")]
RING_AT = {e: n for n, e in enumerate(RING)}
NRING, NRED = len(RING), sum(e[0] != "maxima" for e in RING)
RED_AT = {e: sum(f[0] != "maxima" for f in RING[:n + 1]) for n, e in enumerate(RING)}
WCOLS = 2 * 512

TILE = 256
TH = TILE // P
NTILE = -(-(B * T + E * (TILE - 1)) // TILE) // 2 * 2
MAXT = B * T // TILE
assert NTILE * TILE >= B * T + E * (TILE - 1) - (TILE - 1)


def decoder(nc, x, xT, ctxT, wqkT, wv_l, rf, w_out, b_out, wk, bk, wq, bq, wv, bv, wck, bck, wcq, bcq,
            wcv, bcv, wp, bp, gate_wT, gate_b, w1T, b1p, w2T, b2, ident_d, mask_qk, mask_kq, sel_d,
            tri_d, iota_d, out, nb=B):
    x2d = nc.dram_tensor("x2d", [B * T, C], F32, kind="Internal").ap()
    xs = nc.dram_tensor("xs", [NTILE, TILE, C], F32, kind="Internal").ap()
    ys = nc.dram_tensor("ys", [NTILE, TILE, C], F32, kind="Internal").ap()
    with nc.sbuf_tensor("onehot", [P, B * NT, E], F32) as onehot:
        attentions(nc, x, xT, ctxT, wqkT, wv_l, rf, w_out, b_out, wk, bk, wq, bq, wv, bv, wck, bck,
                   wcq, bcq, wcv, bcv, wp, bp, gate_wT, gate_b, ident_d, mask_qk, mask_kq, sel_d,
                   onehot, x2d.rearrange("(b t) c -> b t c", b=B), xs, nb)
        experts(nc, onehot, x2d, xs, ys, w1T, b1p, w2T, b2, ident_d, tri_d, iota_d, out)


def attentions(nc, x, xT, ctxT, wqkT, wv_l, rf, w_out, b_out, wk, bk, wq, bq, wv, bv, wck, bck,
               wcq, bcq, wcv, bcv, wp, bp, gate_wT, gate_b, ident_d, mask_qk, mask_kq, sel_d,
               onehot, x2d, xs, nb):
    scr_k = nc.dram_tensor("scr_k", [2, C, T + TC_], F32, kind="Internal").ap()
    scr_q = nc.dram_tensor("scr_q", [2, C, 2 * T], F32, kind="Internal").ap()

    ctx = ExitStack()
    with ctx:
        def sb(name, shape, dt=F32):
            return ctx.enter_context(nc.sbuf_tensor(name, shape, dt))

        def sem(name):
            return ctx.enter_context(nc.semaphore(name))

        ident = sb("ident", [P, P])
        identb = sb("identb", [P, P], BF16)
        mqk = sb("mqk", [P, P], BF16)
        mkq = sb("mkq", [P, P], BF16)
        sel = sb("sel", [2 * LH, NPAIR, P], F32R)
        onescol = sb("onescol", [P, 1])
        wqf = sb("wqf", [P, KC, LR])
        wkf = sb("wkf", [P, KC, LR])
        wvl = sb("wvl", [P, KC, LR])
        wo = sb("wo", [P, NPAIR, C])
        wq_s = sb("wq_s", [P, KC, C])
        wk_s = sb("wk_s", [P, KC, C])
        wcq_s = sb("wcq_s", [P, KC, C])
        wv_s = sb("wv_s", [P, KC, C])
        wp_s = sb("wp_s", [P, KC, C])
        wck_s = sb("wck_s", [P, C])
        wcv_s = sb("wcv_s", [P, C])
        gw_s = sb("gw_s", [P, KC, E])
        bias_c = sb("bias_c", [P, 4, KC])
        bo_bc = sb("bo_bc", [P, C])
        bp_bc = sb("bp_bc", [P, C])
        bv_bc = sb("bv_bc", [P, C])
        bcv_bc = sb("bcv_bc", [P, C])
        gb_bc = sb("gb_bc", [P, E])
        rank8 = sb("rank8", [P, E])
        x_s = sb("x_s", [P, NT, C])
        xT_s = sb("xT_s", [P, KC, T])
        ctxT_s = sb("ctxT_s", [P, TC_])
        big_a = sb("big_a", [P, NPAIR * T])
        big_b = sb("big_b", [P, NT * LR])
        phiq = big_a[:].rearrange("p (j t) -> p j t", j=NPAIR)
        phik = big_b[:].rearrange("p (i r) -> p i r", i=NT)
        rfbd = big_a[:, 0:NPAIR * P].rearrange("p (j r) -> p j r", j=NPAIR)
        wqkT_s = big_b[:].rearrange("p (j c) -> p j c", j=2 * NPAIR)
        exps = big_a[:].rearrange("p (n c) -> p n c", n=4)
        stage = big_b[:].rearrange("p (n w c) -> p n w c", n=2, w=2)
        g_s = sb("g_s", [P, KC, LR])
        kvbd = sb("kvbd", [P, NPAIR, P])
        m_s = sb("m_s", [P, NPAIR, C])
        sel_f = m_s[0:2 * LH, 0:4, :].rearrange("p a c -> p (a c)").rearrange("p (j r) -> p j r", j=NPAIR)
        ksbd = sb("ksbd", [P, NPAIR * LH])
        den = sb("den", [P, NT, LH])
        rden = sb("rden", [P, NT, LH])
        rhl = sb("rhl", [P, NT, 2 * LH], F32R)
        rT = sb("rT", [2 * LH, T], F32R)
        xb = sb("xb", [P, NT, C])
        r_s = sb("r_s", [P, NT, C])
        cstage = r_s[:, 0, :]
        stats = sb("stats", [P, NT, 6])
        mv = sb("mv", [P, 4, NT])
        zero1 = sb("zero1", [P, 1])
        nwt = sb("nwt", [P, 5, NT])
        nwi = sb("nwi", [P, 2, NT], I32)
        x1 = sb("x1", [P, NT, C])
        x1T = sb("x1T", [P, KC, T])
        va = sb("va", [P, NT, XH, VW])
        vca = sb("vca", [P, NTC, XH, VW])
        hk = [sb(f"hk{i}", [P, T + TC_], F32R) for i in range(HS)]
        hq = [sb(f"hq{i}", [P, 2 * T], F32R) for i in range(HS)]
        mpad = sb("mpad", [P, NT, P])
        cmax = sb("cmax", [P, NT, 2])
        ykeep = sb("ykeep", [P, 2, T])
        rec = sb("rec", [P, 2, NT, HG])
        yn = sb("yn", [P, 2, NT, HG, XD])
        y_s = sb("y_s", [P, NT, C])
        yT_s = g_s[:, :, 0:T]
        lg = sb("lg", [P, NT, E])
        lmax = sb("lmax", [P, NT])
        lw = sb("lw", [P, NT, E])

        ps = [ctx.enter_context(nc.psum_tensor(f"ps{i}", [P, WCOLS], F32)) for i in range(4)]

        s_const = sem("s_const")
        s_rf = sem("s_rf")
        s_sel = sem("s_sel")
        s_setup = sem("s_setup")
        s_wprod = sem("s_wprod")
        s_x = sem("s_x")
        s_tile = sem("s_tile")
        s_act = sem("s_act")
        s_dve = sem("s_dve")
        s_dstep = sem("s_dstep")
        s_xb = sem("s_xb")
        s_ln = sem("s_ln")
        s_st = {n: sem(f"s_st_{n}") for n in STAGED}
        s_hl = [sem(f"s_hl{i}") for i in range(HS)]
        s_zero = sem("s_zero")
        s_sc = sem("s_sc")
        s_red = sem("s_red")
        s_max = sem("s_max")
        s_mrow = sem("s_mrow")
        s_st2 = sem("s_st2")
        s_exp = sem("s_exp")
        s_av = sem("s_av")
        s_keep = sem("s_keep")
        s_ys = sem("s_ys")
        s_pace = sem("s_pace")
        s_zx = sem("s_zx")
        s_x2 = sem("s_x2")

        def cur(b, per, k):
            return b * per + (per + k)

        block = ctx.enter_context(nc.Block())
        LOADS = 23
        xs_flat = xs.rearrange("t r c -> (t r c)").rearrange("(p n) -> p n", p=P)
        NZ = xs_flat.shape[1] // (NPAIR * P)

        @block.sync
        def _(sp):
            def const(dst, src):
                sp.dma_start(dst, src).then_inc(s_const, 16)

            sp.sem_inc(s_x2, 16)
            for n in STAGED:
                sp.sem_inc(s_st[n], 16 * STORES[n])
            const(wqkT_s, wqkT.rearrange("(j p) c -> p j c", p=P))
            const(ident[:], ident_d)
            const(cstage[:, 0:P], mask_qk)
            const(cstage[:, P:2 * P], mask_kq)
            const(wvl[:], wv_l.rearrange("(k p) r -> p k r", p=P))
            const(wo[:], w_out.rearrange("(j p) c -> p j c", p=P))
            for dst, src in ((wq_s, wq), (wk_s, wk), (wcq_s, wcq), (wv_s, wv), (wp_s, wp)):
                const(dst[:], src.rearrange("(k p) c -> p k c", p=P))
            const(wck_s[:], wck)
            const(wcv_s[:], wcv)
            const(gw_s[:], gate_wT.rearrange("(k p) e -> p k e", p=P))
            for n, src in enumerate((bk, bck, bq, bcq)):
                sp.dma_start(bias_c[:, n, :], src.rearrange("(k p) -> p k", p=P),
                             allow_slow_non_contiguous=True).then_inc(s_const, 16)
            for dst, src in ((bo_bc, b_out), (bp_bc, bp), (bv_bc, bv), (bcv_bc, bcv), (gb_bc, gate_b)):
                const(dst[:], src.rearrange("(a c) -> a c", a=1).broadcast_to([P, dst.shape[1]]))
            sp.dma_start(sel_f, sel_d).then_inc(s_sel, 16)
            sp.wait_ge(s_setup, 1)
            rf_v = rf.rearrange("(j a) d r -> a d j r", a=2)
            sp.dma_start(rfbd[0:LD, :, 0:LD], rf_v[0]).then_inc(s_rf, 16)
            sp.dma_start(rfbd[LD:P, :, LD:P], rf_v[1]).then_inc(s_rf, 16)

            def load_x(b):
                sp.dma_start(x_s[:], x[b].rearrange("(i p) c -> p i c", p=P)).then_inc(s_x, 16)
                sp.dma_start(xT_s[:], xT[b].rearrange("(k p) t -> p k t", p=P)).then_inc(s_x, 16)
                sp.dma_start(ctxT_s[:], ctxT[b]).then_inc(s_x, 16)

            load_x(0)
            for n in range(NZ):
                sp.dma_start(xs_flat[:, n * NPAIR * P:(n + 1) * NPAIR * P],
                             kvbd[:].rearrange("p j r -> p (j r)")).then_inc(s_zx, 16)

            def store(name, stg, scr, cols, m0, nm, b):
                sp.wait_ge(s_dve, cur(b, N_DVE, DVE_AT[name]))
                w = (cols.stop - cols.start)
                for m in range(nm):
                    src = stage[:, stg, :, m * w:(m + 1) * w]
                    dst = scr[:, (m0 + m) * P:(m0 + m + 1) * P, cols].rearrange("w r t -> r w t")
                    sp.dma_start(dst, src).then_inc(s_st[name], 16)

            def load_head(b, h):
                i = h % HS
                sp.wait_ge(s_zero, cur(b, XH, h - HS + 1))
                sp.sem_inc(s_pace, 1)
                sp.wait_ge(s_st2, cur(b, XH * NE_, (h - HS + 1) * NE_))
                sp.sem_inc(s_pace, 1)
                for w in range(2):
                    sp.dma_start(hk[i][32 * w:32 * w + 32, :].bitcast(F32),
                                 scr_k[:, h * XD:(h + 1) * XD, :]).then_inc(s_hl[i], 16)
                    for d in range(2):
                        sp.dma_start(hq[i][32 * w + 16 * d:32 * w + 16 * d + 16, :].bitcast(F32),
                                     scr_q[w, h * XD:(h + 1) * XD, :]).then_inc(s_hl[i], 16)

            with sp.Fori(0, nb) as b:
                store("kc0", 0, scr_k, slice(T, T + TC_), 0, 1, b)
                store("kc1", 1, scr_k, slice(T, T + TC_), 1, 1, b)
                store("k", 0, scr_k, slice(0, T), 0, 2, b)
                store("q", 1, scr_q, slice(0, T), 0, 2, b)
                store("qc", 0, scr_q, slice(T, 2 * T), 0, 2, b)
                following = sp.snap((b + 1) % nb)
                for n in STAGED:
                    sp.wait_ge(s_st[n], cur(b, 16 * STORES[n], 16 * STORES[n]))
                    sp.sem_inc(s_pace, 1)
                for h in range(XH):
                    load_head(b, h)
                    if h == 3:
                        sp.wait_ge(s_xb, cur(b, 2, 1))
                        sp.sem_inc(s_pace, 1)
                        sp.wait_ge(s_tile, cur(b, NJ, JN["v"] + 1))
                        sp.sem_inc(s_pace, 1)
                        load_x(following)
                sp.wait_ge(s_ln, cur(b, 2, 2))
                sp.sem_inc(s_pace, 1)
                sp.dma_start(x2d[b].rearrange("(i p) c -> p i c", p=P), x1[:]).then_inc(s_x2, 16)
            sp.wait_ge(s_x2, (nb + 1) * 16)
            sp.wait_ge(s_x, (nb + 1) * 48)

        @block.gpsimd
        def _(pool):
            pool.sem_inc(s_xb, 2)
            pool.sem_inc(s_zero, XH)
            pool.wait_ge(s_const, 16 * LOADS)
            pool.wait_ge(s_setup, 2)
            with pool.Fori(0, nb) as b:
                pool.wait_ge(s_x, (b + 1) * 48)
                pool.wait_ge(s_dve, cur(b, N_DVE, DVE_AT["proj"] - N_DVE))
                for i in range(NT):
                    last = nc.gpsimd.tensor_tensor(xb[:, i, :], x_s[:, i, :], bo_bc[:], ALU.add)
                last.then_inc(s_xb, 1)
                pool.wait_ge(s_ln, cur(b, 2, 1))
                for i in range(NT):
                    last = nc.gpsimd.tensor_tensor(xb[:, i, :], x1[:, i, :], bp_bc[:], ALU.add)
                last.then_inc(s_xb, 1)
                pool.wait_ge(s_xb, cur(b, 2, 2))
                for h in range(XH):
                    pool.wait_ge(s_st2, cur(b, XH * NE_, (h + 1) * NE_))
                    z = zero1[MROW:MROW + 1, :].broadcast_to([1, 2 * T])
                    nc.gpsimd.tensor_tensor(hq[h % HS][MROW:MROW + 1, :], z, z, ALU.add).then_inc(s_zero, 1)
                    pool.wait_ge(s_zero, cur(b, XH, h + 1))

        @block.tensor
        def _(pe):
            mm, tr = nc.tensor.matmul, nc.tensor.transpose
            pe.sem_inc(s_tile, NJ)
            pe.sem_inc(s_sc, NRING)
            pe.sem_inc(s_st2, XH * NE_)
            pe.sem_inc(s_av, XH * NE_)

            pe.wait_ge(s_const, 16 * LOADS)
            pe.wait_ge(s_rf, 32)
            for n in range(4):
                q, c = n // 2, n % 2
                for j in range(NPAIR):
                    last = mm(ps[n][:, j * P:(j + 1) * P], wqkT_s[:, q * NPAIR + j, c * P:(c + 1) * P],
                              rfbd[:, j, :], start=True, stop=True)
                last.then_inc(s_wprod, 1)

            def job(b, name, fill, act=None, dve=None):
                n = JN[name]
                prev = n - 4 if n >= 4 else max(m for m in range(NJ) if m % 4 == n % 4)
                back = n < 4
                former, who = JOBS[prev]
                a = [ACT_AT[former] - back * N_ACT] if who == "A" else []
                d = [DVE_AT[former] - back * N_DVE] if who != "A" else []
                a += [ACT_AT[act]] if act else []
                d += [DVE_AT[dve]] if dve else []
                if a:
                    pe.wait_ge(s_act, cur(b, N_ACT, max(a)))
                if d:
                    pe.wait_ge(s_dve, cur(b, N_DVE, max(d)))
                fill(ps[n % 4]).then_inc(s_tile, 1)

            def ring_bank(b, entry):
                n = RING_AT[entry]
                if n >= 2:
                    kind, h, _ = former = RING[n - 2]
                    if kind == "maxima":
                        pe.wait_ge(s_mrow, cur(b, XH, h + 1))
                    else:
                        pe.wait_ge(s_red, cur(b, NRED, RED_AT[former]))
                return ps[2][:, (n % 2) * 512:(n % 2) * 512 + 512]

            def score_bank(b, h, n):
                if n == 0:
                    pe.wait_ge(s_hl[h % HS], (b * (XH // HS) + (h // HS + 1)) * (6 * 16))
                    pe.wait_ge(s_zero, cur(b, XH, h - HS + 1))
                pb = ring_bank(b, ("bank", h, n))
                hk_, hq_ = hk[h % HS], hq[h % HS]
                if n < 3:
                    for i, col in SELF_MAX[n]:
                        w = (i + 1) * P
                        mm(pb[:, col:col + w], hq_[:, i * P:(i + 1) * P], hk_[:, 0:w], start=True, stop=False)
                        last = mm(pb[:, col + w - P:col + w], identb[:], mqk[:], start=False, stop=True)
                else:
                    i, half = (n - 3) // 2, (n - 3) % 2
                    last = mm(pb, hq_[:, T + i * P:T + (i + 1) * P],
                              hk_[:, T + half * 512:T + (half + 1) * 512], start=True, stop=True)
                last.then_inc(s_sc, 1)

            def maxima_row(b, h):
                pb = ring_bank(b, ("maxima", h, 0))
                pe.wait_ge(s_max, cur(b, XH, h + 1))
                for i in range(NT):
                    last = tr(pb[:, i * P:(i + 1) * P], mpad[:, i, :], ident[:])
                last.then_inc(s_sc, 1)

            def exp_scores(b, h, n):
                g = h * NE_ + n
                pb = ps[g % 2]
                if n == 0:
                    pe.wait_ge(s_mrow, cur(b, XH, h + 1))
                pe.wait_ge(s_exp, cur(b, XH * NE_, g - 1))
                hk_, hq_ = hk[h % HS], hq[h % HS]
                if n < 2:
                    for j, col in SELF_EXP[n]:
                        mm(pb[:, col:col + T - j * P], hk_[:, j * P:(j + 1) * P], hq_[:, j * P:T],
                           start=True, stop=False)
                        last = mm(pb[:, col:col + P], identb[:], mkq[:], start=False, stop=True)
                else:
                    for a in range(2):
                        j = 2 * (n - 2) + a
                        last = mm(pb[:, a * 512:(a + 1) * 512], hk_[:, T + j * P:T + (j + 1) * P],
                                  hq_[:, T:2 * T], start=True, stop=True)
                last.then_inc(s_st2, 1)

            def weigh(b, h, n):
                g = h * NE_ + n
                pe.wait_ge(s_exp, cur(b, XH * NE_, g + 1))
                if n == 0 and h % HG == 0:
                    pe.wait_ge(s_keep, cur(b, XH // HG, h // HG))
                rows_ = slice(32 * (h % HG), 32 * (h % HG) + VW)
                e = exps[:, g % 4, :]
                if n < 2:
                    for j, col in SELF_EXP[n]:
                        last = mm(ps[3][rows_, j * P:T], va[:, j, h, :], e[:, col:col + T - j * P],
                                  start=n == 0 and j == 0, stop=n == 1)
                else:
                    for a in range(2):
                        j = 2 * (n - 2) + a
                        last = mm(ps[3][rows_, 512:1024], vca[:, j, h, :], e[:, a * 512:(a + 1) * 512],
                                  start=j == 0, stop=j == NTC - 1)
                last.then_inc(s_av, 1)

            def turn_results(b, g, w):
                pb = ring_bank(b, ("turn", g, w))
                pe.wait_ge(s_keep, cur(b, XH // HG, g + 1))
                for i in range(NT):
                    last = tr(pb[:, i * P:(i + 1) * P], ykeep[:, w, i * P:(i + 1) * P], ident[:])
                last.then_inc(s_sc, 1)

            with pe.Fori(0, nb) as b:
                pe.wait_ge(s_x, (b + 1) * 48)
                pe.wait_ge(s_setup, 2)

                def kfeat(i):
                    def fill(t):
                        for half in range(2):
                            for c in range(KC):
                                last = mm(t[:, half * 512:(half + 1) * 512], xT_s[:, c, i * P:(i + 1) * P],
                                          wkf[:, c, half * 512:(half + 1) * 512], start=c == 0, stop=c == KC - 1)
                        return last
                    return fill

                def qfeat(i):
                    def fill(t):
                        for a in range(2):
                            j = 2 * i + a
                            for c in range(KC):
                                last = mm(t[:, a * T:(a + 1) * T], wqf[:, c, j * P:(j + 1) * P],
                                          xT_s[:, c, :], start=c == 0, stop=c == KC - 1)
                        return last
                    return fill

                for i in range(NT):
                    job(b, f"kf{i}", kfeat(i))
                    job(b, f"qf{i}", qfeat(i))

                def gprod(m):
                    def fill(t):
                        for half in range(2):
                            for i in range(NT):
                                last = mm(t[:, half * 512:(half + 1) * 512], x_s[:, i, m * P:(m + 1) * P],
                                          phik[:, i, half * 512:(half + 1) * 512], start=i == 0, stop=i == NT - 1)
                        return last
                    return fill

                job(b, "g0", gprod(0), dve="kf3")
                job(b, "g1", gprod(1))

                def fsum(t):
                    for j in range(NPAIR):
                        for i in range(NT):
                            last = mm(t[:, j:j + 1], phik[:, i, j * P:(j + 1) * P], onescol[:],
                                      start=i == 0, stop=i == NT - 1)
                    return last

                job(b, "ksum", fsum)

                def kvprod(t):
                    for j in range(NPAIR):
                        for c in range(KC):
                            last = mm(t[:, j * P:(j + 1) * P], wvl[:, c, j * P:(j + 1) * P],
                                      g_s[:, c, j * P:(j + 1) * P], start=c == 0, stop=c == KC - 1)
                    return last

                job(b, "kv", kvprod, act="g0", dve="g1")

                def normprod(t):
                    for i in range(NT):
                        for j in range(NPAIR):
                            last = mm(t[:, i * LH:(i + 1) * LH], phiq[:, j, i * P:(i + 1) * P],
                                      ksbd[:, j * LH:(j + 1) * LH], start=j == 0, stop=j == NPAIR - 1)
                    return last

                job(b, "norm", normprod, act="qf3", dve="ksum")

                def mprod(k):
                    def fill(t):
                        for a in range(4):
                            j = 4 * k + a
                            last = mm(t[:, a * C:(a + 1) * C], kvbd[:, j, :], wo[:, j, :], start=True, stop=True)
                        return last
                    return fill

                job(b, "m0", mprod(0), act="kv")
                job(b, "m1", mprod(1))

                def rturn(t):
                    for i in range(NT):
                        last = tr(t[0:2 * LH, i * P:(i + 1) * P], rhl[:, i, :].bitcast(F32), ident[:])
                    return last

                job(b, "rT", rturn, dve="norm")

                def spread(k):
                    def fill(t):
                        for a in range(2):
                            last = mm(t[:, a * T:(a + 1) * T], sel[:, 2 * k + a, :], rT[:], start=True, stop=True)
                        return last
                    return fill

                for k in range(4):
                    job(b, f"bc{k}", spread(k), act="rT")

                def attn(t):
                    for i in range(NT):
                        for j in range(NPAIR):
                            last = mm(t[:, i * C:(i + 1) * C], phiq[:, j, i * P:(i + 1) * P], m_s[:, j, :],
                                      start=j == 0, stop=j == NPAIR - 1)
                    return last

                job(b, "attn", attn, act="m1", dve="bc3")

                def vcprod(k):
                    def fill(t):
                        for a in range(4):
                            last = mm(t[:, a * C:(a + 1) * C], ctxT_s[:, (4 * k + a) * P:(4 * k + a + 1) * P],
                                      wcv_s[:], start=True, stop=True)
                        return last
                    return fill

                def kcprod(m):
                    def fill(t):
                        for half in range(2):
                            last = mm(t[:, half * 512:(half + 1) * 512], wck_s[:, m * P:(m + 1) * P],
                                      ctxT_s[:, half * 512:(half + 1) * 512], start=True, stop=True)
                        return last
                    return fill

                job(b, "vc0", vcprod(0))
                job(b, "vc1", vcprod(1))
                job(b, "kc0", kcprod(0))
                job(b, "kc1", kcprod(1))

                def turn(src):
                    def fill(t):
                        for c in range(KC):
                            for i in range(NT):
                                last = tr(t[:, c * T + i * P:c * T + (i + 1) * P], src[:, i, c * P:(c + 1) * P], ident[:])
                        return last
                    return fill

                pe.wait_ge(s_ln, cur(b, 2, 1))
                job(b, "x1T", turn(x1))
                def proj(w):
                    def fill(t):
                        for m in range(2):
                            for c in range(KC):
                                last = mm(t[:, m * T:(m + 1) * T], w[:, c, m * P:(m + 1) * P], x1T[:, c, :],
                                          start=c == 0, stop=c == KC - 1)
                        return last
                    return fill

                def rows(src, w):
                    def fill(t):
                        for i in range(NT):
                            for c in range(KC):
                                last = mm(t[:, i * C:(i + 1) * C], src[:, c, i * P:(i + 1) * P], w[:, c, :],
                                          start=c == 0, stop=c == KC - 1)
                        return last
                    return fill

                job(b, "k", proj(wk_s), act="x1T")
                job(b, "q", proj(wq_s))
                job(b, "qc", proj(wcq_s))
                job(b, "v", rows(x1T, wv_s))

                pe.wait_ge(s_dve, cur(b, N_DVE, DVE_AT["v"]))

                for kind, h, n in ORDER:
                    if kind == "bank":
                        score_bank(b, h, n)
                    elif kind == "maxima":
                        maxima_row(b, h)
                    elif kind == "scores":
                        exp_scores(b, h, n)
                    elif kind == "weigh":
                        weigh(b, h, n)
                    elif kind == "turn":
                        turn_results(b, h, n)

                pe.wait_ge(s_ys, cur(b, XH // HG, XH // HG))
                job(b, "yT", turn(y_s))
                job(b, "proj", rows(yT_s, wp_s), act="yT")
                pe.wait_ge(s_ln, cur(b, 2, 2))
                job(b, "x2T", turn(x1))
                def gate(t):
                    for i in range(NT):
                        for c in range(KC):
                            last = mm(t[:, i * E:(i + 1) * E], x1T[:, c, i * P:(i + 1) * P], gw_s[:, c, :],
                                      start=c == 0, stop=c == KC - 1)
                    return last

                job(b, "gate", gate, act="x2T")

        @block.scalar
        def _(act):
            act.sem_inc(s_act, N_ACT)
            act.sem_inc(s_mrow, XH)
            act.sem_inc(s_exp, XH * NE_)
            act.sem_inc(s_keep, XH // HG)
            with act.Fori(0, nb) as b:
                def full(name):
                    act.wait_ge(s_tile, cur(b, NJ, JN[name] + 1))
                    return ps[JN[name] % 4]

                def relu_q(i):
                    t = full(f"qf{i}")
                    nc.scalar.activation(phiq[:, 2 * i:2 * i + 2, :], t[:].rearrange("p (a t) -> p a t", a=2),
                                         ACT.Relu).then_inc(s_act, 1)

                for i in range(NT):
                    relu_q(i)
                t = full("g0")
                nc.scalar.activation(g_s[:, 0, :], t[:], ACT.Copy).then_inc(s_act, 1)
                t = full("kv")
                act.wait_ge(s_setup, 2)
                act.wait_ge(s_zx, 16 * NZ)
                tv = t[:].rearrange("p (j r) -> p j r", j=NPAIR)
                nc.scalar.activation(kvbd[0:LD, :, 0:LD], tv[0:LD, :, 0:LD], ACT.Copy)
                nc.scalar.activation(kvbd[LD:P, :, LD:P], tv[LD:P, :, LD:P], ACT.Copy).then_inc(s_act, 1)
                for k in range(2):
                    t = full(f"m{k}")
                    nc.scalar.activation(m_s[:, 4 * k:4 * k + 4, :], t[:].rearrange("p (a c) -> p a c", a=4),
                                         ACT.Copy).then_inc(s_act, 1)
                t = full("rT")
                nc.scalar.activation(rT[:], t[0:2 * LH, 0:T], ACT.Copy).then_inc(s_act, 1)

                def high_part(name, stg, bias_n, whole_m=None):
                    t = full(name)
                    used = {"kc0": "qc", "kc1": "q", "k": "kc0", "q": "kc1", "qc": "k"}[name]
                    back = 1 if name in ("kc0", "kc1") else 0
                    act.wait_ge(s_st[used], cur(b, 16 * STORES[used], (1 - back) * 16 * STORES[used]))
                    if whole_m is not None:
                        last = nc.scalar.activation(stage[:, stg, 0, :].bitcast(F32R), t[:], ACT.Identity,
                                                    bias=bias_c[:, bias_n, whole_m:whole_m + 1])
                    else:
                        for m in range(2):
                            last = nc.scalar.activation(stage[:, stg, 0, m * T:(m + 1) * T].bitcast(F32R),
                                                        t[:, m * T:(m + 1) * T], ACT.Identity,
                                                        bias=bias_c[:, bias_n, m:m + 1])
                    last.then_inc(s_act, 1)

                high_part("kc0", 0, 1, 0)
                high_part("kc1", 1, 1, 1)
                t = full("x1T")
                nc.scalar.activation(x1T[:], t[:].rearrange("p (c t) -> p c t", c=KC), ACT.Copy).then_inc(s_act, 1)
                high_part("k", 0, 0)
                high_part("q", 1, 2)
                high_part("qc", 0, 3)

                def maxima(h):
                    n = RING_AT["maxima", h, 0]
                    act.wait_ge(s_sc, cur(b, NRING, n + 1))
                    pb = ps[2][:, (n % 2) * 512:(n % 2) * 512 + 512]
                    nc.scalar.activation(hq[h % HS][MROW:MROW + 1, 0:T], pb[64:65, :], ACT.Copy)
                    nc.scalar.activation(hq[h % HS][MROW:MROW + 1, T:2 * T], pb[96:97, :],
                                         ACT.Copy).then_inc(s_mrow, 1)

                def exp_step(h, n):
                    g = h * NE_ + n
                    act.wait_ge(s_st2, cur(b, XH * NE_, g + 1))
                    act.wait_ge(s_av, cur(b, XH * NE_, g - 3))
                    w = 256 if n == 1 else 1024
                    nc.scalar.activation(exps[:, g % 4, 0:w], ps[g % 2][:, 0:w], ACT.Exp,
                                         scale=SCALE).then_inc(s_exp, 1)

                def keep(g):
                    act.wait_ge(s_av, cur(b, XH * NE_, (g + 1) * HG * NE_))
                    if g:
                        n = RING_AT["turn", g - 1, 1]
                        act.wait_ge(s_sc, cur(b, NRING, n + 1))
                    for q in range(HG):
                        last = nc.scalar.activation(
                            ykeep[32 * q:32 * q + VW, :, :],
                            ps[3][32 * q:32 * q + VW, :].rearrange("p (w t) -> p w t", w=2), ACT.Copy)
                    last.then_inc(s_keep, 1)

                for kind, h, n in ORDER:
                    if kind == "maxima":
                        maxima(h)
                    elif kind == "scores":
                        exp_step(h, n)
                    elif kind == "keep":
                        keep(h)
                t = full("yT")
                nc.scalar.activation(yT_s, t[:].rearrange("p (c t) -> p c t", c=KC), ACT.Copy).then_inc(s_act, 1)
                t = full("x2T")
                nc.scalar.activation(x1T[:], t[:].rearrange("p (c t) -> p c t", c=KC), ACT.Copy).then_inc(s_act, 1)

        @block.vector
        def _(dve):
            v = nc.vector
            steps = [0]
            NSTEP = 52

            dve.sem_inc(s_dve, N_DVE)
            dve.sem_inc(s_ln, 2)
            dve.sem_inc(s_red, NRED)
            dve.sem_inc(s_max, XH)
            dve.sem_inc(s_ys, XH // HG)

            for t in (rfbd, kvbd[:]):
                v.memset(t, 0.0)
            v.memset(mpad[:], 0.0)
            v.memset(ksbd[:], 0.0)
            v.memset(onescol[:], 1.0)
            v.memset(zero1[:], 0.0)
            v.memset(onehot[:], 0.0)
            v.memset(va[:], 1.0)
            v.memset(vca[:], 1.0)
            for e in range(E):
                v.memset(rank8[:, e:e + 1], float(E - e))
            for i in range(HS):
                v.memset(hk[i][MROW:P, :].bitcast(F32), 0.0)
                v.memset(hq[i][MROW:P, :].bitcast(F32), 0.0)
            v.memset(ykeep[:], 0.0).then_inc(s_setup, 1)
            dve.wait_ge(s_setup, 1)
            for i in range(HS):
                v.memset(hk[i][MROW:MROW + 1, :].bitcast(F32), -1.0)
            dve.wait_ge(s_const, 16 * LOADS)
            v.tensor_copy(identb[:], ident[:])
            v.tensor_copy(mqk[:], cstage[:, 0:P])
            v.tensor_copy(mkq[:], cstage[:, P:2 * P])
            dve.wait_ge(s_sel, 16)
            v.tensor_copy(sel[:], sel_f)
            for n, w in enumerate((wqf, wkf)):
                for c in range(KC):
                    dve.wait_ge(s_wprod, 2 * n + c + 1)
                    last = v.tensor_copy(w[:, c, :], ps[2 * n + c][:])
            last.then_inc(s_setup, 1)

            with dve.Fori(0, nb) as b:
                def step(ins):
                    steps[0] += 1
                    ins.then_inc(s_dstep, 1)
                    dve.wait_ge(s_dstep, b * NSTEP + steps[0])

                def full(name):
                    dve.wait_ge(s_tile, cur(b, NJ, JN[name] + 1))
                    return ps[JN[name] % 4]

                for n in ("q", "qc"):
                    dve.wait_ge(s_st[n], cur(b, 16 * STORES[n], 0))
                for i in range(NT):
                    t = full(f"kf{i}")
                    v.tensor_scalar(phik[:, i, :], t[:], 0.0, None, ALU.max).then_inc(s_dve, 1)
                t = full("g1")
                v.tensor_copy(g_s[:, 1, :], t[:]).then_inc(s_dve, 1)
                t = full("ksum")
                W = LH + 2
                v.tensor_copy(ksbd[0:LD, 0:7 * W + 1:W], t[0:LD, 0:NPAIR])
                v.tensor_copy(ksbd[LD:P, 1:7 * W + 2:W], t[LD:P, 0:NPAIR]).then_inc(s_dve, 1)
                t = full("norm")
                step(v.tensor_scalar(den[:], t[:, 0:NT * LH].rearrange("p (i h) -> p i h", i=NT), STAB, None, ALU.add))
                step(v.reciprocal(rden[:], den[:]))
                step(v.tensor_copy(rhl[:, :, 0:LH], rden[:]))
                v.tensor_tensor(rhl[:, :, LH:2 * LH], rden[:], rhl[:, :, 0:LH].bitcast(F32),
                                ALU.subtract).then_inc(s_dve, 1)
                for k in range(4):
                    t = full(f"bc{k}")
                    v.tensor_tensor(phiq[:, 2 * k:2 * k + 2, :], phiq[:, 2 * k:2 * k + 2, :],
                                    t[:].rearrange("p (a t) -> p a t", a=2), ALU.mult).then_inc(s_dve, 1)

                def layer_norm():
                    layer_norm_steps(v, step, r_s, x1, stats, mv, nwt, nwi, s_ln)

                t = full("attn")
                dve.wait_ge(s_xb, cur(b, 2, 1))
                v.tensor_tensor(r_s[:], t[:].rearrange("p (i c) -> p i c", i=NT), xb[:], ALU.add).then_inc(s_dve, 1)
                dve.wait_ge(s_dve, cur(b, N_DVE, DVE_AT["attn"]))
                dve.wait_ge(s_x2, cur(b, 16, 0))
                layer_norm()

                for k in range(2):
                    t = full(f"vc{k}")
                    for a in range(4):
                        last = v.tensor_tensor(vca[:, 4 * k + a, :, 0:XD],
                                               t[:, a * C:(a + 1) * C].rearrange("p (h d) -> p h d", h=XH),
                                               bcv_bc[:].rearrange("p (h d) -> p h d", h=XH), ALU.add)
                    last.then_inc(s_dve, 1)

                def low_part(name, stg, bias_n, whole_m=None):
                    t = full(name)
                    dve.wait_ge(s_act, cur(b, N_ACT, ACT_AT[name]))
                    for m in range(2):
                        bm = m if whole_m is None else whole_m
                        last = v.scalar_tensor_tensor(stage[:, stg, 1, m * 512:(m + 1) * 512].bitcast(F32R),
                                                      t[:, m * 512:(m + 1) * 512], bias_c[:, bias_n, bm:bm + 1],
                                                      stage[:, stg, 0, m * 512:(m + 1) * 512], ALU.add, ALU.subtract)
                    last.then_inc(s_dve, 1)

                low_part("kc0", 0, 1, 0)
                low_part("kc1", 1, 1, 1)
                low_part("k", 0, 0)
                low_part("q", 1, 2)
                low_part("qc", 0, 3)
                t = full("v")
                for i in range(NT):
                    last = v.tensor_tensor(va[:, i, :, 0:XD],
                                           t[:, i * C:(i + 1) * C].rearrange("p (h d) -> p h d", h=XH),
                                           bv_bc[:].rearrange("p (h d) -> p h d", h=XH), ALU.add)
                last.then_inc(s_dve, 1)

                def reduce(h, n):
                    s = RING_AT["bank", h, n]
                    if n == 0:
                        dve.wait_ge(s_max, cur(b, XH, h))
                    dve.wait_ge(s_sc, cur(b, NRING, s + 1))
                    pb = ps[2][:, (s % 2) * 512:(s % 2) * 512 + 512]
                    if n < 3:
                        for i, col in SELF_MAX[n]:
                            last = v.reduce_max(mpad[:, i, 64:65], pb[:, col:col + (i + 1) * P], AX.X)
                        last.then_inc(s_red, 1)
                    else:
                        i, half = (n - 3) // 2, (n - 3) % 2
                        v.reduce_max(cmax[:, i, half:half + 1], pb, AX.X).then_inc(s_red, 1)
                    if n == NSB - 1:
                        dve.wait_ge(s_red, cur(b, NRED, RED_AT["bank", h, n]))
                        v.tensor_tensor(mpad[:, :, 96], cmax[:, :, 0], cmax[:, :, 1], ALU.max).then_inc(s_max, 1)

                def results(g, w):
                    s = RING_AT["turn", g, w]
                    dve.wait_ge(s_sc, cur(b, NRING, s + 1))
                    tv = ps[2][:, (s % 2) * 512:(s % 2) * 512 + 512].rearrange("p (i h d) -> p i h d", i=NT, h=HG)
                    step(v.reciprocal(rec[:, w], tv[:, :, :, XD]))
                    v.tensor_tensor(yn[:, w], tv[:, :, :, 0:XD],
                                    rec[:, w].unsqueeze(3).broadcast_to([P, NT, HG, XD]), ALU.mult).then_inc(s_red, 1)
                    if w == 1:
                        dve.wait_ge(s_red, cur(b, NRED, RED_AT["turn", g, w]))
                        v.tensor_tensor(y_s[:, :, g * HG * XD:(g + 1) * HG * XD].rearrange("p i (h d) -> p i h d", h=HG),
                                        yn[:, 0], yn[:, 1], ALU.add).then_inc(s_ys, 1)
                        dve.wait_ge(s_ys, cur(b, XH // HG, g + 1))

                for kind, h, n in RING:
                    if kind == "bank":
                        reduce(h, n)
                    elif kind == "turn":
                        results(h, n)

                t = full("proj")
                dve.wait_ge(s_xb, cur(b, 2, 2))
                v.tensor_tensor(r_s[:], t[:].rearrange("p (i c) -> p i c", i=NT), xb[:], ALU.add).then_inc(s_dve, 1)
                dve.wait_ge(s_dve, cur(b, N_DVE, DVE_AT["proj"]))
                layer_norm()
                t = full("gate")
                step(v.tensor_tensor(lg[:], t[:, 0:NT * E].rearrange("p (i e) -> p i e", i=NT),
                                     gb_bc[:].unsqueeze(1).broadcast_to([P, NT, E]), ALU.add))
                step(v.reduce_max(lmax[:], lg[:], AX.X))
                step(v.tensor_tensor(lw[:], lg[:], lmax[:].unsqueeze(2).broadcast_to([P, NT, E]), ALU.is_ge))
                step(v.tensor_tensor(lw[:], lw[:], rank8[:].unsqueeze(1).broadcast_to([P, NT, E]), ALU.mult))
                step(v.reduce_max(lmax[:], lw[:], AX.X))
                v.tensor_tensor(onehot[:, bass.ds(b * NT, NT), :], lw[:],
                                lmax[:].unsqueeze(2).broadcast_to([P, NT, E]), ALU.is_equal).then_inc(s_dve, 1)
            assert steps[0] == NSTEP, steps[0]


def layer_norm_steps(v, step, src, dst, stats, mv, nwt, nwi, done, n=NT):
    for i in range(n):
        last = v.bn_stats(stats[:, i, :], src[:, i, :])
    step(last)
    even, odd = stats[:, :, 1:3], stats[:, :, 4:6]
    v.tensor_tensor(mv[:, 0:2, :].rearrange("p w i -> p i w"), even, odd, ALU.add)
    step(v.tensor_tensor(mv[:, 2, :], stats[:, :, 1], stats[:, :, 4], ALU.subtract))
    v.tensor_scalar(mv[:, 0, :], mv[:, 0, :], 0.5, None, ALU.mult)
    v.tensor_scalar(mv[:, 1, :], mv[:, 1, :], 1.0 / C, LN_EPS, ALU.mult, ALU.add)
    step(v.scalar_tensor_tensor(mv[:, 3, :], mv[:, 2, :], 0.25, mv[:, 2, :], ALU.mult, ALU.mult))
    ve = nwt[:, 0, :]
    step(v.tensor_tensor(ve, mv[:, 1, :], mv[:, 3, :], ALU.add))
    step(v.tensor_scalar(nwi[:, 0, :], ve.bitcast(I32), 1, None, ALU.logical_shift_right))
    step(v.tensor_scalar(nwi[:, 1, :], nwi[:, 0, :], -1.0, float(0x5F3759DF), ALU.mult, ALU.add))
    y0 = nwi[:, 1, :].bitcast(F32)
    for k in range(4):
        a, t2, y1 = nwt[:, 1, :], nwt[:, 2, :], nwt[:, 3 + k % 2, :]
        step(v.scalar_tensor_tensor(a, y0, -0.5, y0, ALU.mult, ALU.mult))
        step(v.tensor_tensor(t2, a, ve, ALU.mult))
        step(v.scalar_tensor_tensor(y1, t2, 1.5, y0, ALU.add, ALU.mult))
        y0 = y1
    for i in range(n):
        last = v.tensor_scalar(dst[:, i, :], src[:, i, :], mv[:, 0, i:i + 1], y0[:, i:i + 1],
                               ALU.subtract, ALU.mult)
    last.then_inc(done, 1)


def experts(nc, onehot, x2d, xs, ys, w1T, b1p, w2T, b2, ident_d, tri_d, iota_d, out):
    ctx = ExitStack()
    with ctx:
        def sb(name, shape, dt=F32):
            return ctx.enter_context(nc.sbuf_tensor(name, shape, dt))

        def sem(name):
            return ctx.enter_context(nc.semaphore(name))

        ident = sb("e_ident", [P, P])
        tri = sb("tri", [P, P])
        ones = sb("ones", [P, P])
        iota = sb("iota", [P, B * NT])
        x2s = sb("x2s", [P, B * NT, C])
        within = sb("within", [P, B * NT, E])
        cnt = sb("cnt", [P, B * NT, E])
        cum = [sb(f"cum{i}", [P, B * NT, E]) for i in range(2)]
        big = sb("big", [P, E, MAXT])
        mt = sb("mt", [P, MAXT])
        tiles = sb("tiles", [P, E])
        st = [sb(f"st{i}", [P, E]) for i in range(2)]
        eidf = sb("eidf", [P, NTILE])
        eidc = sb("eidc", [P, NTILE, E])
        eid = sb("eid", [P, NTILE], I32)
        slotf = sb("slotf", [P, B * NT])
        slot = sb("slot", [P, B * NT], U32)
        w1s = [sb(f"w1s{i}", [P, KC, HID]) for i in range(2)]
        w2s = [sb(f"w2s{i}", [P, NHC, C]) for i in range(2)]
        b1s = [sb(f"b1s{i}", [P, NHC]) for i in range(2)]
        b2s = [sb(f"b2s{i}", [P, C]) for i in range(2)]
        xin = [sb(f"xin{i}", [P, TH, C]) for i in range(2)]
        xinT = [sb(f"xinT{i}", [P, KC, TILE]) for i in range(2)]
        hT = [sb(f"hT{i}", [P, NHC, TILE]) for i in range(2)]
        yo = [sb(f"yo{i}", [P, TH, C]) for i in range(2)]
        rows = [sb(f"rows{i}", [P, NT, C]) for i in range(2)]
        res = [sb(f"res{i}", [P, NT, C]) for i in range(2)]
        stats = sb("e_stats", [P, NT, 6])
        mv = sb("e_mv", [P, 4, NT])
        nwt = sb("e_nwt", [P, 5, NT])
        nwi = sb("e_nwi", [P, 2, NT], I32)
        pr = ctx.enter_context(nc.psum_tensor("pr", [P, 2, 512], F32))
        px = ctx.enter_context(nc.psum_tensor("px", [P, 512], F32))
        ph = [ctx.enter_context(nc.psum_tensor(f"ph{i}", [P, 512], F32)) for i in range(2)]
        py = [ctx.enter_context(nc.psum_tensor(f"py{i}", [P, 512], F32)) for i in range(2)]

        s_c = sem("e_const")
        s_pace = sem("e_pace")
        s_x2 = sem("e_x2")
        s_one = sem("e_ones")
        s_cnt = sem("e_cnt")
        s_step = sem("e_step")
        s_route = sem("e_route")
        s_xs = sem("e_xs")
        s_w = [sem(f"e_w{i}") for i in range(2)]
        s_xt = sem("e_xt")
        s_xc = sem("e_xc")
        s_h = sem("e_h")
        s_ha = sem("e_ha")
        s_y = sem("e_y")
        s_yo = sem("e_yo")
        s_ys = [sem(f"e_ys{i}") for i in range(2)]
        s_g = [sem(f"e_g{i}") for i in range(2)]
        s_r = sem("e_r")
        s_ln = sem("e_ln")
        s_out = [sem(f"e_out{i}") for i in range(2)]

        block = ctx.enter_context(nc.Block())
        NH2 = NHC // 2

        @block.sync
        def _(sp):
            for dst, src in ((ident, ident_d), (tri, tri_d), (iota, iota_d)):
                sp.dma_start(dst[:], src).then_inc(s_c, 16)
            sp.dma_start(x2s[:], x2d.rearrange("(n p) c -> p n c", p=P)).then_inc(s_x2, 16)
            sp.wait_ge(s_route, 2)

            with sp.Fori(0, NTILE // 2) as tt:
                for i in range(2):
                    t = tt * 2 + i
                    e = sp.value_load(eid[0:1, bass.ds(t, 1)], min_val=0, max_val=E - 1)
                    sp.wait_ge(s_yo, tt * 2 + (i + 1))
                    sp.sem_inc(s_pace, 1)
                    sp.dma_start(w1s[i][:], w1T[bass.ds(e, 1)].rearrange("a (k p) h -> p (a k) h", p=P)).then_inc(s_w[i], 16)
                    sp.dma_start(w2s[i][:], w2T[bass.ds(e, 1)].rearrange("a (k p) c -> p (a k) c", p=P)).then_inc(s_w[i], 16)
                    sp.dma_start(b1s[i][:], b1p[bass.ds(e, 1)].rearrange("a p k -> (a p) k")).then_inc(s_w[i], 16)
                    sp.dma_start(b2s[i][:], b2[bass.ds(e, 1)].broadcast_to([P, C])).then_inc(s_w[i], 16)
                    if i == 0:
                        sp.wait_ge(s_xs, 16 * B * NT)
                    sp.dma_start(xin[i][:], xs[bass.ds(t, 1)].rearrange("a (n p) c -> p (a n) c", p=P)).then_inc(s_w[i], 16)
            for n in range(B):
                i = n % 2
                sp.wait_ge(s_ln, n + 1)
                sp.dma_start(out[n].rearrange("(i p) c -> p i c", p=P), res[i][:]).then_inc(s_out[i], 16)
            for i in range(2):
                sp.wait_ge(s_out[i], 16 * B // 2)

        @block.gpsimd
        def _(pool):
            pool.wait_ge(s_x2, 16)
            pool.wait_ge(s_route, 1)
            xs_rows = xs.rearrange("t r c -> (t r) c")
            ys_rows = ys.rearrange("t r c -> (t r) c")
            for j in range(B * NT):
                nc.gpsimd.indirect_dma_start(
                    xs_rows, bass.IndirectOffsetOnAxis(slot[:, j:j + 1], 0), x2s[:, j, :], None,
                    bounds_check=NTILE * TILE - 1).then_inc(s_xs, 16)
            for i in range(2):
                pool.wait_ge(s_ys[i], 16 * NTILE // 2 + 16)
            for n in range(B):
                if n >= 2:
                    pool.wait_ge(s_r, n - 1)
                for a in range(NT):
                    j = n * NT + a
                    nc.gpsimd.indirect_dma_start(
                        rows[n % 2][:, a, :], None, ys_rows, bass.IndirectOffsetOnAxis(slot[:, j:j + 1], 0),
                        bounds_check=NTILE * TILE - 1).then_inc(s_g[n % 2], 16)

        @block.tensor
        def _(pe):
            mm, tr = nc.tensor.matmul, nc.tensor.transpose
            oh = onehot[:].rearrange("p n e -> p (n e)")
            pe.wait_ge(s_c, 48)
            pe.wait_ge(s_one, 1)
            mm(pr[:, 0, 0:B * NT * E], tri[:], oh, start=True, stop=True)
            mm(pr[:, 1, 0:B * NT * E], ones[:], oh, start=True, stop=True).then_inc(s_cnt, 1)
            pe.sem_inc(s_xt, 2)
            pe.sem_inc(s_h, 2 * NH2)
            pe.sem_inc(s_y, 2)
            with pe.Fori(0, NTILE // 2) as tt:
                for i in range(2):
                    pe.wait_ge(s_w[i], (tt + 1) * 80)
                    pe.wait_ge(s_xc, tt * 2 + (i + 1))
                    for k in range(KC):
                        for n in range(TH):
                            last = tr(px[:, k * TILE + n * P:k * TILE + (n + 1) * P], xin[i][:, n, k * P:(k + 1) * P], ident[:])
                    last.then_inc(s_xt, 1)
                    pe.wait_ge(s_xc, tt * 2 + (i + 2))
                    for c in range(NH2):
                        g = i * NH2 + c
                        pe.wait_ge(s_ha, tt * (2 * NH2) + (2 * NH2 + g - 1))
                        for a in range(2):
                            for k in range(KC):
                                last = mm(ph[g % 2][:, a * TILE:(a + 1) * TILE],
                                          w1s[i][:, k, (2 * c + a) * P:(2 * c + a + 1) * P], xinT[i][:, k, :],
                                          start=k == 0, stop=k == KC - 1)
                        last.then_inc(s_h, 1)
                    pe.wait_ge(s_ha, tt * (2 * NH2) + (2 * NH2 + (i + 1) * NH2))
                    pe.wait_ge(s_yo, tt * 2 + (i + 1))
                    for n in range(TH):
                        for c in range(NHC):
                            last = mm(py[i][:, n * C:(n + 1) * C], hT[i][:, c, n * P:(n + 1) * P], w2s[i][:, c, :],
                                      start=c == 0, stop=c == NHC - 1)
                    last.then_inc(s_y, 1)

        @block.scalar
        def _(act):
            act.sem_inc(s_xc, 1)
            act.sem_inc(s_ha, 2 * NH2)
            for i in range(2):
                act.sem_inc(s_ys[i], 16)
            with act.Fori(0, NTILE // 2) as tt:
                for i in range(2):
                    act.wait_ge(s_xt, tt * 2 + (2 + i + 1))
                    nc.scalar.activation(xinT[i][:], px[:].rearrange("p (k t) -> p k t", k=KC), ACT.Copy).then_inc(s_xc, 1)
                    act.wait_ge(s_y, tt * 2 + (i + 1))
                    for c in range(NH2):
                        g = i * NH2 + c
                        act.wait_ge(s_h, tt * (2 * NH2) + (2 * NH2 + g + 1))
                        for a in range(2):
                            last = nc.scalar.activation(hT[i][:, 2 * c + a, :], ph[g % 2][:, a * TILE:(a + 1) * TILE],
                                                        ACT.Relu, bias=b1s[i][:, 2 * c + a:2 * c + a + 1])
                        last.then_inc(s_ha, 1)
                    act.wait_ge(s_yo, tt * 2 + (2 + i + 1))
                    act.dma_start(ys[bass.ds(tt * 2 + i, 1)].rearrange("a (n p) c -> p (a n) c", p=P),
                                  yo[i][:]).then_inc(s_ys[i], 16)

        @block.vector
        def _(dve):
            v = nc.vector
            steps = [0]

            def step(ins):
                steps[0] += 1
                ins.then_inc(s_step, 1)
                dve.wait_ge(s_step, steps[0])

            v.memset(ones[:], 1.0).then_inc(s_one, 1)
            dve.wait_ge(s_c, 48)
            step(v.tensor_scalar(mt[:], iota[:, 0:MAXT], float(TILE), None, ALU.mult))
            dve.wait_ge(s_cnt, 1)
            J = B * NT
            v.tensor_copy(within[:], pr[:, 0, 0:J * E].rearrange("p (n e) -> p n e", n=J))
            step(v.tensor_copy(cnt[:], pr[:, 1, 0:J * E].rearrange("p (n e) -> p n e", n=J)))
            src, k, n = cnt, 1, 0
            while k < J:
                dst = cum[n % 2]
                v.tensor_copy(dst[:, 0:k, :], src[:, 0:k, :])
                step(v.tensor_tensor(dst[:, k:J, :], src[:, k:J, :], src[:, 0:J - k, :], ALU.add))
                src, k, n = dst, 2 * k, n + 1
            total, other = src, cum[n % 2]
            step(v.tensor_tensor(big[:], mt[:].unsqueeze(1).broadcast_to([P, E, MAXT]),
                                 total[:, J - 1, :].unsqueeze(2).broadcast_to([P, E, MAXT]), ALU.is_lt))
            step(v.reduce_sum(tiles[:], big[:], AX.X))
            step(v.memset(st[0][:, 0:1], 0.0))
            step(v.tensor_copy(st[0][:, 1:E], tiles[:, 0:E - 1]))
            src, k, n = st[0], 1, 1
            while k < E:
                dst = st[n % 2]
                v.tensor_copy(dst[:, 0:k], src[:, 0:k])
                step(v.tensor_tensor(dst[:, k:E], src[:, k:E], src[:, 0:E - k], ALU.add))
                src, k, n = dst, 2 * k, n + 1
            first, firstrow = src, st[n % 2]
            step(v.tensor_scalar(firstrow[:], first[:], float(TILE), None, ALU.mult))
            step(v.tensor_tensor(other[:], total[:], cnt[:], ALU.subtract))
            step(v.tensor_tensor(other[:], other[:], within[:], ALU.add))
            step(v.tensor_tensor(other[:], other[:], firstrow[:].unsqueeze(1).broadcast_to([P, J, E]), ALU.add))
            step(v.tensor_tensor(other[:], other[:], onehot[:], ALU.mult))
            step(v.reduce_sum(slotf[:], other[:], AX.X))
            v.tensor_copy(slot[:], slotf[:]).then_inc(s_route, 1)
            step(v.tensor_tensor(eidc[:], iota[:, 0:NTILE].unsqueeze(2).broadcast_to([P, NTILE, E]),
                                 first[:].unsqueeze(1).broadcast_to([P, NTILE, E]), ALU.is_ge))
            step(v.reduce_sum(eidf[:], eidc[:], AX.X))
            v.tensor_scalar(eid[:], eidf[:], 1.0, None, ALU.subtract).then_inc(s_route, 1)

            dve.sem_inc(s_yo, 2)
            with dve.Fori(0, NTILE // 2) as tt:
                for i in range(2):
                    dve.wait_ge(s_y, tt * 2 + (2 + i + 1))
                    dve.wait_ge(s_ys[i], tt * 16 + 16)
                    v.tensor_tensor(yo[i][:], py[i][:].rearrange("p (n c) -> p n c", n=TH),
                                    b2s[i][:].unsqueeze(1).broadcast_to([P, TH, C]), ALU.add).then_inc(s_yo, 1)

            for n in range(B):
                i = n % 2
                dve.wait_ge(s_g[i], (n // 2 + 1) * NT * 16)
                if n >= 2:
                    dve.wait_ge(s_out[i], (n // 2) * 16)
                v.tensor_tensor(res[i][:], rows[i][:], x2s[:, n * NT:(n + 1) * NT, :], ALU.add).then_inc(s_r, 1)
                dve.wait_ge(s_r, n + 1)
                layer_norm_steps(v, step, res[i], res[i], stats, mv, nwt, nwi, s_ln)
                dve.wait_ge(s_ln, n + 1)


_ORDER = ("x xT ctxT wqkT wv_l rf w_out b_out wk bk wq bq wv bv wck bck wcq bcq wcv bcv wp bp "
          "gate_wT gate_b w1T b1p w2T b2 ident mask_qk mask_kq sel tri iota").split()


def kernel(**inputs):
    from concourse import bacc as _bacc
    from concourse.bass_utils import run_bass_kernel_spmd as _run

    d = {k: np.asarray(v) for k, v in inputs.items()}
    c = np.ascontiguousarray
    w_qkv = d["L0_attn_W_qkv"]
    a = {
        "x": d["x"], "xT": c(d["x"].transpose(0, 2, 1)), "ctxT": c(d["ctx_512"].transpose(0, 2, 1)),
        "wqkT": c(w_qkv[:, :2 * LR].T), "wv_l": c(w_qkv[:, 2 * LR:]), "rf": d["L0_attn_RF"],
        "w_out": d["L0_attn_W_out"], "b_out": d["L0_attn_b_out"],
        "gate_wT": c(d["L0_ffn_gate_w"].T), "gate_b": d["L0_ffn_gate_b"],
        "w1T": c(d["L0_ffn_w1"].transpose(0, 2, 1)),
        "b1p": c(d["L0_ffn_b1"].reshape(E, NHC, P).transpose(0, 2, 1)),
        "w2T": c(d["L0_ffn_w2"].transpose(0, 2, 1)), "b2": d["L0_ffn_b2"],
    }
    for n in ("k", "q", "v", "ck", "cq", "cv", "p"):
        a["w" + n], a["b" + n] = d["L0_xattn_W" + n], d["L0_xattn_b" + n]
    at = np.arange(P)
    a["ident"] = np.eye(P, dtype=np.float32)
    a["mask_qk"] = np.where(at[None, :] <= at[:, None], 0, NEG).astype(np.float32)
    a["mask_kq"] = np.where(at[:, None] <= at[None, :], 0, NEG).astype(np.float32)
    head = np.arange(2 * LH) % LH
    a["sel"] = np.zeros((2 * LH, NPAIR, P), np.float32)
    for r in range(2 * LH):
        a["sel"][r, head[r] // 2, head[r] % 2 * LD:(head[r] % 2 + 1) * LD] = 1
    a["tri"] = (at[:, None] < at[None, :]).astype(np.float32)
    a["iota"] = np.ascontiguousarray(np.broadcast_to(np.arange(B * NT, dtype=np.float32), (P, B * NT)))

    nc = _bacc.Bacc("TRN2", target_bir_lowering=False, num_devices=1)
    arrays, args = {}, []
    for name in _ORDER:
        arrays[f"in_{name}"] = c(a[name])
        args.append(nc.dram_tensor(f"in_{name}", a[name].shape, mybir.dt.from_np(a[name].dtype), kind="ExternalInput").ap())
    args.append(nc.dram_tensor("out_0", (B, T, C), F32, kind="ExternalOutput").ap())
    decoder(nc, *args)
    r = _run(nc, [arrays], core_ids=[0])
    return r.results[0]["out_0"]
```

```python
import numpy as np
import concourse.bass as bass
from concourse import mybir
from contextlib import ExitStack

F32 = mybir.dt.float32
F32R = mybir.dt.float32r
BF16 = mybir.dt.bfloat16
I32 = mybir.dt.int32
U32 = mybir.dt.uint32
ALU = mybir.AluOpType
ACT = mybir.ActivationFunctionType
AX = mybir.AxisListType

P = 128
B, T, C = 8, 512, 256
NT = T // P
KC = C // P
LH, LD = 16, 64
LR = LH * LD
NPAIR = LH // 2
XH, XD = 16, 16
TC_, CC = 1024, 128
NTC = TC_ // P
E, HID = 8, 1024
NHC = HID // P
LN_EPS = 1e-5
STAB = 1e-6
SCALE = float(1.0 / np.sqrt(XD))
NEG = -1e30
KROW = 4 * XD
MROW = KROW
VW = 2 * XD + 1
RW = XD + 1

JOBS = [("kf0", "D"), ("kf1", "D"), ("kf2", "D"), ("kf3", "D"), ("g0", "A"), ("ksum", "D"), ("g1", "D"),
        ("norm", "D"), ("kv", "A"), ("kc0", "B"), ("m0", "A"), ("m1", "A"), ("bc0", "D"), ("bc1", "D"),
        ("bc2", "D"), ("bc3", "D"), ("attn0", "D"), ("attn1", "D"), ("vc0", "D"), ("vc1", "D"), ("kc1", "B"),
        ("x1T", "A"), ("k", "B"), ("q", "B"), ("qc", "B"), ("v", "D"),
        ("yT", "A"), ("proj0", "D"), ("proj1", "D"),
        ("qf0", "A"), ("qf1", "A"), ("qf2", "A"), ("qf3", "A"),
        ("x2T", "A"), ("gate", "D")]
NQF = 4
NJ = len(JOBS)
JN = {name: n for n, (name, _) in enumerate(JOBS)}
ACT_AT = {name: sum(w in "AB" for _, w in JOBS[:n + 1]) for n, (name, w) in enumerate(JOBS)}
DVE_AT = {name: sum(w in "DB" for _, w in JOBS[:n + 1]) for n, (name, w) in enumerate(JOBS)}
N_ACT, N_DVE = ACT_AT["gate"], DVE_AT["gate"]
STAGED = ["kc0", "kc1", "k", "q", "qc"]
STORES = {"kc0": 1, "kc1": 1, "k": 2, "q": 2, "qc": 2}

NSX = 2 * NT
NSB = NSX + 3
SELF_MAX = [[(3, 0)], [(2, 0), (0, 384)], [(1, 0)]]
NE_ = 2 + NTC // 2
SELF_EXP = [[(0, 0), (1, 512), (3, 896)], [(2, 0)]]
E_COLS = [1024, 256] + [1024] * (NE_ - 2)
S_PLAN = [2, 2, 2, 2, 2, 2]
AHEAD = 2
ROUND_BY = ["A", "D", "D", "A", "D", "A"]
POOL_COLS = [512, 0, 512, 512, 512, 512]
REST_POS = 2
TURN_AT = 5
HS = 4
HG = 2
HP = P // HG
RING_E = 4
U_AT = [0, 1, 3]
LAG = 3


def heads_order():
    ahead = []
    for h in range(XH + 1):
        banks = [("bank", h, n) for n in range(NSB)] if h < XH else []
        ahead += banks[:2] + [("maxima", h - 1, 0)] * (h > 0) + banks[2:]
    first = ahead.index(("maxima", 0, 0)) + 1 + AHEAD
    order, ahead = ahead[:first], ahead[first:]
    steps = XH * NE_
    for g in range(steps + LAG):
        h, n = divmod(g, NE_)
        if n == LAG and h:
            order.append(("keep", h - 1, 0))
        extra = []
        if g < steps:
            assert n or ("maxima", h, 0) in order
            order.append(("scores", h, n))
            if ROUND_BY[n] == "A":
                order.append(("round", h, n))
            extra, ahead = ahead[:S_PLAN[n]], ahead[S_PLAN[n]:]
        if 1 <= g <= steps:
            former = divmod(g - 1, NE_)
            extra[REST_POS:REST_POS] = [("rest", *former)]
            if ROUND_BY[former[1]] == "D":
                extra[0:0] = [("round", *former)]
        order += extra
        if n == TURN_AT and h and h % HG == 0:
            order.append(("turn", h // HG - 1, 0))
        if g >= LAG:
            order.append(("weigh", *divmod(g - LAG, NE_)))
    assert not ahead
    return order + [("keep", XH - 1, 0), ("turn", XH // HG - 1, 0)]


ORDER = heads_order()
RING = [e for e in ORDER if e[0] in ("bank", "maxima", "turn")]
RING_AT = {e: n for n, e in enumerate(RING)}
NRING, NRED = len(RING), sum(e[0] != "maxima" for e in RING)
RED_AT = {e: sum(f[0] != "maxima" for f in RING[:n + 1]) for n, e in enumerate(RING)}
ROUND_AT = {w: {(h, n): sum(ROUND_BY[m % NE_] == w for m in range(h * NE_ + n + 1))
                for h in range(XH) for n in range(NE_)} for w in "AD"}
N_ROUND = {w: ROUND_BY.count(w) * XH for w in "AD"}
POOL_AT = {(h, n): sum(POOL_COLS[m % NE_] > 0 for m in range(h * NE_ + n + 1)) for h in range(XH) for n in range(NE_)}
N_POOL = sum(c > 0 for c in POOL_COLS) * XH
WCOLS = 2 * 512

TILE = 256
TH = TILE // P
NTILE = -(-(B * T + E * (TILE - 1)) // TILE) // 2 * 2
MAXT = B * T // TILE
assert NTILE * TILE >= B * T + E * (TILE - 1) - (TILE - 1)


def decoder(nc, x, xT, ctxT, wqkT, wv_l, rf, w_out, b_out, wk, bk, wq, bq, wv, bv, wck, bck, wcq, bcq,
            wcv, bcv, wp, bp, gate_wT, gate_b, w1T, b1p, w2T, b2, ident_d, mask_qk, mask_kq, sel_d, fold_d,
            tri_d, iota_d, out, nb=B):
    x2d = nc.dram_tensor("x2d", [B * T, C], F32, kind="Internal").ap()
    xs = nc.dram_tensor("xs", [NTILE, TILE, C], F32, kind="Internal").ap()
    ys = nc.dram_tensor("ys", [NTILE, TILE, C], F32, kind="Internal").ap()
    with nc.sbuf_tensor("onehot", [P, B * NT, E], F32) as onehot:
        attentions(nc, x, xT, ctxT, wqkT, wv_l, rf, w_out, b_out, wk, bk, wq, bq, wv, bv, wck, bck,
                   wcq, bcq, wcv, bcv, wp, bp, gate_wT, gate_b, ident_d, mask_qk, mask_kq, sel_d, fold_d,
                   onehot, x2d.rearrange("(b t) c -> b t c", b=B), xs, nb)
        experts(nc, onehot, x2d, xs, ys, w1T, b1p, w2T, b2, ident_d, tri_d, iota_d, out)


def attentions(nc, x, xT, ctxT, wqkT, wv_l, rf, w_out, b_out, wk, bk, wq, bq, wv, bv, wck, bck,
               wcq, bcq, wcv, bcv, wp, bp, gate_wT, gate_b, ident_d, mask_qk, mask_kq, sel_d, fold_d,
               onehot, x2d, xs, nb):
    scr_k = nc.dram_tensor("scr_k", [2, C, T + TC_], F32, kind="Internal").ap()
    scr_q = nc.dram_tensor("scr_q", [2, C, 2 * T], F32, kind="Internal").ap()

    ctx = ExitStack()
    with ctx:
        def sb(name, shape, dt=F32):
            return ctx.enter_context(nc.sbuf_tensor(name, shape, dt))

        def sem(name):
            return ctx.enter_context(nc.semaphore(name))

        ident = sb("ident", [P, P])
        identb = sb("identb", [P, P], BF16)
        mqk = sb("mqk", [P, P], BF16)
        mkq = sb("mkq", [P, P], BF16)
        sel = sb("sel", [3 * LH, NPAIR, P], F32R)
        onescol = sb("onescol", [P, 1])
        fold = sb("fold", [P, P])
        wqf = sb("wqf", [P, KC, LR])
        wkf = sb("wkf", [P, KC, LR])
        wvl = sb("wvl", [P, KC, LR])
        wo = sb("wo", [P, NPAIR, C])
        wq_s = sb("wq_s", [P, KC, C])
        wk_s = sb("wk_s", [P, KC, C])
        wcq_s = sb("wcq_s", [P, KC, C])
        wv_s = sb("wv_s", [P, KC, C])
        wp_s = sb("wp_s", [P, KC, C])
        wck_s = sb("wck_s", [P, C])
        wcv_s = sb("wcv_s", [P, C])
        gw_s = sb("gw_s", [P, KC, E])
        bias_c = sb("bias_c", [P, 4, KC])
        bo_bc = sb("bo_bc", [P, C])
        bp_bc = sb("bp_bc", [P, C])
        bv_bc = sb("bv_bc", [P, C])
        bcv_bc = sb("bcv_bc", [P, C])
        gb_bc = sb("gb_bc", [P, E])
        ones_s = sb("ones_s", [P, NTC * XH])
        rank8 = sb("rank8", [P, E])
        x_s = sb("x_s", [P, NT, C])
        xT_s = sb("xT_s", [P, KC, T])
        ctxT_s = sb("ctxT_s", [P, TC_])
        with nc.sbuf_tensor("big_a", [P, NPAIR * T], F32) as big_a, \
                nc.sbuf_tensor("big_b", [P, NT * LR], F32) as big_b, \
                nc.sbuf_tensor("big_c", [P, NTC * XH * VW], F32) as big_c:
            pass
        low = sb("low", [P, RING_E, WCOLS], F32R)
        high = sb("high", [P, RING_E, WCOLS], F32R)
        vca = sb("vca", [P, NTC, XH, VW], F32R)
        phiq = big_a[:].rearrange("p (j t) -> p j t", j=NPAIR)
        phik = big_b[:].rearrange("p (i r) -> p i r", i=NT)
        rfbd = big_a[:, 0:NPAIR * P].rearrange("p (j r) -> p j r", j=NPAIR)
        wqkT_s = big_b[:].rearrange("p (j c) -> p j c", j=2 * NPAIR)
        u_s = big_a[:].rearrange("p (n a h d) -> p n a h d", n=4, a=4, h=XH)
        exps = big_a[:].rearrange("p (n c) -> p n c", n=RING_E)
        stage = high[:].rearrange("p (n w) c -> p n w c", n=2)
        g_s = big_c[:, 0:KC * LR].rearrange("p (k r) -> p k r", k=KC)
        m_s = big_c[:, KC * LR:KC * LR + NPAIR * C].rearrange("p (j c) -> p j c", j=NPAIR)
        sel_f = big_c[0:3 * LH, 0:NPAIR * P].rearrange("p (j r) -> p j r", j=NPAIR)
        kvbd = sb("kvbd", [P, NPAIR, P])
        ksbd = sb("ksbd", [P, NPAIR * LH])
        den = sb("den", [LH, T])
        rT = sb("rT", [3 * LH, T], F32R)
        xb = sb("xb", [P, NT, C])
        r_s = sb("r_s", [P, NT, C])
        cstage = r_s[:, 0, :]
        stats = sb("stats", [P, NT, 6])
        mv = sb("mv", [P, 4, NT])
        zero1 = sb("zero1", [P, 1])
        nwt = sb("nwt", [P, 5, NT])
        nwi = sb("nwi", [P, 2, NT], I32)
        x1 = sb("x1", [P, NT, C])
        x1T = sb("x1T", [P, KC, T])
        va = sb("va", [P, NT, XH, VW], F32R)
        hk = [sb(f"hk{i}", [P, T + TC_], F32R) for i in range(HS)]
        hq = [sb(f"hq{i}", [P, 2 * T], F32R) for i in range(HS)]
        mpad = sb("mpad", [P, NT, P])
        cmax = sb("cmax", [P, NT, 2])
        ykeep = sb("ykeep", [P, 2, T])
        rec = sb("rec", [P, 2 * NT, HG])
        yn = sb("yn", [P, 2 * NT, HG, XD])
        y_s = sb("y_s", [P, NT, C])
        psum01 = y_s[:].rearrange("p i c -> p (i c)")
        psum23 = r_s[:].rearrange("p i c -> p (i c)")
        yT_s = g_s[:, :, 0:T]
        lg = sb("lg", [P, NT, E])
        lmax = sb("lmax", [P, NT])
        lw = sb("lw", [P, NT, E])

        ps = [ctx.enter_context(nc.psum_tensor(f"ps{i}", [P, WCOLS], F32)) for i in range(4)]

        s_const = sem("s_const")
        s_rf = sem("s_rf")
        s_sel = sem("s_sel")
        s_setup = sem("s_setup")
        s_wprod = sem("s_wprod")
        s_x = sem("s_x")
        s_tile = sem("s_tile")
        s_act = sem("s_act")
        s_dve = sem("s_dve")
        s_dstep = sem("s_dstep")
        s_xb = sem("s_xb")
        s_ln = sem("s_ln")
        s_st = {n: sem(f"s_st_{n}") for n in STAGED}
        s_hl = [sem(f"s_hl{i}") for i in range(HS)]
        s_zero = sem("s_zero")
        s_sc = sem("s_sc")
        s_red = sem("s_red")
        s_max = sem("s_max")
        s_mrow = sem("s_mrow")
        s_st2 = sem("s_st2")
        s_exp = sem("s_exp")
        s_av = sem("s_av")
        s_rnd = {"A": sem("s_rnd_a"), "D": sem("s_rnd_d")}
        s_rest_d = sem("s_rest_d")
        s_rest_p = sem("s_rest_p")
        s_psum = sem("s_psum")
        s_vh = sem("s_vh")
        s_vl = sem("s_vl")
        s_vone = sem("s_vone")
        s_keep = sem("s_keep")
        s_ys = sem("s_ys")
        s_pace = sem("s_pace")
        s_zx = sem("s_zx")
        s_x2 = sem("s_x2")

        def cur(b, per, k):
            return b * per + (per + k)

        block = ctx.enter_context(nc.Block())
        LOADS = 24
        xs_flat = xs.rearrange("t r c -> (t r c)").rearrange("(p n) -> p n", p=P)
        NZ = xs_flat.shape[1] // (NPAIR * P)

        @block.sync
        def _(sp):
            def const(dst, src):
                sp.dma_start(dst, src).then_inc(s_const, 16)

            sp.sem_inc(s_x2, 16)
            for n in STAGED:
                sp.sem_inc(s_st[n], 16 * STORES[n])
            const(wqkT_s, wqkT.rearrange("(j p) c -> p j c", p=P))
            const(ident[:], ident_d)
            const(fold[:], fold_d)
            const(cstage[:, 0:P], mask_qk)
            const(cstage[:, P:2 * P], mask_kq)
            const(wvl[:], wv_l.rearrange("(k p) r -> p k r", p=P))
            const(wo[:], w_out.rearrange("(j p) c -> p j c", p=P))
            for dst, src in ((wq_s, wq), (wk_s, wk), (wcq_s, wcq), (wv_s, wv), (wp_s, wp)):
                const(dst[:], src.rearrange("(k p) c -> p k c", p=P))
            const(wck_s[:], wck)
            const(wcv_s[:], wcv)
            const(gw_s[:], gate_wT.rearrange("(k p) e -> p k e", p=P))
            for n, src in enumerate((bk, bck, bq, bcq)):
                sp.dma_start(bias_c[:, n, :], src.rearrange("(k p) -> p k", p=P),
                             allow_slow_non_contiguous=True).then_inc(s_const, 16)
            for dst, src in ((bo_bc, b_out), (bp_bc, bp), (bv_bc, bv), (bcv_bc, bcv), (gb_bc, gate_b)):
                const(dst[:], src.rearrange("(a c) -> a c", a=1).broadcast_to([P, dst.shape[1]]))
            sp.dma_start(sel_f, sel_d).then_inc(s_sel, 16)
            sp.wait_ge(s_setup, 1)
            rf_v = rf.rearrange("(j a) d r -> a d j r", a=2)
            sp.dma_start(rfbd[0:LD, :, 0:LD], rf_v[0]).then_inc(s_rf, 16)
            sp.dma_start(rfbd[LD:P, :, LD:P], rf_v[1]).then_inc(s_rf, 16)

            def load_x(b):
                sp.dma_start(x_s[:], x[b].rearrange("(i p) c -> p i c", p=P)).then_inc(s_x, 16)
                sp.dma_start(xT_s[:], xT[b].rearrange("(k p) t -> p k t", p=P)).then_inc(s_x, 16)
                sp.dma_start(ctxT_s[:], ctxT[b]).then_inc(s_x, 16)

            load_x(0)
            for n in range(NZ):
                sp.dma_start(xs_flat[:, n * NPAIR * P:(n + 1) * NPAIR * P],
                             kvbd[:].rearrange("p j r -> p (j r)")).then_inc(s_zx, 16)

            def store(name, stg, scr, cols, m0, nm, b):
                sp.wait_ge(s_dve, cur(b, N_DVE, DVE_AT[name]))
                w = (cols.stop - cols.start)
                for m in range(nm):
                    src = stage[:, stg, :, m * w:(m + 1) * w].bitcast(F32)
                    dst = scr[:, (m0 + m) * P:(m0 + m + 1) * P, cols].rearrange("w r t -> r w t")
                    sp.dma_start(dst, src).then_inc(s_st[name], 16)

            def load_head(b, h):
                i = h % HS
                sp.wait_ge(s_zero, cur(b, XH, h - HS + 1))
                sp.sem_inc(s_pace, 1)
                sp.wait_ge(s_st2, cur(b, XH * NE_, (h - HS + 1) * NE_))
                sp.sem_inc(s_pace, 1)
                for w in range(2):
                    sp.dma_start(hk[i][32 * w:32 * w + 32, :].bitcast(F32),
                                 scr_k[:, h * XD:(h + 1) * XD, :]).then_inc(s_hl[i], 16)
                    for d in range(2):
                        sp.dma_start(hq[i][32 * w + 16 * d:32 * w + 16 * d + 16, :].bitcast(F32),
                                     scr_q[w, h * XD:(h + 1) * XD, :]).then_inc(s_hl[i], 16)

            with sp.Fori(0, nb) as b:
                store("kc0", 0, scr_k, slice(T, T + TC_), 0, 1, b)
                store("kc1", 1, scr_k, slice(T, T + TC_), 1, 1, b)
                store("k", 0, scr_k, slice(0, T), 0, 2, b)
                store("q", 1, scr_q, slice(0, T), 0, 2, b)
                store("qc", 0, scr_q, slice(T, 2 * T), 0, 2, b)
                following = sp.snap((b + 1) % nb)
                for n in STAGED:
                    sp.wait_ge(s_st[n], cur(b, 16 * STORES[n], 16 * STORES[n]))
                    sp.sem_inc(s_pace, 1)
                for h in range(XH):
                    load_head(b, h)
                    if h == 3:
                        sp.wait_ge(s_xb, cur(b, 2, 1))
                        sp.sem_inc(s_pace, 1)
                        sp.wait_ge(s_tile, cur(b, NJ, JN["v"] + 1))
                        sp.sem_inc(s_pace, 1)
                        load_x(following)
                sp.wait_ge(s_ln, cur(b, 2, 2))
                sp.sem_inc(s_pace, 1)
                sp.dma_start(x2d[b].rearrange("(i p) c -> p i c", p=P), x1[:]).then_inc(s_x2, 16)
            sp.wait_ge(s_x2, (nb + 1) * 16)
            sp.wait_ge(s_x, (nb + 1) * 48)

        @block.gpsimd
        def _(pool):
            pool.sem_inc(s_xb, 2)
            pool.sem_inc(s_zero, XH)
            pool.sem_inc(s_psum, 3)
            pool.sem_inc(s_vl, 3)
            pool.sem_inc(s_rest_p, N_POOL)
            pool.wait_ge(s_const, 16 * LOADS)
            pool.wait_ge(s_setup, 2)
            with pool.Fori(0, nb) as b:
                pool.wait_ge(s_x, (b + 1) * 48)
                pool.wait_ge(s_dve, cur(b, N_DVE, DVE_AT["proj1"] - N_DVE))
                for i in range(NT):
                    last = nc.gpsimd.tensor_tensor(xb[:, i, :], x_s[:, i, :], bo_bc[:], ALU.add)
                last.then_inc(s_xb, 1)
                pool.wait_ge(s_dve, cur(b, N_DVE, DVE_AT["kf1"]))
                nc.gpsimd.tensor_tensor(psum01, phik[:, 0, :], phik[:, 1, :], ALU.add).then_inc(s_psum, 1)
                pool.wait_ge(s_dve, cur(b, N_DVE, DVE_AT["kf3"]))
                nc.gpsimd.tensor_tensor(psum23, phik[:, 2, :], phik[:, 3, :], ALU.add).then_inc(s_psum, 1)
                pool.wait_ge(s_psum, cur(b, 3, 2))
                nc.gpsimd.tensor_tensor(psum01, psum01, psum23, ALU.add).then_inc(s_psum, 1)

                def low_values(n, dst):
                    pool.wait_ge(s_vh, cur(b, 3, n + 1))
                    nc.gpsimd.tensor_tensor(dst[:, :, :, RW:VW], u_s[:, U_AT[n]], dst[:, :, :, 0:XD].bitcast(F32),
                                            ALU.subtract).then_inc(s_vl, 1)

                for k in range(2):
                    low_values(k, vca[:, 4 * k:4 * k + 4])
                pool.wait_ge(s_ln, cur(b, 2, 1))
                for i in range(NT):
                    last = nc.gpsimd.tensor_tensor(xb[:, i, :], x1[:, i, :], bp_bc[:], ALU.add)
                last.then_inc(s_xb, 1)
                low_values(2, va)
                for kind, h, n in ORDER:
                    if kind != "rest":
                        continue
                    w = POOL_COLS[n]
                    if w:
                        who = ROUND_BY[n]
                        pool.wait_ge(s_rnd[who], cur(b, N_ROUND[who], ROUND_AT[who][h, n]))
                        slot = (h * NE_ + n) % RING_E
                        nc.gpsimd.tensor_tensor(low[:, slot, 0:w], exps[:, slot, 0:w], high[:, slot, 0:w].bitcast(F32),
                                                ALU.subtract).then_inc(s_rest_p, 1)
                    if n == NE_ - 1:
                        pool.wait_ge(s_st2, cur(b, XH * NE_, (h + 1) * NE_))
                        pool.wait_ge(s_rest_p, cur(b, N_POOL, POOL_AT[h, n]))
                        z = zero1[MROW:MROW + 1, :].broadcast_to([1, 2 * T])
                        nc.gpsimd.tensor_tensor(hq[h % HS][MROW:MROW + 1, :], z, z, ALU.add).then_inc(s_zero, 1)
                        pool.wait_ge(s_zero, cur(b, XH, h + 1))

        @block.tensor
        def _(pe):
            mm, tr = nc.tensor.matmul, nc.tensor.transpose
            pe.sem_inc(s_tile, JN["qf0"])
            pe.sem_inc(s_sc, NRING)
            pe.sem_inc(s_st2, XH * NE_)
            pe.sem_inc(s_av, XH * NE_)

            pe.wait_ge(s_const, 16 * LOADS)
            pe.wait_ge(s_rf, 32)
            for n in range(4):
                q, c = n // 2, n % 2
                for j in range(NPAIR):
                    last = mm(ps[n][:, j * P:(j + 1) * P], wqkT_s[:, q * NPAIR + j, c * P:(c + 1) * P],
                              rfbd[:, j, :], start=True, stop=True)
                last.then_inc(s_wprod, 1)

            def job(b, name, fill, act=None, dve=None):
                n = JN[name]
                prev = n - 4 if n >= 4 else max(m for m in range(NJ) if m % 4 == n % 4)
                back = n < 4
                former, who = JOBS[prev]
                a = [ACT_AT[former] - back * N_ACT] if who == "A" else []
                d = [DVE_AT[former] - back * N_DVE] if who != "A" else []
                a += [ACT_AT[act]] if act else []
                d += [DVE_AT[dve]] if dve else []
                if a:
                    pe.wait_ge(s_act, cur(b, N_ACT, max(a)))
                if d:
                    pe.wait_ge(s_dve, cur(b, N_DVE, max(d)))
                fill(ps[n % 4]).then_inc(s_tile, 1)

            def ring_bank(b, entry):
                n = RING_AT[entry]
                if n >= 2:
                    kind, h, _ = former = RING[n - 2]
                    if kind == "maxima":
                        pe.wait_ge(s_mrow, cur(b, XH, h + 1))
                    else:
                        pe.wait_ge(s_red, cur(b, NRED, RED_AT[former]))
                return ps[2][:, (n % 2) * 512:(n % 2) * 512 + 512]

            def score_bank(b, h, n):
                if n == 0:
                    pe.wait_ge(s_hl[h % HS], (b * (XH // HS) + (h // HS + 1)) * (6 * 16))
                    pe.wait_ge(s_zero, cur(b, XH, h - HS + 1))
                pb = ring_bank(b, ("bank", h, n))
                hk_, hq_ = hk[h % HS], hq[h % HS]
                if n >= NSX:
                    for i, col in SELF_MAX[n - NSX]:
                        w = (i + 1) * P
                        mm(pb[:, col:col + w], hq_[:, i * P:(i + 1) * P], hk_[:, 0:w], start=True, stop=False)
                        last = mm(pb[:, col + w - P:col + w], identb[:], mqk[:], start=False, stop=True)
                else:
                    i, half = n // 2, n % 2
                    last = mm(pb, hq_[:, T + i * P:T + (i + 1) * P],
                              hk_[:, T + half * 512:T + (half + 1) * 512], start=True, stop=True)
                last.then_inc(s_sc, 1)

            def maxima_row(b, h):
                pb = ring_bank(b, ("maxima", h, 0))
                pe.wait_ge(s_max, cur(b, XH, h + 1))
                pe.wait_ge(s_red, cur(b, NRED, RED_AT["bank", h, NSB - 1]))
                for i in range(NT):
                    last = tr(pb[:, i * P:(i + 1) * P], mpad[:, i, :], ident[:])
                last.then_inc(s_sc, 1)

            def exp_scores(b, h, n):
                g = h * NE_ + n
                pb = ps[g % 2]
                if n == 0:
                    pe.wait_ge(s_mrow, cur(b, XH, h + 1))
                pe.wait_ge(s_exp, cur(b, XH * NE_, g - 1))
                hk_, hq_ = hk[h % HS], hq[h % HS]
                if n < 2:
                    for j, col in SELF_EXP[n]:
                        mm(pb[:, col:col + T - j * P], hk_[:, j * P:(j + 1) * P], hq_[:, j * P:T],
                           start=True, stop=False)
                        last = mm(pb[:, col:col + P], identb[:], mkq[:], start=False, stop=True)
                else:
                    for a in range(2):
                        j = 2 * (n - 2) + a
                        last = mm(pb[:, a * 512:(a + 1) * 512], hk_[:, T + j * P:T + (j + 1) * P],
                                  hq_[:, T:2 * T], start=True, stop=True)
                last.then_inc(s_st2, 1)

            def weigh(b, h, n):
                g = h * NE_ + n
                if g == 0:
                    pe.wait_ge(s_vone, b + 1)
                    pe.wait_ge(s_vl, cur(b, 3, 3))
                if n == 0:
                    pe.wait_ge(s_keep, cur(b, XH, h))
                pe.wait_ge(s_rest_d, cur(b, XH * NE_, g + 1))
                if POOL_COLS[n]:
                    pe.wait_ge(s_rest_p, cur(b, N_POOL, POOL_AT[h, n]))
                for part, e in enumerate((high[:, g % RING_E, :], low[:, g % RING_E, :])):
                    if n < 2:
                        for j, col in SELF_EXP[n]:
                            last = mm(ps[3][0:VW, j * P:T], va[:, j, h, :], e[:, col:col + T - j * P],
                                      start=part == 0 and n == 0 and j == 0, stop=part == 1 and n == 1)
                    else:
                        for a in range(2):
                            j = 2 * (n - 2) + a
                            last = mm(ps[3][0:VW, 512:1024], vca[:, j, h, :], e[:, a * 512:(a + 1) * 512],
                                      start=part == 0 and j == 0, stop=part == 1 and j == NTC - 1)
                last.then_inc(s_av, 1)

            def turn_results(b, g):
                pb = ring_bank(b, ("turn", g, 0))
                pe.wait_ge(s_keep, cur(b, XH, (g + 1) * HG))
                for w in range(2):
                    for i in range(NT):
                        col = (w * NT + i) * HG * RW
                        last = mm(pb[:, col:col + P], ykeep[:, w, i * P:(i + 1) * P], fold[:], start=True, stop=True)
                last.then_inc(s_sc, 1)

            def qfeat(i):
                def fill(t):
                    for a in range(2):
                        j = 2 * i + a
                        for c in range(KC):
                            last = mm(t[:, a * T:(a + 1) * T], wqf[:, c, j * P:(j + 1) * P],
                                      xT_s[:, c, :], start=c == 0, stop=c == KC - 1)
                    return last
                return fill

            pe.wait_ge(s_x, 48)
            pe.wait_ge(s_setup, 2)
            for i in range(NQF):
                qfeat(i)(ps[JN[f"qf{i}"] % 4]).then_inc(s_tile, 1)
            pe.wait_ge(s_tile, JN["qf3"] + 1)
            pe.sem_inc(s_tile, NJ - JN["qf3"] - 1)
            with pe.Fori(0, nb) as b:
                def kfeat(i):
                    def fill(t):
                        for half in range(2):
                            for c in range(KC):
                                last = mm(t[:, half * 512:(half + 1) * 512], xT_s[:, c, i * P:(i + 1) * P],
                                          wkf[:, c, half * 512:(half + 1) * 512], start=c == 0, stop=c == KC - 1)
                        return last
                    return fill

                for i in range(NT):
                    job(b, f"kf{i}", kfeat(i))

                def gprod(m):
                    def fill(t):
                        for half in range(2):
                            for i in range(NT):
                                last = mm(t[:, half * 512:(half + 1) * 512], x_s[:, i, m * P:(m + 1) * P],
                                          phik[:, i, half * 512:(half + 1) * 512], start=i == 0, stop=i == NT - 1)
                        return last
                    return fill

                job(b, "g0", gprod(0), dve="kf3")

                def fsum(t):
                    for j in range(NPAIR):
                        last = mm(t[:, j:j + 1], psum01[:, j * P:(j + 1) * P], onescol[:], start=True, stop=True)
                    return last

                pe.wait_ge(s_psum, cur(b, 3, 3))
                job(b, "ksum", fsum)
                job(b, "g1", gprod(1))

                def normprod(t):
                    for j in range(NPAIR):
                        last = mm(t[0:LH, 0:T], ksbd[:, j * LH:(j + 1) * LH], phiq[:, j, :],
                                  start=j == 0, stop=j == NPAIR - 1)
                    return last

                pe.wait_ge(s_act, cur(b, N_ACT, ACT_AT["qf3"] - N_ACT))
                job(b, "norm", normprod, dve="ksum")

                def kvprod(t):
                    for j in range(NPAIR):
                        for c in range(KC):
                            last = mm(t[:, j * P:(j + 1) * P], wvl[:, c, j * P:(j + 1) * P],
                                      g_s[:, c, j * P:(j + 1) * P], start=c == 0, stop=c == KC - 1)
                    return last

                job(b, "kv", kvprod, act="g0", dve="g1")

                def kcprod(m):
                    def fill(t):
                        for half in range(2):
                            last = mm(t[:, half * 512:(half + 1) * 512], wck_s[:, m * P:(m + 1) * P],
                                      ctxT_s[:, half * 512:(half + 1) * 512], start=True, stop=True)
                        return last
                    return fill

                job(b, "kc0", kcprod(0))

                def mprod(k):
                    def fill(t):
                        for a in range(4):
                            j = 4 * k + a
                            last = mm(t[:, a * C:(a + 1) * C], kvbd[:, j, :], wo[:, j, :], start=True, stop=True)
                        return last
                    return fill

                job(b, "m0", mprod(0), act="kv")
                job(b, "m1", mprod(1))

                def spread(k):
                    def fill(t):
                        for a in range(2):
                            last = mm(t[:, a * T:(a + 1) * T], sel[:, 2 * k + a, :], rT[:], start=True, stop=True)
                        return last
                    return fill

                for k in range(4):
                    job(b, f"bc{k}", spread(k), dve="norm")

                def attn(half):
                    def fill(t):
                        for a in range(2):
                            i = 2 * half + a
                            for j in range(NPAIR):
                                last = mm(t[:, a * C:(a + 1) * C], phiq[:, j, i * P:(i + 1) * P], m_s[:, j, :],
                                          start=j == 0, stop=j == NPAIR - 1)
                        return last
                    return fill

                job(b, "attn0", attn(0), act="m1", dve="bc3")
                job(b, "attn1", attn(1))

                def vcprod(k):
                    def fill(t):
                        for a in range(4):
                            last = mm(t[:, a * C:(a + 1) * C], ctxT_s[:, (4 * k + a) * P:(4 * k + a + 1) * P],
                                      wcv_s[:], start=True, stop=True)
                        return last
                    return fill

                job(b, "vc0", vcprod(0))
                job(b, "vc1", vcprod(1))
                job(b, "kc1", kcprod(1))

                def turn(src):
                    def fill(t):
                        for c in range(KC):
                            for i in range(NT):
                                last = tr(t[:, c * T + i * P:c * T + (i + 1) * P], src[:, i, c * P:(c + 1) * P], ident[:])
                        return last
                    return fill

                pe.wait_ge(s_ln, cur(b, 2, 1))
                job(b, "x1T", turn(x1))
                def proj(w):
                    def fill(t):
                        for m in range(2):
                            for c in range(KC):
                                last = mm(t[:, m * T:(m + 1) * T], w[:, c, m * P:(m + 1) * P], x1T[:, c, :],
                                          start=c == 0, stop=c == KC - 1)
                        return last
                    return fill

                def rows(src, w, tiles=range(NT)):
                    def fill(t):
                        for n, i in enumerate(tiles):
                            for c in range(KC):
                                last = mm(t[:, n * C:(n + 1) * C], src[:, c, i * P:(i + 1) * P], w[:, c, :],
                                          start=c == 0, stop=c == KC - 1)
                        return last
                    return fill

                job(b, "k", proj(wk_s), act="x1T")
                job(b, "q", proj(wq_s))
                job(b, "qc", proj(wcq_s))
                job(b, "v", rows(x1T, wv_s))

                pe.wait_ge(s_dve, cur(b, N_DVE, DVE_AT["v"]))

                for kind, h, n in ORDER:
                    if kind == "bank":
                        score_bank(b, h, n)
                    elif kind == "maxima":
                        maxima_row(b, h)
                    elif kind == "scores":
                        exp_scores(b, h, n)
                    elif kind == "weigh":
                        weigh(b, h, n)
                    elif kind == "turn":
                        turn_results(b, h)

                pe.wait_ge(s_ys, cur(b, XH // HG, XH // HG))
                job(b, "yT", turn(y_s))
                job(b, "proj0", rows(yT_s, wp_s, (0, 1)), act="yT")
                job(b, "proj1", rows(yT_s, wp_s, (2, 3)))
                pe.wait_ge(s_x, (b + 2) * 48)
                for i in range(NQF):
                    job(b, f"qf{i}", qfeat(i))
                pe.wait_ge(s_ln, cur(b, 2, 2))
                job(b, "x2T", turn(x1))
                def gate(t):
                    for i in range(NT):
                        for c in range(KC):
                            last = mm(t[:, i * E:(i + 1) * E], x1T[:, c, i * P:(i + 1) * P], gw_s[:, c, :],
                                      start=c == 0, stop=c == KC - 1)
                    return last

                job(b, "gate", gate, act="x2T")

        @block.scalar
        def _(act):
            act.sem_inc(s_act, ACT_AT["qf0"] - 1)
            act.sem_inc(s_mrow, XH)
            act.sem_inc(s_exp, XH * NE_)
            act.sem_inc(s_keep, XH)
            act.sem_inc(s_vh, 3)
            act.sem_inc(s_rnd["A"], N_ROUND["A"])

            def relu_q(i, t):
                nc.scalar.activation(phiq[:, 2 * i:2 * i + 2, :], t[:].rearrange("p (a t) -> p a t", a=2),
                                     ACT.Relu).then_inc(s_act, 1)

            for i in range(NQF):
                act.wait_ge(s_tile, JN[f"qf{i}"] + 1)
                relu_q(i, ps[JN[f"qf{i}"] % 4])
            act.wait_ge(s_act, ACT_AT["qf3"])
            act.sem_inc(s_act, N_ACT - ACT_AT["qf3"])
            with act.Fori(0, nb) as b:
                def full(name):
                    act.wait_ge(s_tile, cur(b, NJ, JN[name] + 1))
                    return ps[JN[name] % 4]

                t = full("g0")
                nc.scalar.activation(g_s[:, 0, :], t[:], ACT.Copy).then_inc(s_act, 1)
                t = full("kv")
                act.wait_ge(s_setup, 2)
                act.wait_ge(s_zx, 16 * NZ)
                tv = t[:].rearrange("p (j r) -> p j r", j=NPAIR)
                nc.scalar.activation(kvbd[0:LD, :, 0:LD], tv[0:LD, :, 0:LD], ACT.Copy)
                nc.scalar.activation(kvbd[LD:P, :, LD:P], tv[LD:P, :, LD:P], ACT.Copy).then_inc(s_act, 1)
                def high_part(name, stg, bias_n, whole_m=None):
                    t = full(name)
                    used = {"kc0": "qc", "kc1": "q", "k": "kc0", "q": "kc1", "qc": "k"}[name]
                    back = 1 if name in ("kc0", "kc1") else 0
                    act.wait_ge(s_st[used], cur(b, 16 * STORES[used], (1 - back) * 16 * STORES[used]))
                    if whole_m is not None:
                        last = nc.scalar.activation(stage[:, stg, 0, :], t[:], ACT.Identity,
                                                    bias=bias_c[:, bias_n, whole_m:whole_m + 1])
                    else:
                        for m in range(2):
                            last = nc.scalar.activation(stage[:, stg, 0, m * T:(m + 1) * T],
                                                        t[:, m * T:(m + 1) * T], ACT.Identity,
                                                        bias=bias_c[:, bias_n, m:m + 1])
                    last.then_inc(s_act, 1)

                high_part("kc0", 0, 1, 0)
                for k in range(2):
                    t = full(f"m{k}")
                    nc.scalar.activation(m_s[:, 4 * k:4 * k + 4, :], t[:].rearrange("p (a c) -> p a c", a=4),
                                         ACT.Copy).then_inc(s_act, 1)

                def high_values(n, name, dst):
                    act.wait_ge(s_dve, cur(b, N_DVE, DVE_AT[name]))
                    nc.scalar.activation(dst[:, :, :, 0:XD], u_s[:, U_AT[n]], ACT.Copy).then_inc(s_vh, 1)

                for k in range(2):
                    high_values(k, f"vc{k}", vca[:, 4 * k:4 * k + 4])
                nc.scalar.activation(vca[:, :, :, XD], ones_s[:].rearrange("p (n h) -> p n h", n=NTC),
                                     ACT.Copy).then_inc(s_vone, 1)
                high_part("kc1", 1, 1, 1)
                t = full("x1T")
                nc.scalar.activation(x1T[:], t[:].rearrange("p (c t) -> p c t", c=KC), ACT.Copy).then_inc(s_act, 1)
                high_part("k", 0, 0)
                high_part("q", 1, 2)
                high_part("qc", 0, 3)
                high_values(2, "v", va)

                def maxima(h):
                    n = RING_AT["maxima", h, 0]
                    act.wait_ge(s_sc, cur(b, NRING, n + 1))
                    pb = ps[2][:, (n % 2) * 512:(n % 2) * 512 + 512]
                    nc.scalar.activation(hq[h % HS][MROW:MROW + 1, 0:T], pb[64:65, :], ACT.Copy)
                    nc.scalar.activation(hq[h % HS][MROW:MROW + 1, T:2 * T], pb[96:97, :],
                                         ACT.Copy).then_inc(s_mrow, 1)

                def exp_step(h, n):
                    g, w = h * NE_ + n, E_COLS[n]
                    act.wait_ge(s_st2, cur(b, XH * NE_, g + 1))
                    act.wait_ge(s_av, cur(b, XH * NE_, g + 1 - RING_E))
                    if g in U_AT:
                        act.wait_ge(s_vl, cur(b, 3, U_AT.index(g) + 1))
                    nc.scalar.activation(exps[:, g % RING_E, 0:w], ps[g % 2][:, 0:w], ACT.Exp,
                                         scale=SCALE).then_inc(s_exp, 1)

                def round_exps(h, n):
                    g, w = h * NE_ + n, E_COLS[n]
                    act.wait_ge(s_exp, cur(b, XH * NE_, g + 1))
                    nc.scalar.activation(high[:, g % RING_E, 0:w], exps[:, g % RING_E, 0:w],
                                         ACT.Copy).then_inc(s_rnd["A"], 1)

                def keep(h):
                    act.wait_ge(s_av, cur(b, XH * NE_, (h + 1) * NE_))
                    if h >= HG:
                        n = RING_AT["turn", h // HG - 1, 0]
                        act.wait_ge(s_sc, cur(b, NRING, n + 1))
                    q = h % HG * HP
                    nc.scalar.activation(ykeep[q:q + VW, :, :], ps[3][0:VW, :].rearrange("p (w t) -> p w t", w=2),
                                         ACT.Copy).then_inc(s_keep, 1)

                for kind, h, n in ORDER:
                    if kind == "maxima":
                        maxima(h)
                    elif kind == "scores":
                        exp_step(h, n)
                    elif kind == "round" and ROUND_BY[n] == "A":
                        round_exps(h, n)
                    elif kind == "keep":
                        keep(h)
                t = full("yT")
                nc.scalar.activation(yT_s, t[:].rearrange("p (c t) -> p c t", c=KC), ACT.Copy).then_inc(s_act, 1)
                for i in range(NQF):
                    relu_q(i, full(f"qf{i}"))
                t = full("x2T")
                nc.scalar.activation(x1T[:], t[:].rearrange("p (c t) -> p c t", c=KC), ACT.Copy).then_inc(s_act, 1)

        @block.vector
        def _(dve):
            v = nc.vector
            steps = [0]
            NSTEP = 48

            dve.sem_inc(s_dve, N_DVE)
            dve.sem_inc(s_ln, 2)
            dve.sem_inc(s_red, NRED)
            dve.sem_inc(s_max, XH)
            dve.sem_inc(s_ys, XH // HG)
            dve.sem_inc(s_rest_d, XH * NE_)
            dve.sem_inc(s_rnd["D"], N_ROUND["D"])

            for t in (rfbd, kvbd[:]):
                v.memset(t, 0.0)
            v.memset(mpad[:], 0.0)
            v.memset(ksbd[:], 0.0)
            v.memset(onescol[:], 1.0)
            v.memset(zero1[:], 0.0)
            v.memset(onehot[:], 0.0)
            v.memset(ones_s[:], 1.0)
            v.memset(va[:].bitcast(F32), 1.0)
            v.memset(rT[:].bitcast(F32), 0.0)
            for e in range(E):
                v.memset(rank8[:, e:e + 1], float(E - e))
            for i in range(HS):
                v.memset(hk[i][MROW:P, :].bitcast(F32), 0.0)
                v.memset(hq[i][MROW:P, :].bitcast(F32), 0.0)
            v.memset(ykeep[:], 0.0).then_inc(s_setup, 1)
            dve.wait_ge(s_setup, 1)
            for i in range(HS):
                v.memset(hk[i][MROW:MROW + 1, :].bitcast(F32), -1.0)
            dve.wait_ge(s_const, 16 * LOADS)
            v.tensor_copy(identb[:], ident[:])
            v.tensor_copy(mqk[:], cstage[:, 0:P])
            v.tensor_copy(mkq[:], cstage[:, P:2 * P])
            dve.wait_ge(s_sel, 16)
            v.tensor_copy(sel[:], sel_f)
            for n, w in enumerate((wqf, wkf)):
                for c in range(KC):
                    dve.wait_ge(s_wprod, 2 * n + c + 1)
                    last = v.tensor_copy(w[:, c, :], ps[2 * n + c][:])
            last.then_inc(s_setup, 1)

            with dve.Fori(0, nb) as b:
                def step(ins):
                    steps[0] += 1
                    ins.then_inc(s_dstep, 1)
                    dve.wait_ge(s_dstep, b * NSTEP + steps[0])

                def full(name):
                    dve.wait_ge(s_tile, cur(b, NJ, JN[name] + 1))
                    return ps[JN[name] % 4]

                for n in ("q", "qc"):
                    dve.wait_ge(s_st[n], cur(b, 16 * STORES[n], 0))
                for i in range(NT):
                    t = full(f"kf{i}")
                    v.tensor_scalar(phik[:, i, :], t[:], 0.0, None, ALU.max).then_inc(s_dve, 1)
                t = full("ksum")
                W = LH + 2
                v.tensor_copy(ksbd[0:LD, 0:7 * W + 1:W], t[0:LD, 0:NPAIR])
                v.tensor_copy(ksbd[LD:P, 1:7 * W + 2:W], t[LD:P, 0:NPAIR]).then_inc(s_dve, 1)
                t = full("g1")
                v.tensor_copy(g_s[:, 1, :], t[:]).then_inc(s_dve, 1)
                t = full("norm")
                step(v.tensor_scalar(den[:], t[0:LH, 0:T], STAB, None, ALU.add))
                step(v.reciprocal(den[:], den[:]))
                step(v.tensor_copy(rT[0:LH, :], den[:]))
                v.tensor_tensor(rT[2 * LH:3 * LH, :], den[:], rT[0:LH, :].bitcast(F32), ALU.subtract).then_inc(s_dve, 1)
                def low_part(name, stg, bias_n, whole_m=None):
                    t = full(name)
                    dve.wait_ge(s_act, cur(b, N_ACT, ACT_AT[name]))
                    for m in range(2):
                        bm = m if whole_m is None else whole_m
                        last = v.scalar_tensor_tensor(stage[:, stg, 1, m * 512:(m + 1) * 512],
                                                      t[:, m * 512:(m + 1) * 512], bias_c[:, bias_n, bm:bm + 1],
                                                      stage[:, stg, 0, m * 512:(m + 1) * 512].bitcast(F32), ALU.add, ALU.subtract)
                    last.then_inc(s_dve, 1)

                low_part("kc0", 0, 1, 0)
                for k in range(4):
                    t = full(f"bc{k}")
                    v.tensor_tensor(phiq[:, 2 * k:2 * k + 2, :], phiq[:, 2 * k:2 * k + 2, :],
                                    t[:].rearrange("p (a t) -> p a t", a=2), ALU.mult).then_inc(s_dve, 1)

                def residual(name, half):
                    t = full(name)
                    i = slice(2 * half, 2 * half + 2)
                    v.tensor_tensor(r_s[:, i, :], t[:, 0:2 * C].rearrange("p (i c) -> p i c", i=2), xb[:, i, :],
                                    ALU.add).then_inc(s_dve, 1)
                    dve.wait_ge(s_dve, cur(b, N_DVE, DVE_AT[name]))
                    for i in range(2 * half, 2 * half + 2):
                        last = v.bn_stats(stats[:, i, :], r_s[:, i, :])
                    step(last)

                def layer_norm():
                    layer_norm_steps(v, step, r_s, x1, stats, mv, nwt, nwi, s_ln)

                dve.wait_ge(s_xb, cur(b, 2, 1))
                residual("attn0", 0)
                residual("attn1", 1)
                dve.wait_ge(s_x2, cur(b, 16, 0))
                layer_norm()

                for k in range(2):
                    t = full(f"vc{k}")
                    for a in range(4):
                        last = v.tensor_tensor(u_s[:, k, a],
                                               t[:, a * C:(a + 1) * C].rearrange("p (h d) -> p h d", h=XH),
                                               bcv_bc[:].rearrange("p (h d) -> p h d", h=XH), ALU.add)
                    last.then_inc(s_dve, 1)

                low_part("kc1", 1, 1, 1)
                low_part("k", 0, 0)
                low_part("q", 1, 2)
                low_part("qc", 0, 3)
                t = full("v")
                for i in range(NT):
                    last = v.tensor_tensor(u_s[:, U_AT[2], i],
                                           t[:, i * C:(i + 1) * C].rearrange("p (h d) -> p h d", h=XH),
                                           bv_bc[:].rearrange("p (h d) -> p h d", h=XH), ALU.add)
                last.then_inc(s_dve, 1)

                def reduce(h, n):
                    s = RING_AT["bank", h, n]
                    if n == 0:
                        dve.wait_ge(s_max, cur(b, XH, h))
                    dve.wait_ge(s_sc, cur(b, NRING, s + 1))
                    pb = ps[2][:, (s % 2) * 512:(s % 2) * 512 + 512]
                    if n >= NSX:
                        for i, col in SELF_MAX[n - NSX]:
                            last = v.reduce_max(mpad[:, i, 64:65], pb[:, col:col + (i + 1) * P], AX.X)
                        last.then_inc(s_red, 1)
                    else:
                        i, half = n // 2, n % 2
                        v.reduce_max(cmax[:, i, half:half + 1], pb, AX.X).then_inc(s_red, 1)
                    if n == NSX - 1:
                        dve.wait_ge(s_red, cur(b, NRED, RED_AT["bank", h, n]))
                        v.tensor_tensor(mpad[:, :, 96], cmax[:, :, 0], cmax[:, :, 1], ALU.max).then_inc(s_max, 1)

                def results(g):
                    s = RING_AT["turn", g, 0]
                    dve.wait_ge(s_sc, cur(b, NRING, s + 1))
                    pb = ps[2][:, (s % 2) * 512:(s % 2) * 512 + 2 * NT * HG * RW]
                    tv = pb.rearrange("p (i h d) -> p i h d", i=2 * NT, h=HG)
                    step(v.reciprocal(rec[:], tv[:, :, :, XD]))
                    v.tensor_tensor(yn[:], tv[:, :, :, 0:XD],
                                    rec[:].unsqueeze(3).broadcast_to([P, 2 * NT, HG, XD]), ALU.mult).then_inc(s_red, 1)
                    dve.wait_ge(s_red, cur(b, NRED, RED_AT["turn", g, 0]))
                    v.tensor_tensor(y_s[:, :, g * HG * XD:(g + 1) * HG * XD].rearrange("p i (h d) -> p i h d", h=HG),
                                    yn[:, 0:NT], yn[:, NT:2 * NT], ALU.add).then_inc(s_ys, 1)
                    dve.wait_ge(s_ys, cur(b, XH // HG, g + 1))

                def round_exps(h, n):
                    g, w = h * NE_ + n, E_COLS[n]
                    dve.wait_ge(s_exp, cur(b, XH * NE_, g + 1))
                    v.tensor_copy(high[:, g % RING_E, 0:w], exps[:, g % RING_E, 0:w]).then_inc(s_rnd["D"], 1)

                def rest_exps(h, n):
                    g, who, c0, c1 = h * NE_ + n, ROUND_BY[n], POOL_COLS[n], E_COLS[n]
                    dve.wait_ge(s_rnd[who], cur(b, N_ROUND[who], ROUND_AT[who][h, n]))
                    v.tensor_tensor(low[:, g % RING_E, c0:c1], exps[:, g % RING_E, c0:c1],
                                    high[:, g % RING_E, c0:c1].bitcast(F32), ALU.subtract).then_inc(s_rest_d, 1)

                for kind, h, n in ORDER:
                    if kind == "bank":
                        reduce(h, n)
                    elif kind == "turn":
                        results(h)
                    elif kind == "round" and ROUND_BY[n] == "D":
                        round_exps(h, n)
                    elif kind == "rest":
                        rest_exps(h, n)

                dve.wait_ge(s_xb, cur(b, 2, 2))
                residual("proj0", 0)
                residual("proj1", 1)
                layer_norm()
                t = full("gate")
                step(v.tensor_tensor(lg[:], t[:, 0:NT * E].rearrange("p (i e) -> p i e", i=NT),
                                     gb_bc[:].unsqueeze(1).broadcast_to([P, NT, E]), ALU.add))
                step(v.reduce_max(lmax[:], lg[:], AX.X))
                step(v.tensor_tensor(lw[:], lg[:], lmax[:].unsqueeze(2).broadcast_to([P, NT, E]), ALU.is_ge))
                step(v.tensor_tensor(lw[:], lw[:], rank8[:].unsqueeze(1).broadcast_to([P, NT, E]), ALU.mult))
                step(v.reduce_max(lmax[:], lw[:], AX.X))
                v.tensor_tensor(onehot[:, bass.ds(b * NT, NT), :], lw[:],
                                lmax[:].unsqueeze(2).broadcast_to([P, NT, E]), ALU.is_equal).then_inc(s_dve, 1)
            assert steps[0] == NSTEP, steps[0]


def layer_norm_steps(v, step, src, dst, stats, mv, nwt, nwi, done, n=NT):
    even, odd = stats[:, :, 1:3], stats[:, :, 4:6]
    v.tensor_tensor(mv[:, 0:2, :].rearrange("p w i -> p i w"), even, odd, ALU.add)
    step(v.tensor_tensor(mv[:, 2, :], stats[:, :, 1], stats[:, :, 4], ALU.subtract))
    v.tensor_scalar(mv[:, 0, :], mv[:, 0, :], 0.5, None, ALU.mult)
    v.tensor_scalar(mv[:, 1, :], mv[:, 1, :], 1.0 / C, LN_EPS, ALU.mult, ALU.add)
    step(v.scalar_tensor_tensor(mv[:, 3, :], mv[:, 2, :], 0.25, mv[:, 2, :], ALU.mult, ALU.mult))
    ve = nwt[:, 0, :]
    step(v.tensor_tensor(ve, mv[:, 1, :], mv[:, 3, :], ALU.add))
    step(v.tensor_scalar(nwi[:, 0, :], ve.bitcast(I32), 1, None, ALU.logical_shift_right))
    step(v.tensor_scalar(nwi[:, 1, :], nwi[:, 0, :], -1.0, float(0x5F3759DF), ALU.mult, ALU.add))
    y0 = nwi[:, 1, :].bitcast(F32)
    for k in range(3):
        a, t2, y1 = nwt[:, 1, :], nwt[:, 2, :], nwt[:, 3 + k % 2, :]
        step(v.scalar_tensor_tensor(a, y0, -0.5, y0, ALU.mult, ALU.mult))
        step(v.tensor_tensor(t2, a, ve, ALU.mult))
        step(v.scalar_tensor_tensor(y1, t2, 1.5, y0, ALU.add, ALU.mult))
        y0 = y1
    for i in range(n):
        last = v.tensor_scalar(dst[:, i, :], src[:, i, :], mv[:, 0, i:i + 1], y0[:, i:i + 1],
                               ALU.subtract, ALU.mult)
    last.then_inc(done, 1)


def experts(nc, onehot, x2d, xs, ys, w1T, b1p, w2T, b2, ident_d, tri_d, iota_d, out):
    ctx = ExitStack()
    with ctx:
        def sb(name, shape, dt=F32):
            return ctx.enter_context(nc.sbuf_tensor(name, shape, dt))

        def sem(name):
            return ctx.enter_context(nc.semaphore(name))

        ident = sb("e_ident", [P, P])
        tri = sb("tri", [P, P])
        ones = sb("ones", [P, P])
        iota = sb("iota", [P, B * NT])
        x2s = sb("x2s", [P, B * NT, C])
        within = sb("within", [P, B * NT, E])
        cnt = sb("cnt", [P, B * NT, E])
        cum = [sb(f"cum{i}", [P, B * NT, E]) for i in range(2)]
        big = sb("big", [P, E, MAXT])
        mt = sb("mt", [P, MAXT])
        tiles = sb("tiles", [P, E])
        st = [sb(f"st{i}", [P, E]) for i in range(2)]
        eidf = sb("eidf", [P, NTILE])
        eidc = sb("eidc", [P, NTILE, E])
        eid = sb("eid", [P, NTILE], I32)
        slotf = sb("slotf", [P, B * NT])
        slot = sb("slot", [P, B * NT], U32)
        w1s = [sb(f"w1s{i}", [P, KC, HID]) for i in range(2)]
        w2s = [sb(f"w2s{i}", [P, NHC, C]) for i in range(2)]
        b1s = [sb(f"b1s{i}", [P, NHC]) for i in range(2)]
        b2s = [sb(f"b2s{i}", [P, C]) for i in range(2)]
        xin = [sb(f"xin{i}", [P, TH, C]) for i in range(2)]
        xinT = [sb(f"xinT{i}", [P, KC, TILE]) for i in range(2)]
        hT = [sb(f"hT{i}", [P, NHC, TILE]) for i in range(2)]
        yo = [sb(f"yo{i}", [P, TH, C]) for i in range(2)]
        rows = [sb(f"rows{i}", [P, NT, C]) for i in range(2)]
        res = [sb(f"res{i}", [P, NT, C]) for i in range(2)]
        stats = sb("e_stats", [P, NT, 6])
        mv = sb("e_mv", [P, 4, NT])
        nwt = sb("e_nwt", [P, 5, NT])
        nwi = sb("e_nwi", [P, 2, NT], I32)
        pr = ctx.enter_context(nc.psum_tensor("pr", [P, 2, 512], F32))
        px = ctx.enter_context(nc.psum_tensor("px", [P, 512], F32))
        ph = [ctx.enter_context(nc.psum_tensor(f"ph{i}", [P, 512], F32)) for i in range(2)]
        py = [ctx.enter_context(nc.psum_tensor(f"py{i}", [P, 512], F32)) for i in range(2)]

        s_c = sem("e_const")
        s_pace = sem("e_pace")
        s_x2 = sem("e_x2")
        s_one = sem("e_ones")
        s_cnt = sem("e_cnt")
        s_step = sem("e_step")
        s_route = sem("e_route")
        s_xs = sem("e_xs")
        s_w = [sem(f"e_w{i}") for i in range(2)]
        s_xt = sem("e_xt")
        s_xc = sem("e_xc")
        s_h = sem("e_h")
        s_ha = sem("e_ha")
        s_y = sem("e_y")
        s_yo = sem("e_yo")
        s_ys = [sem(f"e_ys{i}") for i in range(2)]
        s_g = [sem(f"e_g{i}") for i in range(2)]
        s_r = sem("e_r")
        s_ln = sem("e_ln")
        s_out = [sem(f"e_out{i}") for i in range(2)]

        block = ctx.enter_context(nc.Block())
        NH2 = NHC // 2

        @block.sync
        def _(sp):
            for dst, src in ((ident, ident_d), (tri, tri_d), (iota, iota_d)):
                sp.dma_start(dst[:], src).then_inc(s_c, 16)
            sp.dma_start(x2s[:], x2d.rearrange("(n p) c -> p n c", p=P)).then_inc(s_x2, 16)
            sp.wait_ge(s_route, 2)

            with sp.Fori(0, NTILE // 2) as tt:
                for i in range(2):
                    t = tt * 2 + i
                    e = sp.value_load(eid[0:1, bass.ds(t, 1)], min_val=0, max_val=E - 1)
                    sp.wait_ge(s_yo, tt * 2 + (i + 1))
                    sp.sem_inc(s_pace, 1)
                    sp.dma_start(w1s[i][:], w1T[bass.ds(e, 1)].rearrange("a (k p) h -> p (a k) h", p=P)).then_inc(s_w[i], 16)
                    sp.dma_start(w2s[i][:], w2T[bass.ds(e, 1)].rearrange("a (k p) c -> p (a k) c", p=P)).then_inc(s_w[i], 16)
                    sp.dma_start(b1s[i][:], b1p[bass.ds(e, 1)].rearrange("a p k -> (a p) k")).then_inc(s_w[i], 16)
                    sp.dma_start(b2s[i][:], b2[bass.ds(e, 1)].broadcast_to([P, C])).then_inc(s_w[i], 16)
                    if i == 0:
                        sp.wait_ge(s_xs, 16 * B * NT)
                    sp.dma_start(xin[i][:], xs[bass.ds(t, 1)].rearrange("a (n p) c -> p (a n) c", p=P)).then_inc(s_w[i], 16)
            for n in range(B):
                i = n % 2
                sp.wait_ge(s_ln, n + 1)
                sp.dma_start(out[n].rearrange("(i p) c -> p i c", p=P), res[i][:]).then_inc(s_out[i], 16)
            for i in range(2):
                sp.wait_ge(s_out[i], 16 * B // 2)

        @block.gpsimd
        def _(pool):
            pool.wait_ge(s_x2, 16)
            pool.wait_ge(s_route, 1)
            xs_rows = xs.rearrange("t r c -> (t r) c")
            ys_rows = ys.rearrange("t r c -> (t r) c")
            for j in range(B * NT):
                nc.gpsimd.indirect_dma_start(
                    xs_rows, bass.IndirectOffsetOnAxis(slot[:, j:j + 1], 0), x2s[:, j, :], None,
                    bounds_check=NTILE * TILE - 1).then_inc(s_xs, 16)
            for i in range(2):
                pool.wait_ge(s_ys[i], 16 * NTILE // 2 + 16)
            for n in range(B):
                if n >= 2:
                    pool.wait_ge(s_r, n - 1)
                for a in range(NT):
                    j = n * NT + a
                    nc.gpsimd.indirect_dma_start(
                        rows[n % 2][:, a, :], None, ys_rows, bass.IndirectOffsetOnAxis(slot[:, j:j + 1], 0),
                        bounds_check=NTILE * TILE - 1).then_inc(s_g[n % 2], 16)

        @block.tensor
        def _(pe):
            mm, tr = nc.tensor.matmul, nc.tensor.transpose
            oh = onehot[:].rearrange("p n e -> p (n e)")
            pe.wait_ge(s_c, 48)
            pe.wait_ge(s_one, 1)
            mm(pr[:, 0, 0:B * NT * E], tri[:], oh, start=True, stop=True)
            mm(pr[:, 1, 0:B * NT * E], ones[:], oh, start=True, stop=True).then_inc(s_cnt, 1)
            pe.sem_inc(s_xt, 2)
            pe.sem_inc(s_h, 2 * NH2)
            pe.sem_inc(s_y, 2)
            with pe.Fori(0, NTILE // 2) as tt:
                for i in range(2):
                    pe.wait_ge(s_w[i], (tt + 1) * 80)
                    pe.wait_ge(s_xc, tt * 2 + (i + 1))
                    for k in range(KC):
                        for n in range(TH):
                            last = tr(px[:, k * TILE + n * P:k * TILE + (n + 1) * P], xin[i][:, n, k * P:(k + 1) * P], ident[:])
                    last.then_inc(s_xt, 1)
                    pe.wait_ge(s_xc, tt * 2 + (i + 2))
                    for c in range(NH2):
                        g = i * NH2 + c
                        pe.wait_ge(s_ha, tt * (2 * NH2) + (2 * NH2 + g - 1))
                        for a in range(2):
                            for k in range(KC):
                                last = mm(ph[g % 2][:, a * TILE:(a + 1) * TILE],
                                          w1s[i][:, k, (2 * c + a) * P:(2 * c + a + 1) * P], xinT[i][:, k, :],
                                          start=k == 0, stop=k == KC - 1)
                        last.then_inc(s_h, 1)
                    pe.wait_ge(s_ha, tt * (2 * NH2) + (2 * NH2 + (i + 1) * NH2))
                    pe.wait_ge(s_yo, tt * 2 + (i + 1))
                    for n in range(TH):
                        for c in range(NHC):
                            last = mm(py[i][:, n * C:(n + 1) * C], hT[i][:, c, n * P:(n + 1) * P], w2s[i][:, c, :],
                                      start=c == 0, stop=c == NHC - 1)
                    last.then_inc(s_y, 1)

        @block.scalar
        def _(act):
            act.sem_inc(s_xc, 1)
            act.sem_inc(s_ha, 2 * NH2)
            for i in range(2):
                act.sem_inc(s_ys[i], 16)
            with act.Fori(0, NTILE // 2) as tt:
                for i in range(2):
                    act.wait_ge(s_xt, tt * 2 + (2 + i + 1))
                    nc.scalar.activation(xinT[i][:], px[:].rearrange("p (k t) -> p k t", k=KC), ACT.Copy).then_inc(s_xc, 1)
                    act.wait_ge(s_y, tt * 2 + (i + 1))
                    for c in range(NH2):
                        g = i * NH2 + c
                        act.wait_ge(s_h, tt * (2 * NH2) + (2 * NH2 + g + 1))
                        for a in range(2):
                            last = nc.scalar.activation(hT[i][:, 2 * c + a, :], ph[g % 2][:, a * TILE:(a + 1) * TILE],
                                                        ACT.Relu, bias=b1s[i][:, 2 * c + a:2 * c + a + 1])
                        last.then_inc(s_ha, 1)
                    act.wait_ge(s_yo, tt * 2 + (2 + i + 1))
                    act.dma_start(ys[bass.ds(tt * 2 + i, 1)].rearrange("a (n p) c -> p (a n) c", p=P),
                                  yo[i][:]).then_inc(s_ys[i], 16)

        @block.vector
        def _(dve):
            v = nc.vector
            steps = [0]

            def step(ins):
                steps[0] += 1
                ins.then_inc(s_step, 1)
                dve.wait_ge(s_step, steps[0])

            v.memset(ones[:], 1.0).then_inc(s_one, 1)
            dve.wait_ge(s_c, 48)
            step(v.tensor_scalar(mt[:], iota[:, 0:MAXT], float(TILE), None, ALU.mult))
            dve.wait_ge(s_cnt, 1)
            J = B * NT
            v.tensor_copy(within[:], pr[:, 0, 0:J * E].rearrange("p (n e) -> p n e", n=J))
            step(v.tensor_copy(cnt[:], pr[:, 1, 0:J * E].rearrange("p (n e) -> p n e", n=J)))
            src, k, n = cnt, 1, 0
            while k < J:
                dst = cum[n % 2]
                v.tensor_copy(dst[:, 0:k, :], src[:, 0:k, :])
                step(v.tensor_tensor(dst[:, k:J, :], src[:, k:J, :], src[:, 0:J - k, :], ALU.add))
                src, k, n = dst, 2 * k, n + 1
            total, other = src, cum[n % 2]
            step(v.tensor_tensor(big[:], mt[:].unsqueeze(1).broadcast_to([P, E, MAXT]),
                                 total[:, J - 1, :].unsqueeze(2).broadcast_to([P, E, MAXT]), ALU.is_lt))
            step(v.reduce_sum(tiles[:], big[:], AX.X))
            step(v.memset(st[0][:, 0:1], 0.0))
            step(v.tensor_copy(st[0][:, 1:E], tiles[:, 0:E - 1]))
            src, k, n = st[0], 1, 1
            while k < E:
                dst = st[n % 2]
                v.tensor_copy(dst[:, 0:k], src[:, 0:k])
                step(v.tensor_tensor(dst[:, k:E], src[:, k:E], src[:, 0:E - k], ALU.add))
                src, k, n = dst, 2 * k, n + 1
            first, firstrow = src, st[n % 2]
            step(v.tensor_scalar(firstrow[:], first[:], float(TILE), None, ALU.mult))
            step(v.tensor_tensor(other[:], total[:], cnt[:], ALU.subtract))
            step(v.tensor_tensor(other[:], other[:], within[:], ALU.add))
            step(v.tensor_tensor(other[:], other[:], firstrow[:].unsqueeze(1).broadcast_to([P, J, E]), ALU.add))
            step(v.tensor_tensor(other[:], other[:], onehot[:], ALU.mult))
            step(v.reduce_sum(slotf[:], other[:], AX.X))
            v.tensor_copy(slot[:], slotf[:]).then_inc(s_route, 1)
            step(v.tensor_tensor(eidc[:], iota[:, 0:NTILE].unsqueeze(2).broadcast_to([P, NTILE, E]),
                                 first[:].unsqueeze(1).broadcast_to([P, NTILE, E]), ALU.is_ge))
            step(v.reduce_sum(eidf[:], eidc[:], AX.X))
            v.tensor_scalar(eid[:], eidf[:], 1.0, None, ALU.subtract).then_inc(s_route, 1)

            dve.sem_inc(s_yo, 2)
            with dve.Fori(0, NTILE // 2) as tt:
                for i in range(2):
                    dve.wait_ge(s_y, tt * 2 + (2 + i + 1))
                    dve.wait_ge(s_ys[i], tt * 16 + 16)
                    v.tensor_tensor(yo[i][:], py[i][:].rearrange("p (n c) -> p n c", n=TH),
                                    b2s[i][:].unsqueeze(1).broadcast_to([P, TH, C]), ALU.add).then_inc(s_yo, 1)

            for n in range(B):
                i = n % 2
                dve.wait_ge(s_g[i], (n // 2 + 1) * NT * 16)
                if n >= 2:
                    dve.wait_ge(s_out[i], (n // 2) * 16)
                v.tensor_tensor(res[i][:], rows[i][:], x2s[:, n * NT:(n + 1) * NT, :], ALU.add).then_inc(s_r, 1)
                dve.wait_ge(s_r, n + 1)
                for a in range(NT):
                    last = v.bn_stats(stats[:, a, :], res[i][:, a, :])
                step(last)
                layer_norm_steps(v, step, res[i], res[i], stats, mv, nwt, nwi, s_ln)
                dve.wait_ge(s_ln, n + 1)


_ORDER = ("x xT ctxT wqkT wv_l rf w_out b_out wk bk wq bq wv bv wck bck wcq bcq wcv bcv wp bp "
          "gate_wT gate_b w1T b1p w2T b2 ident mask_qk mask_kq sel fold tri iota").split()


def kernel(**inputs):
    from concourse import bacc as _bacc
    from concourse.bass_utils import run_bass_kernel_spmd as _run

    d = {k: np.asarray(v) for k, v in inputs.items()}
    c = np.ascontiguousarray
    w_qkv = d["L0_attn_W_qkv"]
    a = {
        "x": d["x"], "xT": c(d["x"].transpose(0, 2, 1)), "ctxT": c(d["ctx_512"].transpose(0, 2, 1)),
        "wqkT": c(w_qkv[:, :2 * LR].T), "wv_l": c(w_qkv[:, 2 * LR:]), "rf": d["L0_attn_RF"],
        "w_out": d["L0_attn_W_out"], "b_out": d["L0_attn_b_out"],
        "gate_wT": c(d["L0_ffn_gate_w"].T), "gate_b": d["L0_ffn_gate_b"],
        "w1T": c(d["L0_ffn_w1"].transpose(0, 2, 1)),
        "b1p": c(d["L0_ffn_b1"].reshape(E, NHC, P).transpose(0, 2, 1)),
        "w2T": c(d["L0_ffn_w2"].transpose(0, 2, 1)), "b2": d["L0_ffn_b2"],
    }
    for n in ("k", "q", "v", "ck", "cq", "cv", "p"):
        a["w" + n], a["b" + n] = d["L0_xattn_W" + n], d["L0_xattn_b" + n]
    at = np.arange(P)
    a["ident"] = np.eye(P, dtype=np.float32)
    a["mask_qk"] = np.where(at[None, :] <= at[:, None], 0, NEG).astype(np.float32)
    a["mask_kq"] = np.where(at[:, None] <= at[None, :], 0, NEG).astype(np.float32)
    a["sel"] = np.zeros((3 * LH, NPAIR, P), np.float32)
    for h in range(LH):
        a["sel"][[h, 2 * LH + h], h // 2, h % 2 * LD:(h % 2 + 1) * LD] = 1
    a["fold"] = np.zeros((P, P), np.float32)
    for q in range(HG):
        for d in range(VW):
            a["fold"][q * HP + d, q * RW + d % RW] = 1
    a["tri"] = (at[:, None] < at[None, :]).astype(np.float32)
    a["iota"] = np.ascontiguousarray(np.broadcast_to(np.arange(B * NT, dtype=np.float32), (P, B * NT)))

    nc = _bacc.Bacc("TRN2", target_bir_lowering=False, num_devices=1)
    arrays, args = {}, []
    for name in _ORDER:
        arrays[f"in_{name}"] = c(a[name])
        args.append(nc.dram_tensor(f"in_{name}", a[name].shape, mybir.dt.from_np(a[name].dtype), kind="ExternalInput").ap())
    args.append(nc.dram_tensor("out_0", (B, T, C), F32, kind="ExternalOutput").ap())
    decoder(nc, *args)
    r = _run(nc, [arrays], core_ids=[0])
    return r.results[0]["out_0"]
```

```python
import numpy as np
import concourse.bass as bass
from concourse import mybir
from contextlib import ExitStack

F32 = mybir.dt.float32
F32R = mybir.dt.float32r
BF16 = mybir.dt.bfloat16
I32 = mybir.dt.int32
U32 = mybir.dt.uint32
ALU = mybir.AluOpType
ACT = mybir.ActivationFunctionType
AX = mybir.AxisListType

P = 128
B, T, C = 8, 512, 256
NT = T // P
KC = C // P
LH, LD = 16, 64
LR = LH * LD
NPAIR = LH // 2
XH, XD = 16, 16
TC_, CC = 1024, 128
NTC = TC_ // P
E, HID = 8, 1024
NHC = HID // P
LN_EPS = 1e-5
STAB = 1e-6
SCALE = float(1.0 / np.sqrt(XD))
NEG = -1e30
KROW = 4 * XD
MROW = KROW
VW = 2 * XD + 1
RW = XD + 1

JOBS = [("kf2", "D"), ("kf3", "D"), ("g0", "A"), ("ksum", "D"), ("norm", "D"),
        ("g1", "D"), ("kc0", "B"), ("kv", "A"), ("bc0", "D"), ("m0", "A"), ("bc1", "D"), ("m1", "A"),
        ("bc2", "D"), ("bc3", "D"), ("attn0", "D"), ("attn1", "D"), ("vc0", "D"), ("vc1", "D"), ("kc1", "B"),
        ("x1T", "A"), ("k0", "B"), ("q0", "B"), ("qc0", "B"), ("k1", "B"), ("q1", "B"), ("qc1", "B"), ("v", "D"),
        ("yT", "A"), ("proj0", "D"), ("proj1", "D"),
        ("qf0", "A"), ("qf1", "A"), ("qf2", "A"), ("qf3", "A"), ("kf0", "D"), ("x2T", "A"), ("kf1", "D"),
        ("gate", "D")]
NQF = 4
NJ = len(JOBS)
JN = {name: n for n, (name, _) in enumerate(JOBS)}
ACT_AT = {name: sum(w in "AB" for _, w in JOBS[:n + 1]) for n, (name, w) in enumerate(JOBS)}
DVE_AT = {name: sum(w in "DB" for _, w in JOBS[:n + 1]) for n, (name, w) in enumerate(JOBS)}
N_ACT, N_DVE = ACT_AT["gate"], DVE_AT["gate"]
STAGED = {"kc0": (0, 0, ("q1", "qc1")), "kc1": (1, 0, ("qc0", "k1")), "k0": (0, 0, ("kc0",)), "q0": (0, T, ("kc0",)),
          "qc0": (1, 0, ("kc1",)), "k1": (1, T, ("kc1",)), "q1": (0, 0, ("k0",)), "qc1": (0, T, ("q0",))}
LAST_STAGED = ("qc0", "k1", "q1", "qc1")

NSX = 2 * NT
NSB = NSX + 3
SELF_MAX = [[(3, 0)], [(2, 0), (0, 384)], [(1, 0)]]
NE_ = 2 + NTC // 2
SELF_EXP = [[(0, 0), (1, 512), (3, 896)], [(2, 0)]]
E_COLS = [1024, 256] + [1024] * (NE_ - 2)
S_PLAN = [2, 2, 2, 2, 2, 2]
AHEAD = 2
ROUND_BY = ["A", "D", "D", "A", "D", "A"]
POOL_COLS = [576, 0, 576, 576, 576, 576]
REST_POS = 2
TURN_AT = 5
HS = 4
HG = 2
HP = P // HG
RING_E = 4
U_AT = [0, 1, 3]
LAG = 3


def heads_order():
    ahead = []
    for h in range(XH + 1):
        banks = [("bank", h, n) for n in range(NSB)] if h < XH else []
        ahead += banks[:2] + [("maxima", h - 1, 0)] * (h > 0) + banks[2:]
    first = ahead.index(("maxima", 0, 0)) + 1 + AHEAD
    order, ahead = ahead[:first], ahead[first:]
    steps = XH * NE_
    for g in range(steps + LAG):
        h, n = divmod(g, NE_)
        if n == LAG and h:
            order.append(("keep", h - 1, 0))
        extra = []
        if g < steps:
            assert n or ("maxima", h, 0) in order
            order.append(("scores", h, n))
            if ROUND_BY[n] == "A":
                order.append(("round", h, n))
            extra, ahead = ahead[:S_PLAN[n]], ahead[S_PLAN[n]:]
        if 1 <= g <= steps:
            former = divmod(g - 1, NE_)
            extra[REST_POS:REST_POS] = [("rest", *former)]
            if ROUND_BY[former[1]] == "D":
                extra[0:0] = [("round", *former)]
        order += extra
        if n == TURN_AT and h and h % HG == 0:
            order.append(("turn", h // HG - 1, 0))
        if g >= LAG:
            order.append(("weigh", *divmod(g - LAG, NE_)))
    assert not ahead
    return order + [("keep", XH - 1, 0), ("turn", XH // HG - 1, 0)]


ORDER = heads_order()
RING = [e for e in ORDER if e[0] in ("bank", "maxima", "turn")]
RING_AT = {e: n for n, e in enumerate(RING)}
NRING, NRED = len(RING), sum(e[0] != "maxima" for e in RING)
RED_AT = {e: sum(f[0] != "maxima" for f in RING[:n + 1]) for n, e in enumerate(RING)}
ROUND_AT = {w: {(h, n): sum(ROUND_BY[m % NE_] == w for m in range(h * NE_ + n + 1))
                for h in range(XH) for n in range(NE_)} for w in "AD"}
N_ROUND = {w: ROUND_BY.count(w) * XH for w in "AD"}
POOL_AT = {(h, n): sum(POOL_COLS[m % NE_] > 0 for m in range(h * NE_ + n + 1)) for h in range(XH) for n in range(NE_)}
N_POOL = sum(c > 0 for c in POOL_COLS) * XH
WCOLS = 2 * 512

TILE = 256
TH = TILE // P
NTILE = (B * T + E * (TILE - 1)) // TILE
assert NTILE % 2 == 1
MAXT = B * T // TILE
CR = C + 1
E_STEPS = 30
NOBODY = float(1 << 20)
BLANKS = 2
assert NTILE * TILE >= B * T + E * (TILE - 1) - (TILE - 1)


def decoder(nc, x, xT, ctxT, wqkT, wv_l, rf, w_out, b_out, wk, bk, wq, bq, wv, bv, wck, bck, wcq, bcq,
            wcv, bcv, wp, bp, gate_wT, gate_b, w1T, b1p, w2T, b2, ident_d, mask_qk, mask_kq, sel_d, fold_d,
            tri_d, iota_d, number_d, out, nb=B):
    x2d = nc.dram_tensor("x2d", [B * T, C], F32, kind="Internal").ap()
    xs = nc.dram_tensor("xs", [NTILE, TILE, CR], F32, kind="Internal").ap()
    with nc.sbuf_tensor("onehot", [P, B * NT, E], F32) as onehot:
        attentions(nc, x, xT, ctxT, wqkT, wv_l, rf, w_out, b_out, wk, bk, wq, bq, wv, bv, wck, bck,
                   wcq, bcq, wcv, bcv, wp, bp, gate_wT, gate_b, ident_d, mask_qk, mask_kq, sel_d, fold_d,
                   onehot, x2d.rearrange("(b t) c -> b t c", b=B), xs, nb)
        experts(nc, onehot, x2d, xs, w1T, b1p, w2T, b2, ident_d, tri_d, iota_d, number_d, out)


def attentions(nc, x, xT, ctxT, wqkT, wv_l, rf, w_out, b_out, wk, bk, wq, bq, wv, bv, wck, bck,
               wcq, bcq, wcv, bcv, wp, bp, gate_wT, gate_b, ident_d, mask_qk, mask_kq, sel_d, fold_d,
               onehot, x2d, xs, nb):
    scr_k = nc.dram_tensor("scr_k", [2, C, T + TC_], F32, kind="Internal").ap()
    scr_q = nc.dram_tensor("scr_q", [2, C, 2 * T], F32, kind="Internal").ap()

    ctx = ExitStack()
    with ctx:
        def sb(name, shape, dt=F32):
            return ctx.enter_context(nc.sbuf_tensor(name, shape, dt))

        def sem(name):
            return ctx.enter_context(nc.semaphore(name))

        ident = sb("ident", [P, P])
        identb = sb("identb", [P, P], BF16)
        mqk = sb("mqk", [P, P], BF16)
        mkq = sb("mkq", [P, P], BF16)
        sel = sb("sel", [3 * LH, NPAIR, P], F32R)
        onescol = sb("onescol", [P, 1])
        fold = sb("fold", [P, P])
        wqf = sb("wqf", [P, KC, LR])
        wkf = sb("wkf", [P, KC, LR])
        wvl = sb("wvl", [P, KC, LR])
        wo = sb("wo", [P, NPAIR, C])
        wq_s = sb("wq_s", [P, KC, C])
        wk_s = sb("wk_s", [P, KC, C])
        wcq_s = sb("wcq_s", [P, KC, C])
        wv_s = sb("wv_s", [P, KC, C])
        wp_s = sb("wp_s", [P, KC, C])
        wck_s = sb("wck_s", [P, C])
        wcv_s = sb("wcv_s", [P, C])
        gw_s = sb("gw_s", [P, KC, E])
        bias_c = sb("bias_c", [P, 4, KC])
        bo_bc = sb("bo_bc", [P, C])
        bp_bc = sb("bp_bc", [P, C])
        bv_bc = sb("bv_bc", [P, C])
        bcv_bc = sb("bcv_bc", [P, C])
        gb_bc = sb("gb_bc", [P, E])
        ones_s = sb("ones_s", [P, NTC * XH])
        rank8 = sb("rank8", [P, E])
        x_s = sb("x_s", [P, NT, C])
        xT_s = sb("xT_s", [P, KC, T])
        ctxT_s = sb("ctxT_s", [P, TC_])
        with nc.sbuf_tensor("big_a", [P, NPAIR * T], F32) as big_a, \
                nc.sbuf_tensor("big_b", [P, NT * LR], F32) as big_b, \
                nc.sbuf_tensor("big_c", [P, NTC * XH * VW], F32) as big_c:
            pass
        low = sb("low", [P, RING_E, WCOLS], F32R)
        high = sb("high", [P, RING_E, WCOLS], F32R)
        vca = sb("vca", [P, NTC, XH, VW], F32R)
        phiq = big_a[:].rearrange("p (j t) -> p j t", j=NPAIR)
        phik = big_b[:].rearrange("p (i r) -> p i r", i=NT)
        rfbd = big_a[:, 0:NPAIR * P].rearrange("p (j r) -> p j r", j=NPAIR)
        wqkT_s = big_b[:].rearrange("p (j c) -> p j c", j=2 * NPAIR)
        u_s = big_a[:].rearrange("p (n a h d) -> p n a h d", n=4, a=4, h=XH)
        exps = big_a[:].rearrange("p (n c) -> p n c", n=RING_E)
        stage = high[:].rearrange("p (n w) c -> p n w c", n=2)
        g_s = big_c[:, 0:KC * LR].rearrange("p (k r) -> p k r", k=KC)
        m_s = big_c[:, KC * LR:KC * LR + NPAIR * C].rearrange("p (j c) -> p j c", j=NPAIR)
        sel_f = big_c[0:3 * LH, 0:NPAIR * P].rearrange("p (j r) -> p j r", j=NPAIR)
        kvbd = sb("kvbd", [P, NPAIR, P])
        ksbd = sb("ksbd", [P, NPAIR * LH])
        den = sb("den", [LH, T])
        rT = sb("rT", [3 * LH, T], F32R)
        xb = sb("xb", [P, NT, C])
        r_s = sb("r_s", [P, NT, C])
        cstage = r_s[:, 0, :]
        stats = sb("stats", [P, NT, 6])
        mv = sb("mv", [P, 4, NT])
        zero1 = sb("zero1", [P, 1])
        nwt = sb("nwt", [P, 5, NT])
        nwi = sb("nwi", [P, 2, NT], I32)
        x1 = sb("x1", [P, NT, C])
        x1T = sb("x1T", [P, KC, T])
        va = sb("va", [P, NT, XH, VW], F32R)
        hk = [sb(f"hk{i}", [P, T + TC_], F32R) for i in range(HS)]
        hq = [sb(f"hq{i}", [P, 2 * T], F32R) for i in range(HS)]
        mpad = sb("mpad", [P, NT, P])
        cmax = sb("cmax", [P, NT, 2])
        ykeep = sb("ykeep", [P, 2, T])
        rec = sb("rec", [P, 2 * NT, HG])
        yn = sb("yn", [P, 2 * NT, HG, XD])
        y_s = sb("y_s", [P, NT, C])
        psum01 = y_s[:].rearrange("p i c -> p (i c)")
        psum23 = r_s[:].rearrange("p i c -> p (i c)")
        yT_s = g_s[:, :, 0:T]
        lg = sb("lg", [P, NT, E])
        lmax = sb("lmax", [P, NT])
        lw = sb("lw", [P, NT, E])

        ps = [ctx.enter_context(nc.psum_tensor(f"ps{i}", [P, WCOLS], F32)) for i in range(4)]

        s_const = sem("s_const")
        s_wqk = sem("s_wqk")
        s_zrf = sem("s_zrf")
        s_rf = sem("s_rf")
        s_pset = sem("s_pset")
        s_sel = sem("s_sel")
        s_setup = sem("s_setup")
        s_wprod = sem("s_wprod")
        s_x = sem("s_x")
        s_tile = sem("s_tile")
        s_act = sem("s_act")
        s_dve = sem("s_dve")
        s_dstep = sem("s_dstep")
        s_xb = sem("s_xb")
        s_ln = sem("s_ln")
        s_st = {n: sem(f"s_st_{n}") for n in STAGED}
        s_hl = [sem(f"s_hl{i}") for i in range(HS)]
        s_zero = sem("s_zero")
        s_sc = sem("s_sc")
        s_red = sem("s_red")
        s_max = sem("s_max")
        s_mrow = sem("s_mrow")
        s_st2 = sem("s_st2")
        s_exp = sem("s_exp")
        s_av = sem("s_av")
        s_rnd = {"A": sem("s_rnd_a"), "D": sem("s_rnd_d")}
        s_rest_d = sem("s_rest_d")
        s_rest_p = sem("s_rest_p")
        s_psum = sem("s_psum")
        s_vh = sem("s_vh")
        s_vl = sem("s_vl")
        s_vone = sem("s_vone")
        s_keep = sem("s_keep")
        s_ys = sem("s_ys")
        s_pace = sem("s_pace")
        s_blank = sem("s_blank")
        s_x2 = sem("s_x2")

        def cur(b, per, k):
            return b * per + (per + k)

        block = ctx.enter_context(nc.Block())
        LOADS = 23
        xs_flat = xs.rearrange("t r c -> (t r c)").rearrange("(p n) -> p n", p=P)
        blank = x1[:].rearrange("p i c -> p (i c)")[:, 0:BLANKS * CR]
        NZ = NTILE * TILE // (P * BLANKS)
        assert NZ * P * BLANKS == NTILE * TILE

        @block.sync
        def _(sp):
            def const(dst, src):
                sp.dma_start(dst, src).then_inc(s_const, 16)

            sp.sem_inc(s_x2, 16)
            for n in STAGED:
                sp.sem_inc(s_st[n], 16)
            sp.dma_start(wqkT_s, wqkT.rearrange("(j p) c -> p j c", p=P)).then_inc(s_wqk, 16)
            sp.wait_ge(s_zrf, 1)
            rf_v = rf.rearrange("(j a) d r -> a d j r", a=2)
            sp.dma_start(rfbd[0:LD, :, 0:LD], rf_v[0]).then_inc(s_rf, 16)
            sp.dma_start(rfbd[LD:P, :, LD:P], rf_v[1]).then_inc(s_rf, 16)

            def load_x(b):
                sp.dma_start(x_s[:], x[b].rearrange("(i p) c -> p i c", p=P)).then_inc(s_x, 16)
                sp.dma_start(xT_s[:], xT[b].rearrange("(k p) t -> p k t", p=P)).then_inc(s_x, 16)
                sp.dma_start(ctxT_s[:], ctxT[b]).then_inc(s_x, 16)

            load_x(0)
            const(ident[:], ident_d)
            const(fold[:], fold_d)
            const(cstage[:, 0:P], mask_qk)
            const(cstage[:, P:2 * P], mask_kq)
            const(wvl[:], wv_l.rearrange("(k p) r -> p k r", p=P))
            const(wo[:], w_out.rearrange("(j p) c -> p j c", p=P))
            for dst, src in ((wq_s, wq), (wk_s, wk), (wcq_s, wcq), (wv_s, wv), (wp_s, wp)):
                const(dst[:], src.rearrange("(k p) c -> p k c", p=P))
            const(wck_s[:], wck)
            const(wcv_s[:], wcv)
            const(gw_s[:], gate_wT.rearrange("(k p) e -> p k e", p=P))
            for n, src in enumerate((bk, bck, bq, bcq)):
                sp.dma_start(bias_c[:, n, :], src.rearrange("(k p) -> p k", p=P),
                             allow_slow_non_contiguous=True).then_inc(s_const, 16)
            for dst, src in ((bo_bc, b_out), (bp_bc, bp), (bv_bc, bv), (bcv_bc, bcv), (gb_bc, gate_b)):
                const(dst[:], src.rearrange("(a c) -> a c", a=1).broadcast_to([P, dst.shape[1]]))
            sp.dma_start(sel_f, sel_d).then_inc(s_sel, 16)
            sp.wait_ge(s_setup, 2)
            for n in range(NZ):
                sp.dma_start(xs_flat[:, n * BLANKS * CR:(n + 1) * BLANKS * CR], blank).then_inc(s_blank, 16)

            def store(b, name, scr, col, w, m):
                stg, at, _ = STAGED[name]
                sp.wait_ge(s_dve, cur(b, N_DVE, DVE_AT[name]))
                sp.dma_start(scr[:, m * P:(m + 1) * P, col:col + w].rearrange("w r t -> r w t"),
                             stage[:, stg, :, at:at + w].bitcast(F32)).then_inc(s_st[name], 16)

            def stored(b, names):
                for n in names:
                    sp.wait_ge(s_st[n], cur(b, 16, 16))
                    sp.sem_inc(s_pace, 1)

            def load_head(b, h):
                i = h % HS
                sp.wait_ge(s_zero, cur(b, XH, h - HS + 1))
                sp.sem_inc(s_pace, 1)
                sp.wait_ge(s_st2, cur(b, XH * NE_, (h - HS + 1) * NE_))
                sp.sem_inc(s_pace, 1)
                for w in range(2):
                    sp.dma_start(hk[i][32 * w:32 * w + 32, :].bitcast(F32),
                                 scr_k[:, h * XD:(h + 1) * XD, :]).then_inc(s_hl[i], 16)
                    for d in range(2):
                        sp.dma_start(hq[i][32 * w + 16 * d:32 * w + 16 * d + 16, :].bitcast(F32),
                                     scr_q[w, h * XD:(h + 1) * XD, :]).then_inc(s_hl[i], 16)

            with sp.Fori(0, nb) as b:
                store(b, "kc0", scr_k, T, TC_, 0)
                store(b, "kc1", scr_k, T, TC_, 1)
                store(b, "k0", scr_k, 0, T, 0)
                store(b, "q0", scr_q, 0, T, 0)
                store(b, "qc0", scr_q, T, T, 0)
                store(b, "k1", scr_k, 0, T, 1)
                sp.sem_inc(s_pace, 1)
                following = sp.snap((b + 1) % nb)
                stored(b, ("kc0", "k0", "q0", "qc0"))
                for h in range(XH):
                    load_head(b, h)
                    if h == 0:
                        store(b, "q1", scr_q, 0, T, 1)
                        store(b, "qc1", scr_q, T, T, 1)
                        sp.sem_inc(s_pace, 1)
                    if h == 2:
                        stored(b, ("kc1", "k1", "q1", "qc1"))
                    if h == 3:
                        sp.wait_ge(s_xb, cur(b, 2, 1))
                        sp.sem_inc(s_pace, 1)
                        sp.wait_ge(s_tile, cur(b, NJ, JN["v"] + 1))
                        sp.sem_inc(s_pace, 1)
                        load_x(following)
                sp.wait_ge(s_ln, cur(b, 2, 2))
                sp.sem_inc(s_pace, 1)
                sp.dma_start(x2d[b].rearrange("(i p) c -> p i c", p=P), x1[:]).then_inc(s_x2, 16)
            sp.wait_ge(s_x2, (nb + 1) * 16)
            sp.wait_ge(s_x, (nb + 1) * 48)
            sp.wait_ge(s_blank, 16 * NZ)

        @block.gpsimd
        def _(pool):
            pool.sem_inc(s_xb, 2)
            pool.sem_inc(s_zero, XH)
            pool.sem_inc(s_psum, 3)
            pool.sem_inc(s_vl, 3)
            pool.sem_inc(s_rest_p, N_POOL)
            for i in range(HS):
                nc.gpsimd.memset(hk[i][MROW:P, :].bitcast(F32), 0.0)
                last = nc.gpsimd.memset(hq[i][MROW:P, :].bitcast(F32), 0.0)
            last.then_inc(s_pset, 1)
            pool.wait_ge(s_pset, 1)
            for i in range(HS):
                last = nc.gpsimd.memset(hk[i][MROW:MROW + 1, :].bitcast(F32), -1.0)
            last.then_inc(s_pset, 1)
            pool.wait_ge(s_pset, 2)
            pool.wait_ge(s_const, 16 * LOADS)
            pool.wait_ge(s_setup, 4)
            with pool.Fori(0, nb) as b:
                pool.wait_ge(s_x, (b + 1) * 48)
                pool.wait_ge(s_dve, cur(b, N_DVE, DVE_AT["proj1"] - N_DVE))
                for i in range(NT):
                    last = nc.gpsimd.tensor_tensor(xb[:, i, :], x_s[:, i, :], bo_bc[:], ALU.add)
                last.then_inc(s_xb, 1)
                pool.wait_ge(s_dve, cur(b, N_DVE, DVE_AT["kf1"] - N_DVE))
                nc.gpsimd.tensor_tensor(psum01, phik[:, 0, :], phik[:, 1, :], ALU.add).then_inc(s_psum, 1)
                pool.wait_ge(s_dve, cur(b, N_DVE, DVE_AT["kf3"]))
                nc.gpsimd.tensor_tensor(psum23, phik[:, 2, :], phik[:, 3, :], ALU.add).then_inc(s_psum, 1)
                pool.wait_ge(s_psum, cur(b, 3, 2))
                nc.gpsimd.tensor_tensor(psum01, psum01, psum23, ALU.add).then_inc(s_psum, 1)

                def low_values(n, dst):
                    pool.wait_ge(s_vh, cur(b, 3, n + 1))
                    nc.gpsimd.tensor_tensor(dst[:, :, :, RW:VW], u_s[:, U_AT[n]], dst[:, :, :, 0:XD].bitcast(F32),
                                            ALU.subtract).then_inc(s_vl, 1)

                for k in range(2):
                    low_values(k, vca[:, 4 * k:4 * k + 4])
                pool.wait_ge(s_ln, cur(b, 2, 1))
                for i in range(NT):
                    last = nc.gpsimd.tensor_tensor(xb[:, i, :], x1[:, i, :], bp_bc[:], ALU.add)
                last.then_inc(s_xb, 1)
                low_values(2, va)
                for kind, h, n in ORDER:
                    if kind != "rest":
                        continue
                    w = POOL_COLS[n]
                    if w:
                        who = ROUND_BY[n]
                        pool.wait_ge(s_rnd[who], cur(b, N_ROUND[who], ROUND_AT[who][h, n]))
                        slot = (h * NE_ + n) % RING_E
                        nc.gpsimd.tensor_tensor(low[:, slot, 0:w], exps[:, slot, 0:w], high[:, slot, 0:w].bitcast(F32),
                                                ALU.subtract).then_inc(s_rest_p, 1)
                    if n == NE_ - 1:
                        pool.wait_ge(s_st2, cur(b, XH * NE_, (h + 1) * NE_))
                        pool.wait_ge(s_rest_p, cur(b, N_POOL, POOL_AT[h, n]))
                        z = zero1[MROW:MROW + 1, :].broadcast_to([1, 2 * T])
                        nc.gpsimd.tensor_tensor(hq[h % HS][MROW:MROW + 1, :], z, z, ALU.add).then_inc(s_zero, 1)
                        pool.wait_ge(s_zero, cur(b, XH, h + 1))

        @block.tensor
        def _(pe):
            mm, tr = nc.tensor.matmul, nc.tensor.transpose
            pe.sem_inc(s_tile, JN["qf0"])
            pe.sem_inc(s_sc, NRING)
            pe.sem_inc(s_st2, XH * NE_)
            pe.sem_inc(s_av, XH * NE_)

            pe.wait_ge(s_wqk, 16)
            pe.wait_ge(s_rf, 32)
            for n in range(4):
                q, c = n // 2, n % 2
                for j in range(NPAIR):
                    last = mm(ps[n][:, j * P:(j + 1) * P], wqkT_s[:, q * NPAIR + j, c * P:(c + 1) * P],
                              rfbd[:, j, :], start=True, stop=True)
                last.then_inc(s_wprod, 1)

            def job(b, name, fill, act=None, dve=None):
                n = JN[name]
                prev = n - 4 if n >= 4 else max(m for m in range(NJ) if m % 4 == n % 4)
                back = n < 4
                former, who = JOBS[prev]
                a = [ACT_AT[former] - back * N_ACT] if who == "A" else []
                d = [DVE_AT[former] - back * N_DVE] if who != "A" else []
                a += [ACT_AT[act]] if act else []
                d += [DVE_AT[dve]] if dve else []
                if a:
                    pe.wait_ge(s_act, cur(b, N_ACT, max(a)))
                if d:
                    pe.wait_ge(s_dve, cur(b, N_DVE, max(d)))
                fill(ps[n % 4]).then_inc(s_tile, 1)

            def ring_bank(b, entry):
                n = RING_AT[entry]
                if n >= 2:
                    kind, h, _ = former = RING[n - 2]
                    if kind == "maxima":
                        pe.wait_ge(s_mrow, cur(b, XH, h + 1))
                    else:
                        pe.wait_ge(s_red, cur(b, NRED, RED_AT[former]))
                return ps[2][:, (n % 2) * 512:(n % 2) * 512 + 512]

            def score_bank(b, h, n):
                if n == 0:
                    pe.wait_ge(s_hl[h % HS], (b * (XH // HS) + (h // HS + 1)) * (6 * 16))
                    pe.wait_ge(s_zero, cur(b, XH, h - HS + 1))
                pb = ring_bank(b, ("bank", h, n))
                hk_, hq_ = hk[h % HS], hq[h % HS]
                if n >= NSX:
                    for i, col in SELF_MAX[n - NSX]:
                        w = (i + 1) * P
                        mm(pb[:, col:col + w], hq_[:, i * P:(i + 1) * P], hk_[:, 0:w], start=True, stop=False)
                        last = mm(pb[:, col + w - P:col + w], identb[:], mqk[:], start=False, stop=True)
                else:
                    i, half = n // 2, n % 2
                    last = mm(pb, hq_[:, T + i * P:T + (i + 1) * P],
                              hk_[:, T + half * 512:T + (half + 1) * 512], start=True, stop=True)
                last.then_inc(s_sc, 1)

            def maxima_row(b, h):
                pb = ring_bank(b, ("maxima", h, 0))
                pe.wait_ge(s_max, cur(b, XH, h + 1))
                pe.wait_ge(s_red, cur(b, NRED, RED_AT["bank", h, NSB - 1]))
                for i in range(NT):
                    last = tr(pb[:, i * P:(i + 1) * P], mpad[:, i, :], ident[:])
                last.then_inc(s_sc, 1)

            def exp_scores(b, h, n):
                g = h * NE_ + n
                pb = ps[g % 2]
                if n == 0:
                    pe.wait_ge(s_mrow, cur(b, XH, h + 1))
                pe.wait_ge(s_exp, cur(b, XH * NE_, g - 1))
                hk_, hq_ = hk[h % HS], hq[h % HS]
                if n < 2:
                    for j, col in SELF_EXP[n]:
                        mm(pb[:, col:col + T - j * P], hk_[:, j * P:(j + 1) * P], hq_[:, j * P:T],
                           start=True, stop=False)
                        last = mm(pb[:, col:col + P], identb[:], mkq[:], start=False, stop=True)
                else:
                    for a in range(2):
                        j = 2 * (n - 2) + a
                        last = mm(pb[:, a * 512:(a + 1) * 512], hk_[:, T + j * P:T + (j + 1) * P],
                                  hq_[:, T:2 * T], start=True, stop=True)
                last.then_inc(s_st2, 1)

            def weigh(b, h, n):
                g = h * NE_ + n
                if g == 0:
                    pe.wait_ge(s_vone, b + 1)
                    pe.wait_ge(s_vl, cur(b, 3, 3))
                if n == 0:
                    pe.wait_ge(s_keep, cur(b, XH, h))
                pe.wait_ge(s_rest_d, cur(b, XH * NE_, g + 1))
                if POOL_COLS[n]:
                    pe.wait_ge(s_rest_p, cur(b, N_POOL, POOL_AT[h, n]))
                for part, e in enumerate((high[:, g % RING_E, :], low[:, g % RING_E, :])):
                    if n < 2:
                        for j, col in SELF_EXP[n]:
                            last = mm(ps[3][0:VW, j * P:T], va[:, j, h, :], e[:, col:col + T - j * P],
                                      start=part == 0 and n == 0 and j == 0, stop=part == 1 and n == 1)
                    else:
                        for a in range(2):
                            j = 2 * (n - 2) + a
                            last = mm(ps[3][0:VW, 512:1024], vca[:, j, h, :], e[:, a * 512:(a + 1) * 512],
                                      start=part == 0 and j == 0, stop=part == 1 and j == NTC - 1)
                last.then_inc(s_av, 1)

            def turn_results(b, g):
                pb = ring_bank(b, ("turn", g, 0))
                pe.wait_ge(s_keep, cur(b, XH, (g + 1) * HG))
                for w in range(2):
                    for i in range(NT):
                        col = (w * NT + i) * HG * RW
                        last = mm(pb[:, col:col + P], ykeep[:, w, i * P:(i + 1) * P], fold[:], start=True, stop=True)
                last.then_inc(s_sc, 1)

            def qfeat(i):
                def fill(t):
                    for a in range(2):
                        j = 2 * i + a
                        for c in range(KC):
                            last = mm(t[:, a * T:(a + 1) * T], wqf[:, c, j * P:(j + 1) * P],
                                      xT_s[:, c, :], start=c == 0, stop=c == KC - 1)
                    return last
                return fill

            def kfeat(i):
                def fill(t):
                    for half in range(2):
                        for c in range(KC):
                            last = mm(t[:, half * 512:(half + 1) * 512], xT_s[:, c, i * P:(i + 1) * P],
                                      wkf[:, c, half * 512:(half + 1) * 512], start=c == 0, stop=c == KC - 1)
                    return last
                return fill

            pe.wait_ge(s_x, 48)
            pe.wait_ge(s_setup, 3)
            for i in range(NQF):
                qfeat(i)(ps[JN[f"qf{i}"] % 4]).then_inc(s_tile, 1)
            assert (JN["kf0"] - JN["qf0"]) % 4 == 0 and (JN["kf1"] - JN["qf2"]) % 4 == 0
            pe.wait_ge(s_act, ACT_AT["qf0"])
            kfeat(0)(ps[JN["kf0"] % 4]).then_inc(s_tile, 1)
            pe.wait_ge(s_tile, JN["kf0"] + 1)
            pe.sem_inc(s_tile, 1)
            pe.wait_ge(s_act, ACT_AT["qf3"])
            kfeat(1)(ps[JN["kf1"] % 4]).then_inc(s_tile, 1)
            pe.wait_ge(s_tile, JN["kf1"] + 1)
            pe.sem_inc(s_tile, 1)
            pe.wait_ge(s_const, 16 * LOADS)
            pe.wait_ge(s_setup, 4)
            pe.wait_ge(s_pset, 2)
            with pe.Fori(0, nb) as b:
                for i in range(2, NT):
                    job(b, f"kf{i}", kfeat(i))

                def gprod(m):
                    def fill(t):
                        for half in range(2):
                            for i in range(NT):
                                last = mm(t[:, half * 512:(half + 1) * 512], x_s[:, i, m * P:(m + 1) * P],
                                          phik[:, i, half * 512:(half + 1) * 512], start=i == 0, stop=i == NT - 1)
                        return last
                    return fill

                job(b, "g0", gprod(0), dve="kf3")

                def fsum(t):
                    for j in range(NPAIR):
                        last = mm(t[:, j:j + 1], psum01[:, j * P:(j + 1) * P], onescol[:], start=True, stop=True)
                    return last

                pe.wait_ge(s_psum, cur(b, 3, 3))
                job(b, "ksum", fsum)

                def normprod(t):
                    for j in range(NPAIR):
                        last = mm(t[0:LH, 0:T], ksbd[:, j * LH:(j + 1) * LH], phiq[:, j, :],
                                  start=j == 0, stop=j == NPAIR - 1)
                    return last

                pe.wait_ge(s_act, cur(b, N_ACT, ACT_AT["qf3"] - N_ACT))
                job(b, "norm", normprod, dve="ksum")
                job(b, "g1", gprod(1))

                def kvprod(t):
                    for j in range(NPAIR):
                        for c in range(KC):
                            last = mm(t[:, j * P:(j + 1) * P], wvl[:, c, j * P:(j + 1) * P],
                                      g_s[:, c, j * P:(j + 1) * P], start=c == 0, stop=c == KC - 1)
                    return last

                def kcprod(m):
                    def fill(t):
                        for half in range(2):
                            last = mm(t[:, half * 512:(half + 1) * 512], wck_s[:, m * P:(m + 1) * P],
                                      ctxT_s[:, half * 512:(half + 1) * 512], start=True, stop=True)
                        return last
                    return fill

                job(b, "kc0", kcprod(0))
                job(b, "kv", kvprod, act="g0", dve="g1")

                def mprod(k):
                    def fill(t):
                        for a in range(4):
                            j = 4 * k + a
                            last = mm(t[:, a * C:(a + 1) * C], kvbd[:, j, :], wo[:, j, :], start=True, stop=True)
                        return last
                    return fill

                def spread(k):
                    def fill(t):
                        for a in range(2):
                            last = mm(t[:, a * T:(a + 1) * T], sel[:, 2 * k + a, :], rT[:], start=True, stop=True)
                        return last
                    return fill

                job(b, "bc0", spread(0), dve="norm")
                job(b, "m0", mprod(0), act="kv")
                job(b, "bc1", spread(1))
                job(b, "m1", mprod(1))
                job(b, "bc2", spread(2))
                job(b, "bc3", spread(3))

                def attn(half):
                    def fill(t):
                        for a in range(2):
                            i = 2 * half + a
                            for j in range(NPAIR):
                                last = mm(t[:, a * C:(a + 1) * C], phiq[:, j, i * P:(i + 1) * P], m_s[:, j, :],
                                          start=j == 0, stop=j == NPAIR - 1)
                        return last
                    return fill

                job(b, "attn0", attn(0), act="m1", dve="bc3")
                job(b, "attn1", attn(1))

                def vcprod(k):
                    def fill(t):
                        for a in range(4):
                            last = mm(t[:, a * C:(a + 1) * C], ctxT_s[:, (4 * k + a) * P:(4 * k + a + 1) * P],
                                      wcv_s[:], start=True, stop=True)
                        return last
                    return fill

                job(b, "vc0", vcprod(0))
                job(b, "vc1", vcprod(1))
                job(b, "kc1", kcprod(1))

                def turn(src):
                    def fill(t):
                        for c in range(KC):
                            for i in range(NT):
                                last = tr(t[:, c * T + i * P:c * T + (i + 1) * P], src[:, i, c * P:(c + 1) * P], ident[:])
                        return last
                    return fill

                pe.wait_ge(s_ln, cur(b, 2, 1))
                job(b, "x1T", turn(x1))
                def proj(w, m):
                    def fill(t):
                        for c in range(KC):
                            last = mm(t[:, 0:T], w[:, c, m * P:(m + 1) * P], x1T[:, c, :],
                                      start=c == 0, stop=c == KC - 1)
                        return last
                    return fill

                def rows(src, w, tiles=range(NT)):
                    def fill(t):
                        for n, i in enumerate(tiles):
                            for c in range(KC):
                                last = mm(t[:, n * C:(n + 1) * C], src[:, c, i * P:(i + 1) * P], w[:, c, :],
                                          start=c == 0, stop=c == KC - 1)
                        return last
                    return fill

                for m in range(2):
                    job(b, f"k{m}", proj(wk_s, m), act="x1T")
                    job(b, f"q{m}", proj(wq_s, m))
                    job(b, f"qc{m}", proj(wcq_s, m))
                job(b, "v", rows(x1T, wv_s))

                pe.wait_ge(s_dve, cur(b, N_DVE, DVE_AT["v"]))

                for kind, h, n in ORDER:
                    if kind == "bank":
                        score_bank(b, h, n)
                    elif kind == "maxima":
                        maxima_row(b, h)
                    elif kind == "scores":
                        exp_scores(b, h, n)
                    elif kind == "weigh":
                        weigh(b, h, n)
                    elif kind == "turn":
                        turn_results(b, h)

                pe.wait_ge(s_ys, cur(b, XH // HG, XH // HG))
                job(b, "yT", turn(y_s))
                job(b, "proj0", rows(yT_s, wp_s, (0, 1)), act="yT")
                job(b, "proj1", rows(yT_s, wp_s, (2, 3)))
                pe.wait_ge(s_x, (b + 2) * 48)
                for i in range(NQF):
                    job(b, f"qf{i}", qfeat(i))
                job(b, "kf0", kfeat(0))
                pe.wait_ge(s_ln, cur(b, 2, 2))
                job(b, "x2T", turn(x1))
                job(b, "kf1", kfeat(1))
                def gate(t):
                    for i in range(NT):
                        for c in range(KC):
                            last = mm(t[:, i * E:(i + 1) * E], x1T[:, c, i * P:(i + 1) * P], gw_s[:, c, :],
                                      start=c == 0, stop=c == KC - 1)
                    return last

                job(b, "gate", gate, act="x2T")

        @block.scalar
        def _(act):
            act.sem_inc(s_act, ACT_AT["qf0"] - 1)
            act.sem_inc(s_mrow, XH)
            act.sem_inc(s_exp, XH * NE_)
            act.sem_inc(s_keep, XH)
            act.sem_inc(s_vh, 3)
            act.sem_inc(s_rnd["A"], N_ROUND["A"])

            def relu_q(i, t):
                nc.scalar.activation(phiq[:, 2 * i:2 * i + 2, :], t[:].rearrange("p (a t) -> p a t", a=2),
                                     ACT.Relu).then_inc(s_act, 1)

            for i in range(NQF):
                act.wait_ge(s_tile, JN[f"qf{i}"] + 1)
                relu_q(i, ps[JN[f"qf{i}"] % 4])
            act.wait_ge(s_act, ACT_AT["qf3"])
            act.sem_inc(s_act, N_ACT - ACT_AT["qf3"])
            with act.Fori(0, nb) as b:
                def full(name):
                    act.wait_ge(s_tile, cur(b, NJ, JN[name] + 1))
                    return ps[JN[name] % 4]

                t = full("g0")
                nc.scalar.activation(g_s[:, 0, :], t[:], ACT.Copy).then_inc(s_act, 1)
                def high_part(name, bias_n, m, w):
                    stg, at, before = STAGED[name]
                    t = full(name)
                    for n in before:
                        act.wait_ge(s_st[n], cur(b, 16, 0 if n in LAST_STAGED else 16))
                    nc.scalar.activation(stage[:, stg, 0, at:at + w], t[:, 0:w], ACT.Identity,
                                         bias=bias_c[:, bias_n, m:m + 1]).then_inc(s_act, 1)

                high_part("kc0", 1, 0, TC_)
                t = full("kv")
                act.wait_ge(s_setup, 4)
                tv = t[:].rearrange("p (j r) -> p j r", j=NPAIR)
                nc.scalar.activation(kvbd[0:LD, :, 0:LD], tv[0:LD, :, 0:LD], ACT.Copy)
                nc.scalar.activation(kvbd[LD:P, :, LD:P], tv[LD:P, :, LD:P], ACT.Copy).then_inc(s_act, 1)
                for k in range(2):
                    t = full(f"m{k}")
                    nc.scalar.activation(m_s[:, 4 * k:4 * k + 4, :], t[:].rearrange("p (a c) -> p a c", a=4),
                                         ACT.Copy).then_inc(s_act, 1)

                def high_values(n, name, dst):
                    act.wait_ge(s_dve, cur(b, N_DVE, DVE_AT[name]))
                    nc.scalar.activation(dst[:, :, :, 0:XD], u_s[:, U_AT[n]], ACT.Copy).then_inc(s_vh, 1)

                high_part("kc1", 1, 1, TC_)
                t = full("x1T")
                nc.scalar.activation(x1T[:], t[:].rearrange("p (c t) -> p c t", c=KC), ACT.Copy).then_inc(s_act, 1)
                for m in range(2):
                    high_part(f"k{m}", 0, m, T)
                    high_part(f"q{m}", 2, m, T)
                    high_part(f"qc{m}", 3, m, T)
                for k in range(2):
                    high_values(k, f"vc{k}", vca[:, 4 * k:4 * k + 4])
                nc.scalar.activation(vca[:, :, :, XD], ones_s[:].rearrange("p (n h) -> p n h", n=NTC),
                                     ACT.Copy).then_inc(s_vone, 1)
                high_values(2, "v", va)

                def maxima(h):
                    n = RING_AT["maxima", h, 0]
                    act.wait_ge(s_sc, cur(b, NRING, n + 1))
                    pb = ps[2][:, (n % 2) * 512:(n % 2) * 512 + 512]
                    nc.scalar.activation(hq[h % HS][MROW:MROW + 1, 0:T], pb[64:65, :], ACT.Copy)
                    nc.scalar.activation(hq[h % HS][MROW:MROW + 1, T:2 * T], pb[96:97, :],
                                         ACT.Copy).then_inc(s_mrow, 1)

                def exp_step(h, n):
                    g, w = h * NE_ + n, E_COLS[n]
                    act.wait_ge(s_st2, cur(b, XH * NE_, g + 1))
                    act.wait_ge(s_av, cur(b, XH * NE_, g + 1 - RING_E))
                    if g in U_AT:
                        act.wait_ge(s_vl, cur(b, 3, U_AT.index(g) + 1))
                    nc.scalar.activation(exps[:, g % RING_E, 0:w], ps[g % 2][:, 0:w], ACT.Exp,
                                         scale=SCALE).then_inc(s_exp, 1)

                def round_exps(h, n):
                    g, w = h * NE_ + n, E_COLS[n]
                    act.wait_ge(s_exp, cur(b, XH * NE_, g + 1))
                    nc.scalar.activation(high[:, g % RING_E, 0:w], exps[:, g % RING_E, 0:w],
                                         ACT.Copy).then_inc(s_rnd["A"], 1)

                def keep(h):
                    act.wait_ge(s_av, cur(b, XH * NE_, (h + 1) * NE_))
                    if h >= HG:
                        n = RING_AT["turn", h // HG - 1, 0]
                        act.wait_ge(s_sc, cur(b, NRING, n + 1))
                    q = h % HG * HP
                    nc.scalar.activation(ykeep[q:q + VW, :, :], ps[3][0:VW, :].rearrange("p (w t) -> p w t", w=2),
                                         ACT.Copy).then_inc(s_keep, 1)

                for kind, h, n in ORDER:
                    if kind == "maxima":
                        maxima(h)
                    elif kind == "scores":
                        exp_step(h, n)
                    elif kind == "round" and ROUND_BY[n] == "A":
                        round_exps(h, n)
                    elif kind == "keep":
                        keep(h)
                t = full("yT")
                nc.scalar.activation(yT_s, t[:].rearrange("p (c t) -> p c t", c=KC), ACT.Copy).then_inc(s_act, 1)
                for i in range(NQF):
                    relu_q(i, full(f"qf{i}"))
                t = full("x2T")
                nc.scalar.activation(x1T[:], t[:].rearrange("p (c t) -> p c t", c=KC), ACT.Copy).then_inc(s_act, 1)

        @block.vector
        def _(dve):
            v = nc.vector
            steps = [0]
            NSTEP = 48

            dve.sem_inc(s_dve, DVE_AT["kf0"] - 1)
            dve.sem_inc(s_ln, 2)
            dve.sem_inc(s_red, NRED)
            dve.sem_inc(s_max, XH)
            dve.sem_inc(s_ys, XH // HG)
            dve.sem_inc(s_rest_d, XH * NE_)
            dve.sem_inc(s_rnd["D"], N_ROUND["D"])

            v.memset(rfbd, 0.0).then_inc(s_zrf, 1)
            for t in (kvbd[:], blank):
                v.memset(t, 0.0)
            v.memset(mpad[:], 0.0)
            v.memset(ksbd[:], 0.0)
            v.memset(onescol[:], 1.0)
            v.memset(zero1[:], 0.0)
            v.memset(onehot[:], 0.0)
            v.memset(ones_s[:], 1.0)
            v.memset(va[:].bitcast(F32), 1.0)
            v.memset(rT[:].bitcast(F32), 0.0)
            for e in range(E):
                v.memset(rank8[:, e:e + 1], float(E - e))
            v.memset(ykeep[:], 0.0).then_inc(s_setup, 1)
            dve.wait_ge(s_setup, 1)
            for n in range(BLANKS):
                last = v.memset(blank[:, n * CR + C:(n + 1) * CR], NOBODY)
            last.then_inc(s_setup, 1)
            for n, w in enumerate((wqf, wkf)):
                for c in range(KC):
                    dve.wait_ge(s_wprod, 2 * n + c + 1)
                    last = v.tensor_copy(w[:, c, :], ps[2 * n + c][:])
            last.then_inc(s_setup, 1)
            dve.wait_ge(s_const, 16 * LOADS)
            v.tensor_copy(identb[:], ident[:])
            v.tensor_copy(mqk[:], cstage[:, 0:P])
            v.tensor_copy(mkq[:], cstage[:, P:2 * P])
            dve.wait_ge(s_sel, 16)
            v.tensor_copy(sel[:], sel_f).then_inc(s_setup, 1)

            def relu_k(i, t):
                v.tensor_scalar(phik[:, i, :], t[:], 0.0, None, ALU.max).then_inc(s_dve, 1)

            for i in range(2):
                dve.wait_ge(s_tile, JN[f"kf{i}"] + 1)
                relu_k(i, ps[JN[f"kf{i}"] % 4])
            dve.wait_ge(s_dve, DVE_AT["kf1"])
            dve.sem_inc(s_dve, N_DVE - DVE_AT["kf1"])
            with dve.Fori(0, nb) as b:
                def step(ins):
                    steps[0] += 1
                    ins.then_inc(s_dstep, 1)
                    dve.wait_ge(s_dstep, b * NSTEP + steps[0])

                def full(name):
                    dve.wait_ge(s_tile, cur(b, NJ, JN[name] + 1))
                    return ps[JN[name] % 4]

                for i in range(2, NT):
                    relu_k(i, full(f"kf{i}"))
                t = full("ksum")
                W = LH + 2
                v.tensor_copy(ksbd[0:LD, 0:7 * W + 1:W], t[0:LD, 0:NPAIR])
                v.tensor_copy(ksbd[LD:P, 1:7 * W + 2:W], t[LD:P, 0:NPAIR]).then_inc(s_dve, 1)
                t = full("norm")
                step(v.tensor_scalar(den[:], t[0:LH, 0:T], STAB, None, ALU.add))
                step(v.reciprocal(den[:], den[:]))
                step(v.tensor_copy(rT[0:LH, :], den[:]))
                v.tensor_tensor(rT[2 * LH:3 * LH, :], den[:], rT[0:LH, :].bitcast(F32), ALU.subtract).then_inc(s_dve, 1)
                t = full("g1")
                v.tensor_copy(g_s[:, 1, :], t[:]).then_inc(s_dve, 1)

                def low_part(name, bias_n, m, w):
                    stg, at, _ = STAGED[name]
                    t = full(name)
                    dve.wait_ge(s_act, cur(b, N_ACT, ACT_AT[name]))
                    for c in range(0, w, 512):
                        last = v.scalar_tensor_tensor(stage[:, stg, 1, at + c:at + c + 512], t[:, c:c + 512],
                                                      bias_c[:, bias_n, m:m + 1],
                                                      stage[:, stg, 0, at + c:at + c + 512].bitcast(F32), ALU.add, ALU.subtract)
                    last.then_inc(s_dve, 1)

                low_part("kc0", 1, 0, TC_)
                for k in range(4):
                    t = full(f"bc{k}")
                    v.tensor_tensor(phiq[:, 2 * k:2 * k + 2, :], phiq[:, 2 * k:2 * k + 2, :],
                                    t[:].rearrange("p (a t) -> p a t", a=2), ALU.mult).then_inc(s_dve, 1)

                def residual(name, half):
                    t = full(name)
                    i = slice(2 * half, 2 * half + 2)
                    v.tensor_tensor(r_s[:, i, :], t[:, 0:2 * C].rearrange("p (i c) -> p i c", i=2), xb[:, i, :],
                                    ALU.add).then_inc(s_dve, 1)
                    dve.wait_ge(s_dve, cur(b, N_DVE, DVE_AT[name]))
                    for i in range(2 * half, 2 * half + 2):
                        last = v.bn_stats(stats[:, i, :], r_s[:, i, :])
                    step(last)

                def layer_norm():
                    layer_norm_steps(v, step, r_s, x1, stats, mv, nwt, nwi, s_ln)

                dve.wait_ge(s_xb, cur(b, 2, 1))
                residual("attn0", 0)
                residual("attn1", 1)
                dve.wait_ge(s_x2, cur(b, 16, 0))
                dve.wait_ge(s_blank, 16 * NZ)
                layer_norm()

                for k in range(2):
                    t = full(f"vc{k}")
                    for a in range(4):
                        last = v.tensor_tensor(u_s[:, k, a],
                                               t[:, a * C:(a + 1) * C].rearrange("p (h d) -> p h d", h=XH),
                                               bcv_bc[:].rearrange("p (h d) -> p h d", h=XH), ALU.add)
                    last.then_inc(s_dve, 1)

                low_part("kc1", 1, 1, TC_)
                for m in range(2):
                    low_part(f"k{m}", 0, m, T)
                    low_part(f"q{m}", 2, m, T)
                    low_part(f"qc{m}", 3, m, T)
                t = full("v")
                for i in range(NT):
                    last = v.tensor_tensor(u_s[:, U_AT[2], i],
                                           t[:, i * C:(i + 1) * C].rearrange("p (h d) -> p h d", h=XH),
                                           bv_bc[:].rearrange("p (h d) -> p h d", h=XH), ALU.add)
                last.then_inc(s_dve, 1)

                def reduce(h, n):
                    s = RING_AT["bank", h, n]
                    if n == 0:
                        dve.wait_ge(s_max, cur(b, XH, h))
                    dve.wait_ge(s_sc, cur(b, NRING, s + 1))
                    pb = ps[2][:, (s % 2) * 512:(s % 2) * 512 + 512]
                    if n >= NSX:
                        for i, col in SELF_MAX[n - NSX]:
                            last = v.reduce_max(mpad[:, i, 64:65], pb[:, col:col + (i + 1) * P], AX.X)
                        last.then_inc(s_red, 1)
                    else:
                        i, half = n // 2, n % 2
                        v.reduce_max(cmax[:, i, half:half + 1], pb, AX.X).then_inc(s_red, 1)
                    if n == NSX - 1:
                        dve.wait_ge(s_red, cur(b, NRED, RED_AT["bank", h, n]))
                        v.tensor_tensor(mpad[:, :, 96], cmax[:, :, 0], cmax[:, :, 1], ALU.max).then_inc(s_max, 1)

                def results(g):
                    s = RING_AT["turn", g, 0]
                    dve.wait_ge(s_sc, cur(b, NRING, s + 1))
                    pb = ps[2][:, (s % 2) * 512:(s % 2) * 512 + 2 * NT * HG * RW]
                    tv = pb.rearrange("p (i h d) -> p i h d", i=2 * NT, h=HG)
                    step(v.reciprocal(rec[:], tv[:, :, :, XD]))
                    v.tensor_tensor(yn[:], tv[:, :, :, 0:XD],
                                    rec[:].unsqueeze(3).broadcast_to([P, 2 * NT, HG, XD]), ALU.mult).then_inc(s_red, 1)
                    dve.wait_ge(s_red, cur(b, NRED, RED_AT["turn", g, 0]))
                    v.tensor_tensor(y_s[:, :, g * HG * XD:(g + 1) * HG * XD].rearrange("p i (h d) -> p i h d", h=HG),
                                    yn[:, 0:NT], yn[:, NT:2 * NT], ALU.add).then_inc(s_ys, 1)
                    dve.wait_ge(s_ys, cur(b, XH // HG, g + 1))

                def round_exps(h, n):
                    g, w = h * NE_ + n, E_COLS[n]
                    dve.wait_ge(s_exp, cur(b, XH * NE_, g + 1))
                    v.tensor_copy(high[:, g % RING_E, 0:w], exps[:, g % RING_E, 0:w]).then_inc(s_rnd["D"], 1)

                def rest_exps(h, n):
                    g, who, c0, c1 = h * NE_ + n, ROUND_BY[n], POOL_COLS[n], E_COLS[n]
                    dve.wait_ge(s_rnd[who], cur(b, N_ROUND[who], ROUND_AT[who][h, n]))
                    v.tensor_tensor(low[:, g % RING_E, c0:c1], exps[:, g % RING_E, c0:c1],
                                    high[:, g % RING_E, c0:c1].bitcast(F32), ALU.subtract).then_inc(s_rest_d, 1)

                for kind, h, n in ORDER:
                    if kind == "bank":
                        reduce(h, n)
                    elif kind == "turn":
                        results(h)
                    elif kind == "round" and ROUND_BY[n] == "D":
                        round_exps(h, n)
                    elif kind == "rest":
                        rest_exps(h, n)

                dve.wait_ge(s_xb, cur(b, 2, 2))
                residual("proj0", 0)
                residual("proj1", 1)
                layer_norm()
                for n in LAST_STAGED:
                    dve.wait_ge(s_st[n], cur(b, 16, 16))
                for i in range(2):
                    relu_k(i, full(f"kf{i}"))
                t = full("gate")
                step(v.tensor_tensor(lg[:], t[:, 0:NT * E].rearrange("p (i e) -> p i e", i=NT),
                                     gb_bc[:].unsqueeze(1).broadcast_to([P, NT, E]), ALU.add))
                step(v.reduce_max(lmax[:], lg[:], AX.X))
                step(v.tensor_tensor(lw[:], lg[:], lmax[:].unsqueeze(2).broadcast_to([P, NT, E]), ALU.is_ge))
                step(v.tensor_tensor(lw[:], lw[:], rank8[:].unsqueeze(1).broadcast_to([P, NT, E]), ALU.mult))
                step(v.reduce_max(lmax[:], lw[:], AX.X))
                v.tensor_tensor(onehot[:, bass.ds(b * NT, NT), :], lw[:],
                                lmax[:].unsqueeze(2).broadcast_to([P, NT, E]), ALU.is_equal).then_inc(s_dve, 1)
            assert steps[0] == NSTEP, steps[0]


def layer_norm_steps(v, step, src, dst, stats, mv, nwt, nwi, done, n=NT):
    even, odd = stats[:, :, 1:3], stats[:, :, 4:6]
    v.tensor_tensor(mv[:, 0:2, :].rearrange("p w i -> p i w"), even, odd, ALU.add)
    step(v.tensor_tensor(mv[:, 2, :], stats[:, :, 1], stats[:, :, 4], ALU.subtract))
    v.tensor_scalar(mv[:, 0, :], mv[:, 0, :], 0.5, None, ALU.mult)
    v.tensor_scalar(mv[:, 1, :], mv[:, 1, :], 1.0 / C, LN_EPS, ALU.mult, ALU.add)
    step(v.scalar_tensor_tensor(mv[:, 3, :], mv[:, 2, :], 0.25, mv[:, 2, :], ALU.mult, ALU.mult))
    ve = nwt[:, 0, :]
    step(v.tensor_tensor(ve, mv[:, 1, :], mv[:, 3, :], ALU.add))
    step(v.tensor_scalar(nwi[:, 0, :], ve.bitcast(I32), 1, None, ALU.logical_shift_right))
    step(v.tensor_scalar(nwi[:, 1, :], nwi[:, 0, :], -1.0, float(0x5F3759DF), ALU.mult, ALU.add))
    y0 = nwi[:, 1, :].bitcast(F32)
    for k in range(3):
        a, t2, y1 = nwt[:, 1, :], nwt[:, 2, :], nwt[:, 3 + k % 2, :]
        step(v.scalar_tensor_tensor(a, y0, -0.5, y0, ALU.mult, ALU.mult))
        step(v.tensor_tensor(t2, a, ve, ALU.mult))
        step(v.scalar_tensor_tensor(y1, t2, 1.5, y0, ALU.add, ALU.mult))
        y0 = y1
    for i in range(n):
        last = v.tensor_scalar(dst[:, i, :], src[:, i, :], mv[:, 0, i:i + 1], y0[:, i:i + 1],
                               ALU.subtract, ALU.mult)
    last.then_inc(done, 1)


def experts(nc, onehot, x2d, xs, w1T, b1p, w2T, b2, ident_d, tri_d, iota_d, number_d, out):
    ctx = ExitStack()
    with ctx:
        def sb(name, shape, dt=F32):
            return ctx.enter_context(nc.sbuf_tensor(name, shape, dt))

        def sem(name):
            return ctx.enter_context(nc.semaphore(name))

        J = B * NT
        ident = sb("e_ident", [P, P])
        tri = sb("tri", [P, P])
        ones = sb("ones", [P, P])
        iota = sb("iota", [P, J])
        number = sb("number", [P, J])
        x2s = sb("x2s", [P, J, CR])
        within = sb("within", [P, J, E])
        cnt = sb("cnt", [P, J, E])
        cum = [sb(f"cum{i}", [P, J, E]) for i in range(2)]
        big = sb("big", [P, E, MAXT])
        mt = sb("mt", [P, MAXT])
        tiles = sb("tiles", [P, E])
        st = [sb(f"st{i}", [P, E]) for i in range(2)]
        eidf = sb("eidf", [P, NTILE])
        eidc = sb("eidc", [P, NTILE, E])
        eid = sb("eid", [P, NTILE], I32)
        slotf = sb("slotf", [P, J])
        slot = sb("slot", [P, J], U32)
        w1s = [sb(f"w1s{i}", [P, KC, HID]) for i in range(2)]
        w2s = [sb(f"w2s{i}", [P, NHC, C]) for i in range(2)]
        b1s = [sb(f"b1s{i}", [P, NHC]) for i in range(2)]
        b2s = [sb(f"b2s{i}", [P, C]) for i in range(2)]
        xin = [sb(f"xin{i}", [P, TH, CR]) for i in range(2)]
        home = [sb(f"home{i}", [P, TH], U32) for i in range(2)]
        base = [sb(f"base{i}", [P, TH, C]) for i in range(2)]
        xinT = [sb(f"xinT{i}", [P, KC, TILE]) for i in range(2)]
        hT = [sb(f"hT{i}", [P, NHC, TILE]) for i in range(2)]
        yr = sb("yr", [P, TH, C])
        yo = [sb(f"yo{i}", [P, TH, C]) for i in range(2)]
        stats = sb("e_stats", [P, TH, 6])
        mv = sb("e_mv", [P, 4, TH])
        nwt = sb("e_nwt", [P, 5, TH])
        nwi = sb("e_nwi", [P, 2, TH], I32)
        px = ctx.enter_context(nc.psum_tensor("px", [P, 512], F32))
        ph = [ctx.enter_context(nc.psum_tensor(f"ph{i}", [P, 512], F32)) for i in range(2)]
        py = [ctx.enter_context(nc.psum_tensor(f"py{i}", [P, TH, 512], F32)) for i in range(2)]
        pr = py[0]

        s_c = sem("e_const")
        s_pace = sem("e_pace")
        s_past = sem("e_past")
        s_x2 = sem("e_x2")
        s_one = sem("e_ones")
        s_cnt = sem("e_cnt")
        s_step = sem("e_step")
        s_route = sem("e_route")
        s_xs = sem("e_xs")
        s_w = [sem(f"e_w{i}") for i in range(2)]
        s_in = [sem(f"e_in{i}") for i in range(2)]
        s_xt = sem("e_xt")
        s_xc = sem("e_xc")
        s_base = sem("e_base")
        s_h = sem("e_h")
        s_ha = sem("e_ha")
        s_y = sem("e_y")
        s_yr = sem("e_yr")
        s_ln = sem("e_ln")
        s_out = [sem(f"e_out{i}") for i in range(2)]
        s_sent = sem("e_sent")

        block = ctx.enter_context(nc.Block())
        NH2 = NHC // 2
        W_DMA, IN_DMA = 3 * 16, 2 * 16

        @block.sync
        def _(sp):
            for dst, src in ((ident, ident_d), (tri, tri_d), (iota, iota_d), (number, number_d)):
                sp.dma_start(dst[:], src).then_inc(s_c, 16)
            for n in range(B):
                sp.dma_start(x2s[:, n * NT:(n + 1) * NT, 0:C],
                             x2d[n * T:(n + 1) * T].rearrange("(n p) c -> p n c", p=P)).then_inc(s_x2, 16)
            sp.wait_ge(s_route, 2)

            def load_weights(t, i):
                e = sp.value_load(eid[0:1, bass.ds(t, 1)], min_val=0, max_val=E - 1)
                sp.dma_start(w1s[i][:], w1T[bass.ds(e, 1)].rearrange("a (k p) h -> p (a k) h", p=P)).then_inc(s_w[i], 16)
                sp.dma_start(w2s[i][:], w2T[bass.ds(e, 1)].rearrange("a (k p) c -> p (a k) c", p=P)).then_inc(s_w[i], 16)
                sp.dma_start(b1s[i][:], b1p[bass.ds(e, 1)].rearrange("a p k -> (a p) k")).then_inc(s_w[i], 16)

            def load_rows(t, i):
                e = sp.value_load(eid[0:1, bass.ds(t, 1)], min_val=0, max_val=E - 1)
                sp.dma_start(b2s[i][:], b2[bass.ds(e, 1)].broadcast_to([P, C])).then_inc(s_in[i], 16)
                sp.dma_start(xin[i][:], xs[bass.ds(t, 1)].rearrange("a (n p) c -> p (a n) c", p=P)).then_inc(s_in[i], 16)

            load_weights(0, 0)
            sp.wait_ge(s_xs, 16 * J)
            load_rows(0, 0)
            with sp.Fori(0, NTILE // 2) as tt:
                for i in range(2):
                    following = tt * 2 + (i + 1)
                    sp.wait_ge(s_base, tt * 2 + (i + 1))
                    sp.sem_inc(s_pace, 1)
                    sp.wait_ge(s_xt, tt * 2 + (i + 1))
                    sp.sem_inc(s_pace, 1)
                    load_rows(following, 1 - i)
                    sp.wait_ge(s_y, tt * 2 + (i + 1))
                    sp.sem_inc(s_pace, 1)
                    load_weights(following, 1 - i)
            for i in range(2):
                sp.wait_ge(s_w[i], (NTILE // 2 + (i == 0)) * W_DMA)
                sp.wait_ge(s_in[i], (NTILE // 2 + (i == 0)) * IN_DMA)

        @block.gpsimd
        def _(pool):
            pool.wait_ge(s_x2, 16 * B)
            pool.wait_ge(s_route, 1)
            xs_rows = xs.rearrange("t r c -> (t r) c")
            for j in range(J):
                nc.gpsimd.indirect_dma_start(
                    xs_rows, bass.IndirectOffsetOnAxis(slot[:, j:j + 1], 0), x2s[:, j, :], None,
                    bounds_check=NTILE * TILE - 1).then_inc(s_xs, 16)
            pool.sem_inc(s_base, 1)
            pool.sem_inc(s_sent, 2)
            out_rows = out.rearrange("b t c -> (b t) c")
            def tile(tt, i):
                pool.wait_ge(s_in[i], (tt + 1) * IN_DMA)
                pool.wait_ge(s_yr, tt * 2 + (i + 1))
                nc.gpsimd.tensor_tensor(base[i][:], xin[i][:, :, 0:C],
                                        b2s[i][:].unsqueeze(1).broadcast_to([P, TH, C]), ALU.add)
                nc.gpsimd.tensor_copy(home[i][:], xin[i][:, :, C]).then_inc(s_base, 1)
                pool.wait_ge(s_base, tt * 2 + (i + 2))
                pool.sem_inc(s_past, 1)
                pool.wait_ge(s_ln, tt * 2 + (i + 1))
                pool.sem_inc(s_past, 1)
                for n in range(TH):
                    nc.gpsimd.indirect_dma_start(
                        out_rows, bass.IndirectOffsetOnAxis(home[i][:, n:n + 1], 0), yo[i][:, n, :], None,
                        bounds_check=B * T - 1, oob_is_err=False).then_inc(s_out[i], 16)
                pool.wait_ge(s_out[i], (tt + 1) * (TH * 16))
                pool.sem_inc(s_sent, 1)

            with pool.Fori(0, NTILE // 2) as tt:
                for i in range(2):
                    tile(tt, i)
            tile(NTILE // 2, 0)
            for i in range(2):
                pool.wait_ge(s_out[i], (NTILE // 2 + (i == 0)) * (TH * 16))

        @block.tensor
        def _(pe):
            mm, tr = nc.tensor.matmul, nc.tensor.transpose
            oh = onehot[:].rearrange("p n e -> p (n e)")
            pe.wait_ge(s_c, 64)
            pe.wait_ge(s_one, 1)
            mm(pr[:, 0, 0:J * E], tri[:], oh, start=True, stop=True)
            mm(pr[:, 1, 0:J * E], ones[:], oh, start=True, stop=True).then_inc(s_cnt, 1)
            pe.sem_inc(s_h, 2 * NH2)
            pe.sem_inc(s_y, 1)

            def turn(i):
                for k in range(KC):
                    for n in range(TH):
                        last = tr(px[:, k * TILE + n * P:k * TILE + (n + 1) * P], xin[i][:, n, k * P:(k + 1) * P], ident[:])
                last.then_inc(s_xt, 1)

            pe.wait_ge(s_in[0], IN_DMA)
            turn(0)
            def tile(tt, i, more=True):
                pe.wait_ge(s_w[i], (tt + 1) * W_DMA)
                pe.wait_ge(s_xc, tt * 2 + (i + 1))
                for c in range(NH2):
                    g = i * NH2 + c
                    pe.wait_ge(s_ha, tt * (2 * NH2) + (2 * NH2 + g - 1))
                    for a in range(2):
                        for k in range(KC):
                            last = mm(ph[g % 2][:, a * TILE:(a + 1) * TILE],
                                      w1s[i][:, k, (2 * c + a) * P:(2 * c + a + 1) * P], xinT[i][:, k, :],
                                      start=k == 0, stop=k == KC - 1)
                    last.then_inc(s_h, 1)
                if more:
                    pe.wait_ge(s_in[1 - i], tt * IN_DMA + (i + 1) * IN_DMA)
                    turn(1 - i)
                pe.wait_ge(s_yr, tt * 2 + (i + 1))
                for c in range(NHC):
                    if c % 2 == 0:
                        pe.wait_ge(s_ha, tt * (2 * NH2) + (2 * NH2 + i * NH2 + c // 2 + 1))
                    for n in range(TH):
                        last = mm(py[i][:, n, 0:C], hT[i][:, c, n * P:(n + 1) * P], w2s[i][:, c, :],
                                  start=c == 0, stop=c == NHC - 1)
                last.then_inc(s_y, 1)

            with pe.Fori(0, NTILE // 2) as tt:
                for i in range(2):
                    tile(tt, i)
            tile(NTILE // 2, 0, False)

        @block.scalar
        def _(act):
            act.sem_inc(s_ha, 2 * NH2)

            def copy_turned(i):
                nc.scalar.activation(xinT[i][:], px[:].rearrange("p (k t) -> p k t", k=KC), ACT.Copy).then_inc(s_xc, 1)

            act.wait_ge(s_xt, 1)
            copy_turned(0)
            def tile(tt, i, more=True):
                for c in range(NH2):
                    g = i * NH2 + c
                    act.wait_ge(s_h, tt * (2 * NH2) + (2 * NH2 + g + 1))
                    for a in range(2):
                        last = nc.scalar.activation(hT[i][:, 2 * c + a, :], ph[g % 2][:, a * TILE:(a + 1) * TILE],
                                                    ACT.Relu, bias=b1s[i][:, 2 * c + a:2 * c + a + 1])
                    last.then_inc(s_ha, 1)
                if more:
                    act.wait_ge(s_xt, tt * 2 + (i + 2))
                    copy_turned(1 - i)

            with act.Fori(0, NTILE // 2) as tt:
                for i in range(2):
                    tile(tt, i)
            tile(NTILE // 2, 0, False)

        @block.vector
        def _(dve):
            v = nc.vector
            steps = [0]

            def step(ins):
                steps[0] += 1
                ins.then_inc(s_step, 1)
                dve.wait_ge(s_step, steps[0])

            v.memset(ones[:], 1.0).then_inc(s_one, 1)
            dve.wait_ge(s_c, 64)
            v.tensor_copy(x2s[:, :, C], number[:])
            step(v.tensor_scalar(mt[:], iota[:, 0:MAXT], float(TILE), None, ALU.mult))
            dve.wait_ge(s_cnt, 1)
            v.tensor_copy(within[:], pr[:, 0, 0:J * E].rearrange("p (n e) -> p n e", n=J))
            step(v.tensor_copy(cnt[:], pr[:, 1, 0:J * E].rearrange("p (n e) -> p n e", n=J)))
            src, k, n = cnt, 1, 0
            while k < J:
                dst = cum[n % 2]
                v.tensor_copy(dst[:, 0:k, :], src[:, 0:k, :])
                step(v.tensor_tensor(dst[:, k:J, :], src[:, k:J, :], src[:, 0:J - k, :], ALU.add))
                src, k, n = dst, 2 * k, n + 1
            total, other = src, cum[n % 2]
            step(v.tensor_tensor(big[:], mt[:].unsqueeze(1).broadcast_to([P, E, MAXT]),
                                 total[:, J - 1, :].unsqueeze(2).broadcast_to([P, E, MAXT]), ALU.is_lt))
            step(v.reduce_sum(tiles[:], big[:], AX.X))
            step(v.memset(st[0][:, 0:1], 0.0))
            step(v.tensor_copy(st[0][:, 1:E], tiles[:, 0:E - 1]))
            src, k, n = st[0], 1, 1
            while k < E:
                dst = st[n % 2]
                v.tensor_copy(dst[:, 0:k], src[:, 0:k])
                step(v.tensor_tensor(dst[:, k:E], src[:, k:E], src[:, 0:E - k], ALU.add))
                src, k, n = dst, 2 * k, n + 1
            first, firstrow = src, st[n % 2]
            step(v.tensor_scalar(firstrow[:], first[:], float(TILE), None, ALU.mult))
            step(v.tensor_tensor(other[:], total[:], cnt[:], ALU.subtract))
            step(v.tensor_tensor(other[:], other[:], within[:], ALU.add))
            step(v.tensor_tensor(other[:], other[:], firstrow[:].unsqueeze(1).broadcast_to([P, J, E]), ALU.add))
            step(v.tensor_tensor(other[:], other[:], onehot[:], ALU.mult))
            step(v.reduce_sum(slotf[:], other[:], AX.X))
            v.tensor_copy(slot[:], slotf[:]).then_inc(s_route, 1)
            step(v.tensor_tensor(eidc[:], iota[:, 0:NTILE].unsqueeze(2).broadcast_to([P, NTILE, E]),
                                 first[:].unsqueeze(1).broadcast_to([P, NTILE, E]), ALU.is_ge))
            step(v.reduce_sum(eidf[:], eidc[:], AX.X))
            v.tensor_scalar(eid[:], eidf[:], 1.0, None, ALU.subtract).then_inc(s_route, 1)


            dve.sem_inc(s_yr, 2)
            routed = steps[0]
            steps[0] = 0
            dve.wait_ge(s_route, 2)

            def tile(tt, i):
                def tile_step(ins):
                    steps[0] += 1
                    ins.then_inc(s_step, 1)
                    dve.wait_ge(s_step, tt * E_STEPS + (routed + steps[0]))

                dve.wait_ge(s_y, tt * 2 + (i + 2))
                dve.wait_ge(s_base, tt * 2 + (i + 2))
                v.tensor_tensor(yr[:], py[i][:, :, 0:C], base[i][:], ALU.add).then_inc(s_yr, 1)
                dve.wait_ge(s_yr, tt * 2 + (i + 3))
                for n in range(TH):
                    last = v.bn_stats(stats[:, n, :], yr[:, n, :])
                tile_step(last)
                dve.wait_ge(s_sent, tt * 2 + (i + 1))
                layer_norm_steps(v, tile_step, yr, yo[i], stats, mv, nwt, nwi, s_ln, TH)
                dve.wait_ge(s_ln, tt * 2 + (i + 1))

            with dve.Fori(0, NTILE // 2) as tt:
                for i in range(2):
                    tile(tt, i)
            assert steps[0] == E_STEPS, steps[0]
            steps[0] = 0
            tile(NTILE // 2, 0)


_ORDER = ("x xT ctxT wqkT wv_l rf w_out b_out wk bk wq bq wv bv wck bck wcq bcq wcv bcv wp bp "
          "gate_wT gate_b w1T b1p w2T b2 ident mask_qk mask_kq sel fold tri iota number").split()


def kernel(**inputs):
    from concourse import bacc as _bacc
    from concourse.bass_utils import run_bass_kernel_spmd as _run

    d = {k: np.asarray(v) for k, v in inputs.items()}
    c = np.ascontiguousarray
    w_qkv = d["L0_attn_W_qkv"]
    a = {
        "x": d["x"], "xT": c(d["x"].transpose(0, 2, 1)), "ctxT": c(d["ctx_512"].transpose(0, 2, 1)),
        "wqkT": c(w_qkv[:, :2 * LR].T), "wv_l": c(w_qkv[:, 2 * LR:]), "rf": d["L0_attn_RF"],
        "w_out": d["L0_attn_W_out"], "b_out": d["L0_attn_b_out"],
        "gate_wT": c(d["L0_ffn_gate_w"].T), "gate_b": d["L0_ffn_gate_b"],
        "w1T": c(d["L0_ffn_w1"].transpose(0, 2, 1)),
        "b1p": c(d["L0_ffn_b1"].reshape(E, NHC, P).transpose(0, 2, 1)),
        "w2T": c(d["L0_ffn_w2"].transpose(0, 2, 1)), "b2": d["L0_ffn_b2"],
    }
    for n in ("k", "q", "v", "ck", "cq", "cv", "p"):
        a["w" + n], a["b" + n] = d["L0_xattn_W" + n], d["L0_xattn_b" + n]
    at = np.arange(P)
    a["ident"] = np.eye(P, dtype=np.float32)
    a["mask_qk"] = np.where(at[None, :] <= at[:, None], 0, NEG).astype(np.float32)
    a["mask_kq"] = np.where(at[:, None] <= at[None, :], 0, NEG).astype(np.float32)
    a["sel"] = np.zeros((3 * LH, NPAIR, P), np.float32)
    for h in range(LH):
        a["sel"][[h, 2 * LH + h], h // 2, h % 2 * LD:(h % 2 + 1) * LD] = 1
    a["fold"] = np.zeros((P, P), np.float32)
    for q in range(HG):
        for d in range(VW):
            a["fold"][q * HP + d, q * RW + d % RW] = 1
    a["tri"] = (at[:, None] < at[None, :]).astype(np.float32)
    a["iota"] = np.ascontiguousarray(np.broadcast_to(np.arange(B * NT, dtype=np.float32), (P, B * NT)))

    a["number"] = a["iota"] * P + at[:, None].astype(np.float32)

    nc = _bacc.Bacc("TRN2", target_bir_lowering=False, num_devices=1)
    arrays, args = {}, []
    for name in _ORDER:
        arrays[f"in_{name}"] = c(a[name])
        args.append(nc.dram_tensor(f"in_{name}", a[name].shape, mybir.dt.from_np(a[name].dtype), kind="ExternalInput").ap())
    args.append(nc.dram_tensor("out_0", (B, T, C), F32, kind="ExternalOutput").ap())
    decoder(nc, *args)
    r = _run(nc, [arrays], core_ids=[0])
    return r.results[0]["out_0"]
```
